# Optimizing a Trainium2 kernel written in Bass

```python
import numpy as np
import jax
import jax.numpy as jnp

def _softmax(x, axis=-1):
    return jax.nn.softmax(x, axis=axis)

def _gelu(x):
    return jax.nn.gelu(x, approximate=True)

def _silu(x):
    return jax.nn.silu(x)

def _sigmoid(x):
    return jax.nn.sigmoid(x)

def _layernorm(x, axis=-1, eps=1e-05):
    m = jnp.mean(x, axis=axis, keepdims=True)
    v = jnp.var(x, axis=axis, keepdims=True)
    return (x - m) / jnp.sqrt(v + eps)

def _scatter_add(tgt, idx, src, axis=0):
    return tgt.at[idx].add(src)

def _segment_sum(src, seg, n):
    return jax.ops.segment_sum(src, seg, n)
kernel_name = 'mk_adaln_d2_jaxref_r4_6aed17'

def setup_inputs(seed: int=0):
    np.random.seed(seed)
    _w = jnp.asarray

    def _L0_attn_setup():
        import jax, jax.numpy as jnp
        import numpy as np
        DIM = 256
        QK = 128
        HID = 512
        B, N = (4, 512)
        EPS = 1e-05
        key = jax.random.key(seed)
        ks = jax.random.split(key, 8)
        std = 0.02
        return {'x': jax.random.normal(ks[0], (B, N, DIM), jnp.float32), 'ln_scale': jnp.ones((DIM,), jnp.float32), 'ln_bias': jnp.zeros((DIM,), jnp.float32), 'W_hidden': jax.random.normal(ks[1], (DIM, 2 * HID), jnp.float32) * std, 'b_hidden': jnp.zeros((2 * HID,), jnp.float32), 'W_qk': jax.random.normal(ks[2], (DIM, QK), jnp.float32) * std, 'b_qk': jnp.zeros((QK,), jnp.float32), 'os_weight': jax.random.normal(ks[3], (2, QK), jnp.float32) * std, 'os_bias': jnp.zeros((2, QK), jnp.float32), 'W_out': jax.random.normal(ks[4], (HID, DIM), jnp.float32) * std, 'b_out': jnp.zeros((DIM,), jnp.float32)}
    _L0_attn_in = _L0_attn_setup()

    def _L0_ffn_setup():
        import jax, jax.numpy as jnp
        import numpy as np
        B, S, D = (4, 128, 256)
        E, K, H = (64, 8, 64)
        ES, HS = (2, 512)
        key = jax.random.key(seed)
        ks = jax.random.split(key, 8)
        scale = 0.02
        rn = lambda k, shape, s: jax.random.normal(k, shape, jnp.float32) * s
        return {'x': rn(ks[0], (B, S, D), 1.0), 'router_w': rn(ks[1], (D, E), scale), 'router_b': jnp.zeros((E,), jnp.float32), 'w1': rn(ks[2], (E, D, H), scale), 'b1': jnp.zeros((E, H), jnp.float32), 'w2': rn(ks[3], (E, H, D), scale), 'b2': jnp.zeros((E, D), jnp.float32), 'sw1': rn(ks[4], (ES, D, HS), scale), 'sb1': jnp.zeros((ES, HS), jnp.float32), 'sw2': rn(ks[5], (ES, HS, D), scale), 'sb2': jnp.zeros((ES, D), jnp.float32)}
    _L0_ffn_in = _L0_ffn_setup()
    _L0_c = _w((lambda *s: np.random.randn(*s).astype(np.float32) * 0.05)(4, 256))
    _L0_wmod = _w((lambda *s: np.random.randn(*s).astype(np.float32) * 0.05)(256, 6 * 256) * 256 ** (-0.5))

    def _L1_attn_setup():
        import jax, jax.numpy as jnp
        import numpy as np
        DIM = 256
        H = 16
        HD = DIM // H
        R = 8
        QK = 32
        B = 4
        S = 256
        EPS = 1e-05

        def _lin(x, W, b):
            return x @ W.T + b

        def _ln(x, g, b):
            m = x.mean(-1, keepdims=True)
            v = ((x - m) ** 2).mean(-1, keepdims=True)
            return (x - m) / jnp.sqrt(v + EPS) * g + b
        key = jax.random.key(seed)
        ks = iter(jax.random.split(key, 32))

        def w(shape, fan):
            s = 1.0 / np.sqrt(fan)
            return jax.random.uniform(next(ks), shape, jnp.float32, -s, s)
        d = {}
        d['x'] = jax.random.normal(next(ks), (B, S, DIM), jnp.float32)
        d['Wq'] = w((DIM, DIM), DIM)
        d['bq'] = w((DIM,), DIM)
        d['Wk'] = w((DIM, DIM), DIM)
        d['bk'] = w((DIM,), DIM)
        d['Wv'] = w((HD * R, DIM), DIM)
        d['bv'] = w((HD * R,), DIM)
        d['Wqv'] = w((QK * H, DIM), DIM)
        d['bqv'] = w((QK * H,), DIM)
        d['Ws'] = w((1, HD + QK), HD + QK)
        d['bs'] = w((1,), HD + QK)
        d['Wf'] = w((DIM, DIM), DIM)
        d['bf'] = w((DIM,), DIM)
        d['Wr1'] = w((2 * DIM, DIM), DIM)
        d['br1'] = w((2 * DIM,), DIM)
        d['Wr2'] = w((DIM, 2 * DIM), 2 * DIM)
        d['br2'] = w((DIM,), 2 * DIM)
        d['g1'] = jnp.ones((DIM,), jnp.float32)
        d['b1'] = jnp.zeros((DIM,), jnp.float32)
        d['g2'] = jnp.ones((DIM,), jnp.float32)
        d['b2'] = jnp.zeros((DIM,), jnp.float32)
        return d
    _L1_attn_in = _L1_attn_setup()

    def _L1_ffn_setup():
        import jax, jax.numpy as jnp
        import numpy as np
        DIM = 256

        def _reference_tuple_inner(x, W_r, W_k, W_v, mu_r, mu_k):
            B, T, C = x.shape
            x_prev = jnp.concatenate([jnp.zeros((B, 1, C), x.dtype), x[:, :-1, :]], axis=1)
            xr = mu_r * x + (1.0 - mu_r) * x_prev
            xk = mu_k * x + (1.0 - mu_k) * x_prev
            r = jax.nn.sigmoid(jnp.einsum('btc,dc->btd', xr, W_r))
            k = jnp.einsum('btc,dc->btd', xk, W_k)
            k_act = jnp.square(jax.nn.relu(k))
            out = r * jnp.einsum('btc,dc->btd', k_act, W_v)
            new_state = x[:, -1, :]
            return (out, new_state)
        key = jax.random.key(seed)
        ks = jax.random.split(key, 6)
        B, T, C = (8, 512, DIM)
        x = jax.random.normal(ks[0], (B, T, C), dtype=jnp.float32)
        s = 1.0 / np.sqrt(C)
        W_r = jax.random.uniform(ks[1], (C, C), jnp.float32, -s, s)
        W_k = jax.random.uniform(ks[2], (C, C), jnp.float32, -s, s)
        W_v = jax.random.uniform(ks[3], (C, C), jnp.float32, -s, s)
        mu_r = jax.random.uniform(ks[4], (C,), jnp.float32)
        mu_k = jax.random.uniform(ks[5], (C,), jnp.float32)
        return {'x': x, 'W_r': W_r, 'W_k': W_k, 'W_v': W_v, 'mu_r': mu_r, 'mu_k': mu_k}
    _L1_ffn_in = _L1_ffn_setup()
    _L1_c = _w((lambda *s: np.random.randn(*s).astype(np.float32) * 0.05)(4, 256))
    _L1_wmod = _w((lambda *s: np.random.randn(*s).astype(np.float32) * 0.05)(256, 6 * 256) * 256 ** (-0.5))
    _d = {'L0_attn_x': _L0_attn_in['x'], 'L0_attn_ln_scale': _L0_attn_in['ln_scale'], 'L0_attn_ln_bias': _L0_attn_in['ln_bias'], 'L0_attn_W_hidden': _L0_attn_in['W_hidden'], 'L0_attn_b_hidden': _L0_attn_in['b_hidden'], 'L0_attn_W_qk': _L0_attn_in['W_qk'], 'L0_attn_b_qk': _L0_attn_in['b_qk'], 'L0_attn_os_weight': _L0_attn_in['os_weight'], 'L0_attn_os_bias': _L0_attn_in['os_bias'], 'L0_attn_W_out': _L0_attn_in['W_out'], 'L0_attn_b_out': _L0_attn_in['b_out'], 'L0_ffn_router_w': _L0_ffn_in['router_w'], 'L0_ffn_router_b': _L0_ffn_in['router_b'], 'L0_ffn_w1': _L0_ffn_in['w1'], 'L0_ffn_b1': _L0_ffn_in['b1'], 'L0_ffn_w2': _L0_ffn_in['w2'], 'L0_ffn_b2': _L0_ffn_in['b2'], 'L0_ffn_sw1': _L0_ffn_in['sw1'], 'L0_ffn_sb1': _L0_ffn_in['sb1'], 'L0_ffn_sw2': _L0_ffn_in['sw2'], 'L0_ffn_sb2': _L0_ffn_in['sb2'], 'L0_c': _L0_c, 'L0_wmod': _L0_wmod, 'L1_attn_Wq': _L1_attn_in['Wq'], 'L1_attn_bq': _L1_attn_in['bq'], 'L1_attn_Wk': _L1_attn_in['Wk'], 'L1_attn_bk': _L1_attn_in['bk'], 'L1_attn_Wv': _L1_attn_in['Wv'], 'L1_attn_bv': _L1_attn_in['bv'], 'L1_attn_Wqv': _L1_attn_in['Wqv'], 'L1_attn_bqv': _L1_attn_in['bqv'], 'L1_attn_Ws': _L1_attn_in['Ws'], 'L1_attn_bs': _L1_attn_in['bs'], 'L1_attn_Wf': _L1_attn_in['Wf'], 'L1_attn_bf': _L1_attn_in['bf'], 'L1_attn_Wr1': _L1_attn_in['Wr1'], 'L1_attn_br1': _L1_attn_in['br1'], 'L1_attn_Wr2': _L1_attn_in['Wr2'], 'L1_attn_br2': _L1_attn_in['br2'], 'L1_attn_g1': _L1_attn_in['g1'], 'L1_attn_b1': _L1_attn_in['b1'], 'L1_attn_g2': _L1_attn_in['g2'], 'L1_attn_b2': _L1_attn_in['b2'], 'L1_ffn_W_r': _L1_ffn_in['W_r'], 'L1_ffn_W_k': _L1_ffn_in['W_k'], 'L1_ffn_W_v': _L1_ffn_in['W_v'], 'L1_ffn_mu_r': _L1_ffn_in['mu_r'], 'L1_ffn_mu_k': _L1_ffn_in['mu_k'], 'L1_c': _L1_c, 'L1_wmod': _L1_wmod}
    _x0 = _d['L0_attn_x']
    _d['L0_attn_x'] = jax.random.normal(jax.random.fold_in(jax.random.key(seed), 1), (4, 1024, 256), dtype=_x0.dtype)
    del _x0
    return _d

def reference(L0_attn_x, L0_attn_ln_scale, L0_attn_ln_bias, L0_attn_W_hidden, L0_attn_b_hidden, L0_attn_W_qk, L0_attn_b_qk, L0_attn_os_weight, L0_attn_os_bias, L0_attn_W_out, L0_attn_b_out, L0_ffn_router_w, L0_ffn_router_b, L0_ffn_w1, L0_ffn_b1, L0_ffn_w2, L0_ffn_b2, L0_ffn_sw1, L0_ffn_sb1, L0_ffn_sw2, L0_ffn_sb2, L0_c, L0_wmod, L1_attn_Wq, L1_attn_bq, L1_attn_Wk, L1_attn_bk, L1_attn_Wv, L1_attn_bv, L1_attn_Wqv, L1_attn_bqv, L1_attn_Ws, L1_attn_bs, L1_attn_Wf, L1_attn_bf, L1_attn_Wr1, L1_attn_br1, L1_attn_Wr2, L1_attn_br2, L1_attn_g1, L1_attn_b1, L1_attn_g2, L1_attn_b2, L1_ffn_W_r, L1_ffn_W_k, L1_ffn_W_v, L1_ffn_mu_r, L1_ffn_mu_k, L1_c, L1_wmod):

    def _L0_attn_ref(x, ln_scale, ln_bias, W_hidden, b_hidden, W_qk, b_qk, os_weight, os_bias, W_out, b_out):
        import jax, jax.numpy as jnp
        import numpy as np
        DIM = 256
        QK = 128
        HID = 512
        B, N = (4, 512)
        EPS = 1e-05
        n = x.shape[1]
        mu = jnp.mean(x, axis=-1, keepdims=True)
        var = jnp.mean(jnp.square(x - mu), axis=-1, keepdims=True)
        xn = (x - mu) / jnp.sqrt(var + EPS) * ln_scale + ln_bias
        hid = jax.nn.silu(xn @ W_hidden + b_hidden)
        v, gate = (hid[..., :HID], hid[..., HID:])
        qk = jax.nn.silu(xn @ W_qk + b_qk)
        qk2 = qk[..., None, :] * os_weight + os_bias
        q, k = (qk2[..., 0, :], qk2[..., 1, :])
        sim = jnp.einsum('bid,bjd->bij', q, k) / n
        attn = jnp.square(jax.nn.relu(sim))
        out = jnp.einsum('bij,bjd->bid', attn, v)
        out = out * gate
        return out @ W_out + b_out

    def _L0_ffn_ref(x, router_w, router_b, w1, b1, w2, b2, sw1, sb1, sw2, sb2):
        import jax, jax.numpy as jnp
        import numpy as np
        B, S, D = (4, 128, 256)
        E, K, H = (64, 8, 64)
        ES, HS = (2, 512)
        b_, s_, d_ = x.shape
        xf = x.reshape(-1, d_)
        probs = jax.nn.softmax(xf @ router_w + router_b, axis=-1)
        tw, ti = jax.lax.top_k(probs, K)
        tw = tw / jnp.sum(tw, axis=-1, keepdims=True)

        def body(acc, p):
            W1, B1, W2, B2, e = p
            h = jax.nn.silu(xf @ W1 + B1) @ W2 + B2
            cw = jnp.sum(jnp.where(ti == e, tw, 0.0), axis=-1)
            return (acc + cw[:, None] * h, None)
        routed, _ = jax.lax.scan(body, jnp.zeros_like(xf), (w1, b1, w2, b2, jnp.arange(w1.shape[0])))

        def shared_mlp(W1, B1, W2, B2):
            return jax.nn.silu(xf @ W1 + B1) @ W2 + B2
        shared = jnp.sum(jax.vmap(shared_mlp)(sw1, sb1, sw2, sb2), axis=0)
        return (routed + shared).reshape(b_, s_, d_)

    def _L1_attn_ref(x, Wq, bq, Wk, bk, Wv, bv, Wqv, bqv, Ws, bs, Wf, bf, Wr1, br1, Wr2, br2, g1, b1, g2, b2):
        import jax, jax.numpy as jnp
        import numpy as np
        DIM = 256
        H = 16
        HD = DIM // H
        R = 8
        QK = 32
        B = 4
        S = 256
        EPS = 1e-05

        def _lin(x, W, b):
            return x @ W.T + b

        def _ln(x, g, b):
            m = x.mean(-1, keepdims=True)
            v = ((x - m) ** 2).mean(-1, keepdims=True)
            return (x - m) / jnp.sqrt(v + EPS) * g + b
        b, n, _ = x.shape
        res = x
        xn = _ln(x, g1, b1)
        q = _lin(xn, Wq, bq).reshape(b, n, H, HD) / np.sqrt(HD).astype(np.float32)
        k = _lin(xn, Wk, bk).reshape(b, n, H, HD)
        score = jax.nn.softmax(jnp.einsum('bihd,bjhd->bhij', q, k), axis=-1)
        v = _lin(xn, Wv, bv).reshape(b, n, R, HD)
        out = jnp.einsum('bhij,bjrd->bihrd', score, v)
        qv = _lin(xn, Wqv, bqv).reshape(b, n, H, 1, QK) / np.sqrt(QK).astype(np.float32)
        qv = jnp.broadcast_to(qv, (b, n, H, R, QK))
        comp = jnp.concatenate([qv, out], axis=-1) @ Ws.T + bs
        comp = jax.nn.softmax(comp, axis=3)
        out = (comp * out).sum(axis=3).reshape(b, n, DIM)
        out = res + _lin(out, Wf, bf)
        res2 = out
        on = _ln(out, g2, b2)
        ffn = _lin(jax.nn.relu(_lin(on, Wr1, br1)), Wr2, br2)
        return res2 + ffn

    def _L1_ffn_ref(x, W_r, W_k, W_v, mu_r, mu_k):
        import jax, jax.numpy as jnp
        import numpy as np
        DIM = 256

        def _reference_tuple_inner(x, W_r, W_k, W_v, mu_r, mu_k):
            B, T, C = x.shape
            x_prev = jnp.concatenate([jnp.zeros((B, 1, C), x.dtype), x[:, :-1, :]], axis=1)
            xr = mu_r * x + (1.0 - mu_r) * x_prev
            xk = mu_k * x + (1.0 - mu_k) * x_prev
            r = jax.nn.sigmoid(jnp.einsum('btc,dc->btd', xr, W_r))
            k = jnp.einsum('btc,dc->btd', xk, W_k)
            k_act = jnp.square(jax.nn.relu(k))
            out = r * jnp.einsum('btc,dc->btd', k_act, W_v)
            new_state = x[:, -1, :]
            return (out, new_state)
        return _reference_tuple_inner(x, W_r, W_k, W_v, mu_r, mu_k)[0]
    x = L0_attn_x
    mod = (_silu(L0_c) @ L0_wmod).reshape(L0_c.shape[0], 6, 1, -1)
    sa, ca, ga, sb, cb, gb = (mod[:, 0], mod[:, 1], mod[:, 2], mod[:, 3], mod[:, 4], mod[:, 5])
    ga = (2 * (ga >= 0) - 1) * jnp.maximum(jnp.abs(ga), 0.25)
    gb = (2 * (gb >= 0) - 1) * jnp.maximum(jnp.abs(gb), 0.25)
    h = _layernorm(x, axis=-1) * (1 + ca) + sa
    x = x + ga * _L0_attn_ref(h, L0_attn_ln_scale, L0_attn_ln_bias, L0_attn_W_hidden, L0_attn_b_hidden, L0_attn_W_qk, L0_attn_b_qk, L0_attn_os_weight, L0_attn_os_bias, L0_attn_W_out, L0_attn_b_out)
    h = _layernorm(x, axis=-1) * (1 + cb) + sb
    x = x + gb * _L0_ffn_ref(h, L0_ffn_router_w, L0_ffn_router_b, L0_ffn_w1, L0_ffn_b1, L0_ffn_w2, L0_ffn_b2, L0_ffn_sw1, L0_ffn_sb1, L0_ffn_sw2, L0_ffn_sb2)
    mod = (_silu(L1_c) @ L1_wmod).reshape(L1_c.shape[0], 6, 1, -1)
    sa, ca, ga, sb, cb, gb = (mod[:, 0], mod[:, 1], mod[:, 2], mod[:, 3], mod[:, 4], mod[:, 5])
    ga = (2 * (ga >= 0) - 1) * jnp.maximum(jnp.abs(ga), 0.25)
    gb = (2 * (gb >= 0) - 1) * jnp.maximum(jnp.abs(gb), 0.25)
    h = _layernorm(x, axis=-1) * (1 + ca) + sa
    x = x + ga * _L1_attn_ref(h, L1_attn_Wq, L1_attn_bq, L1_attn_Wk, L1_attn_bk, L1_attn_Wv, L1_attn_bv, L1_attn_Wqv, L1_attn_bqv, L1_attn_Ws, L1_attn_bs, L1_attn_Wf, L1_attn_bf, L1_attn_Wr1, L1_attn_br1, L1_attn_Wr2, L1_attn_br2, L1_attn_g1, L1_attn_b1, L1_attn_g2, L1_attn_b2)
    h = _layernorm(x, axis=-1) * (1 + cb) + sb
    x = x + gb * _L1_ffn_ref(h, L1_ffn_W_r, L1_ffn_W_k, L1_ffn_W_v, L1_ffn_mu_r, L1_ffn_mu_k)
    return x

_drawn_inputs = setup_inputs


def setup_inputs(seed=0):
    import zlib

    import numpy as np

    out = dict(_drawn_inputs(seed))
    spreads = {'L0_attn_ln_scale': (1.0, 0.2),
     'L0_attn_ln_bias': (0.0, 0.1),
     'L0_attn_b_hidden': (0.0, 0.1),
     'L0_attn_b_qk': (0.0, 0.1),
     'L0_attn_os_bias': (0.0, 0.1),
     'L0_attn_b_out': (0.0, 0.337),
     'L0_ffn_router_b': (0.0, 0.8),
     'L0_ffn_b1': (0.0, 0.8),
     'L0_ffn_b2': (0.0, 0.8),
     'L0_ffn_sb1': (0.0, 0.8),
     'L0_ffn_sb2': (0.0, 0.1),
     'L1_attn_g1': (1.0, 0.6),
     'L1_attn_b1': (0.0, 0.8),
     'L1_attn_g2': (1.0, 0.6),
     'L1_attn_b2': (0.0, 2.0)}
    factors = {'L0_ffn_router_w': 6.622,
     'L0_ffn_w1': 8.0,
     'L0_ffn_w2': 8.0,
     'L1_attn_Wq': 8.0,
     'L1_attn_bq': 8.0,
     'L1_attn_Wk': 8.0,
     'L1_attn_bk': 64.0,
     'L1_attn_Wv': 8.0,
     'L1_attn_bv': 8.0,
     'L1_attn_Wqv': 64.0,
     'L1_attn_bqv': 64.0,
     'L1_attn_Ws': 8.0,
     'L1_attn_Wf': 8.0,
     'L1_attn_bf': 52.168,
     'L1_attn_br1': 64.0,
     'L1_attn_br2': 64.0,
     'L1_ffn_W_r': 8.0,
     'L1_ffn_W_k': 3.082,
     'L1_ffn_W_v': 2.816,
     'L1_ffn_mu_r': 8.0,
     'L1_ffn_mu_k': 5.073,
     'L1_attn_Wr1': 3.869,
     'L1_attn_Wr2': 3.666}
    for name, (base, spread) in spreads.items():
        noise = np.random.default_rng([zlib.crc32(name.encode()), seed]).standard_normal(out[name].shape)
        drawn = base * np.exp(spread * noise) if base else spread * noise
        out[name] = jnp.asarray(drawn.astype(out[name].dtype))
    for name, factor in factors.items():
        out[name] = (out[name] * factor).astype(out[name].dtype)
    return out
```

```python
from contextlib import ExitStack

import numpy as np
import concourse.bass as bass
from concourse import mybir

F32 = mybir.dt.float32
F32R = mybir.dt.float32r
BF16 = mybir.dt.bfloat16
ACT = mybir.ActivationFunctionType
ALU = mybir.AluOpType
X_AXIS = mybir.AxisListType.X

P = 128
DIM = 256
KT = DIM // P
BATCH, SEQ = 4, 1024
TILES = SEQ // P
CHUNK = 512
CT = CHUNK // P
CHUNKS = SEQ // CHUNK
TOKENS = BATCH * SEQ
EPS = 1e-5
SHIFT_A, SCALE_A, GATE_A, SHIFT_B, SCALE_B, GATE_B = range(6)
MOD = 6 * DIM
START = 1


def at(trip, per_trip, step):
    return START + trip * per_trip + step


class Steps:

    def __init__(self, engine, semaphore):
        self.engine, self.semaphore, self.n = engine, semaphore, 0

    def one(self):
        self.n += 1
        return 1

    def wait(self, back=0):
        self.engine.wait_ge(self.semaphore, self.n - back)

    def restart(self):
        self.wait()
        self.engine.sem_clear(self.semaphore)
        self.n = 0


class Room:
    raised = []

    def __init__(self, nc, ctx, name):
        self.nc, self.ctx, self.name, self.counters = nc, ctx, name, []

    def sb(self, name, shape, dt=F32):
        return self.ctx.enter_context(self.nc.sbuf_tensor(f"{self.name}_{name}", list(shape), dt))

    def ps(self, name, shape, dt=F32):
        return self.ctx.enter_context(self.nc.psum_tensor(f"{self.name}_{name}", list(shape), dt))

    def sem(self, name):
        semaphore = self.ctx.enter_context(self.nc.semaphore(f"{self.name}_{name}"))
        Room.raised.append(semaphore)
        return semaphore

    def counter(self, name):
        self.counters.append(self.sem(name))
        return self.counters[-1]

    def pair(self, name, shape):
        return self.sb(name + "_hi", shape, F32R), self.sb(name + "_lo", shape, F32R)


def start_counters(nc, room):
    with nc.Block() as block:
        @block.gpsimd
        def _(pool):
            for counter in room.counters:
                pool.sem_inc(counter, START)


def clear_semaphores(nc):
    numbers = sorted({semaphore.num for semaphore in Room.raised})
    Room.raised.clear()
    with nc.Block() as block:
        @block.gpsimd
        def _(pool):
            start = 0
            for n in range(1, len(numbers) + 1):
                if n == len(numbers) or numbers[n] != numbers[n - 1] + 1:
                    pool.sem_clear(range(numbers[start], numbers[n - 1] + 1))
                    start = n


def product3(pe, out, weights, moving, first, last):
    (w_hi, w_lo), (m_hi, m_lo) = weights, moving
    pe.matmul(out, w_hi, m_hi, start=first, stop=False)
    pe.matmul(out, w_hi, m_lo, start=False, stop=False)
    return pe.matmul(out, w_lo, m_hi, start=False, stop=last)


def cut(pair, *index):
    return tuple(half[index] for half in pair)


def column(bc, rows, n):
    return bc.unsqueeze(2).to_broadcast([bc.shape[0], rows, n])


def load_block(nc, room, loads, weights, identity=None):
    SLOTS, STAGE = 4, 1024
    with ExitStack() as ctx:
        own = Room(nc, ctx, room.name + "_load")
        staging = own.sb("staging", [P, SLOTS, STAGE]) if weights else None
        loaded, ident_zero, ident_done = own.sem("loaded"), own.sem("ident_zero"), own.sem("ident_done")
        landed = [own.sem(f"landed{s}") for s in range(SLOTS)]
        hi_done, lo_done = own.sem("hi_done"), own.sem("lo_done")

        def staged(n, like):
            flat = staging[:, n % SLOTS, 0:like.free_size()]
            shape = like.shape
            if len(shape) == 3:
                return flat.rearrange("p (a b) -> p a b", b=shape[2])
            if len(shape) == 4:
                return flat.rearrange("p (a b c) -> p a b c", b=shape[2], c=shape[3])
            return flat

        with nc.Block() as block:
            @block.sync
            def _(sp):
                for n, ((hi, lo), source) in enumerate(weights):
                    if n >= SLOTS:
                        sp.wait_ge(lo_done, n - SLOTS + 1)
                    sp.dma_start(staged(n, hi), source).then_inc(landed[n % SLOTS], 16)

            @block.gpsimd
            def _(pool):
                if identity is not None:
                    pool.memset(identity, 0.0).then_inc(ident_zero, 1)
                    pool.wait_ge(ident_zero, 1)
                    pool.affine_select(out=identity, in_=identity, compare_op=ALU.not_equal, fill=1.0,
                                       base=0, pattern=[[-1, P]], channel_multiplier=1).then_inc(ident_done, 1)
                    pool.wait_ge(ident_done, 1)

            @block.scalar
            def _(act):
                for destination, source in loads:
                    act.dma_start(destination, source).then_inc(loaded, 16)
                for n, ((hi, lo), _) in enumerate(weights):
                    act.wait_ge(landed[n % SLOTS], 16 * (n // SLOTS + 1))
                    act.activation(hi, staged(n, hi), ACT.Copy).then_inc(hi_done, 1)
                if loads:
                    act.wait_ge(loaded, 16 * len(loads))

            @block.vector
            def _(vec):
                for n, ((hi, lo), _) in enumerate(weights):
                    vec.wait_ge(hi_done, n + 1)
                    vec.tensor_tensor(lo, staged(n, hi), hi.bitcast(F32), ALU.subtract).then_inc(lo_done, 1)


def newton_rsqrt(vec, step, y, v, scratch):
    vec.tensor_tensor(scratch, y, y, ALU.mult).then_inc(step.semaphore, step.one())
    step.wait()
    vec.tensor_tensor(scratch, scratch, v, ALU.mult).then_inc(step.semaphore, step.one())
    step.wait()
    vec.tensor_scalar(scratch, scratch, -0.5, 1.5, ALU.mult, ALU.add).then_inc(step.semaphore, step.one())
    step.wait()
    vec.tensor_tensor(y, y, scratch, ALU.mult).then_inc(step.semaphore, step.one())


def stage_mod(nc, c_t, wmods, mod_d, mod_cols_d):
    LAYERS = 2
    with ExitStack() as ctx:
        room = Room(nc, ctx, "mod")
        c_raw, c_act = room.sb("c_raw", [P, KT, LAYERS * BATCH]), room.sb("c_act", [P, KT, LAYERS * BATCH])
        w = room.sb("w", [P, LAYERS, KT, MOD])
        mod = room.sb("mod", [BATCH, LAYERS, MOD])
        sign = room.sb("sign", [BATCH, 4, DIM])
        out_ps = [room.ps(f"out{n}", [P, 512]) for n in range(MOD // 512 * LAYERS)]
        c_in, silu_done, mod_step, mod_out = (room.sem(n) for n in ("c_in", "silu_done", "mod_step", "mod_out"))
        w_in = [room.sem(f"w_in{layer}") for layer in range(LAYERS)]
        product_done, mod_ready = room.sem("product_done"), room.sem("mod_ready")
        ident = room.sb("ident", [BATCH, BATCH])
        cols = room.sb("cols", [P, LAYERS, MOD // P, BATCH])
        cols_ps = room.ps("cols_ps", [P, LAYERS, MOD // P, BATCH])
        ident_ready, cols_full, cols_ready = room.sem("ident_ready"), room.sem("cols_full"), room.sem("cols_ready")
        PARTS = MOD // 512
        with nc.Block() as block:
            @block.sync
            def _(sp):
                sp.dma_start(c_raw[:], c_t.rearrange("(k p) n -> p k n", p=P)).then_inc(c_in, 16)
                for layer in range(LAYERS):
                    sp.dma_start(w[:, layer], wmods[layer].rearrange("(k p) n -> p k n", p=P)).then_inc(w_in[layer], 16)
                sp.wait_ge(mod_ready, 1)
                sp.dma_start(mod_d.rearrange("l b n -> b l n"), mod[:]).then_inc(mod_out, 16)
                sp.wait_ge(cols_ready, 1)
                sp.dma_start(mod_cols_d, cols[:]).then_inc(mod_out, 16)
                sp.wait_ge(mod_out, 32)

            @block.gpsimd
            def _(pool):
                pool.memset(ident[:], 0.0).then_inc(ident_ready, 1)
                pool.wait_ge(ident_ready, 1)
                pool.affine_select(out=ident[:], in_=ident[:], compare_op=ALU.not_equal, fill=1.0, base=0,
                                   pattern=[[-1, BATCH]], channel_multiplier=1).then_inc(ident_ready, 1)

            @block.scalar
            def _(act):
                act.wait_ge(c_in, 16)
                act.activation(c_act[:], c_raw[:], ACT.Silu).then_inc(silu_done, 1)

            @block.tensor
            def _(pe):
                pe.wait_ge(silu_done, 1)
                for layer in range(LAYERS):
                    pe.wait_ge(w_in[layer], 16)
                    for n in range(PARTS):
                        for k in range(KT):
                            mm = pe.matmul(out_ps[layer * PARTS + n][0:BATCH, :],
                                           c_act[:, k, layer * BATCH:(layer + 1) * BATCH],
                                           w[:, layer, k, n * 512:(n + 1) * 512], start=(k == 0), stop=(k == KT - 1))
                        mm.then_inc(product_done, 1)
                pe.wait_ge(ident_ready, 2)
                pe.wait_ge(mod_ready, 1)
                for layer in range(LAYERS):
                    for n in range(MOD // P):
                        mm = pe.transpose(cols_ps[:, layer, n], mod[:, layer, n * P:(n + 1) * P], ident[:])
                mm.then_inc(cols_full, 1)

            @block.vector
            def _(vec):
                step = Steps(vec, mod_step)
                for n in range(LAYERS * PARTS):
                    vec.wait_ge(product_done, n + 1)
                    vec.tensor_copy(mod[:, n // PARTS, (n % PARTS) * 512:(n % PARTS + 1) * 512],
                                    out_ps[n][0:BATCH, :]).then_inc(mod_step, step.one())
                step.wait()
                for layer in range(LAYERS):
                    for which in (SCALE_A, SCALE_B):
                        part = mod[:, layer, which * DIM:(which + 1) * DIM]
                        vec.tensor_scalar(part, part, 1.0, None, ALU.add).then_inc(mod_step, step.one())
                    for n, which in enumerate((GATE_A, GATE_B)):
                        part = mod[:, layer, which * DIM:(which + 1) * DIM]
                        s = sign[:, 2 * layer + n]
                        vec.tensor_scalar(s, part, 0.0, 2.0, ALU.is_ge, ALU.mult).then_inc(mod_step, step.one())
                        step.wait()
                        vec.scalar_tensor_tensor(part, part, -1.0, part, ALU.mult, ALU.max).then_inc(mod_step, step.one())
                        step.wait()
                        vec.tensor_scalar(part, part, 0.25, None, ALU.max).then_inc(mod_step, step.one())
                        step.wait()
                        vec.scalar_tensor_tensor(part, s, -1.0, part, ALU.add, ALU.mult).then_inc(mod_step, step.one())
                step.wait()
                vec.tensor_copy(sign[:, 0, 0:1], sign[:, 0, 0:1]).then_inc(mod_ready, 1)
                vec.wait_ge(cols_full, 1)
                vec.tensor_copy(cols[:], cols_ps[:]).then_inc(cols_ready, 1)


def stage_gated_attention(nc, x_in, x_out, mod_d, w):
    HID, QK = 512, P
    HT = HID // P
    STEPS = CHUNKS * TILES
    RING = 3
    T0, QK0, G0, V0, Y0 = 0, CHUNKS * KT, CHUNKS * KT + CHUNKS, CHUNKS * KT + CHUNKS + CHUNKS * HT, \
        CHUNKS * KT + CHUNKS + CHUNKS * HT + TILES
    USES = Y0 + TILES
    assert USES % 2 == 0
    with ExitStack() as ctx:
        room = Room(nc, ctx, "ga")
        sb, sem = room.sb, room.counter
        ident = sb("ident", [P, P])
        w_hidden = room.pair("w_hidden", [P, KT, 2 * HID])
        w_qk = room.pair("w_qk", [P, KT, QK])
        w_out = room.pair("w_out", [P, HT, DIM])
        ln_col = sb("ln_col", [P, 2, KT])
        gate_bias = sb("gate_bias", [P, HT])
        qk_cols = sb("qk_cols", [P, 5])
        v_bias = sb("v_bias", [P, HID])
        out_bias = sb("out_bias", [P, DIM])
        mod = sb("mod", [P, BATCH, 3, DIM])
        load_block(nc, room, [
            (ln_col[:], w["ln_cols"]),
            (gate_bias[:], w["gate_bias"]),
            (qk_cols[:], w["qk_cols"]),
            (v_bias[:], w["v_bias"].partition_broadcast(P)),
            (out_bias[:], w["b_out"].partition_broadcast(P)),
            (mod[:], mod_d[0, :, 0:3 * DIM].rearrange("b (w n) -> b w n", n=DIM).partition_broadcast(P)),
        ], [((w_hidden[0][:, k], w_hidden[1][:, k]), w["W_hidden"][k * P:(k + 1) * P]) for k in range(KT)] + [
            ((w_qk[0][:], w_qk[1][:]), w["W_qk"].rearrange("(k p) n -> p k n", p=P)),
            ((w_out[0][:], w_out[1][:]), w["W_out"].rearrange("(m p) n -> p m n", p=P))], ident[:])

        x_ln = sb("x_ln", [P, TILES, DIM])
        rows = sb("rows", [P, TILES, DIM])
        x_res = sb("x_res", [P, CHUNKS, CT, DIM])
        stats, moments = sb("stats", [P, TILES, 6]), sb("moments", [P, TILES, 2])
        var, rstd, scratch = sb("var", [P, TILES]), sb("rstd", [P, TILES]), sb("scratch", [P, TILES])
        gate_now, mark = sb("gate_now", [P, DIM]), sb("mark", [P, 1])
        power = sb("power", [P, TILES])
        xt = sb("xt", [P, 2, CHUNK])
        x_t = room.pair("x_t", [P, KT, SEQ])
        qk_act = sb("qk_act", [P, CHUNKS, CHUNK])
        q_tmp, k_tmp = sb("q_tmp", [P, CHUNK]), sb("k_tmp", [P, CHUNK])
        q_t, k_t = room.pair("q_t", [P, SEQ]), room.pair("k_t", [P, SEQ])
        v_tmp = sb("v_tmp", [P, 2, HID])
        v = room.pair("v", [P, TILES, HID])
        gate_t = sb("gate_t", [P, HT, SEQ])
        relu = sb("relu", [P, RING, CHUNK])
        square = sb("square", [P, CHUNK])
        attn = room.pair("attn", [P, RING, CHUNK])
        og_tmp = sb("og_tmp", [P, 2, CHUNK])
        og = room.pair("og", [P, HT, CHUNK])
        y_tmp = sb("y_tmp", [P, 2, DIM])
        shared_ps = [room.ps(f"shared{n}", [P, 512]) for n in range(2)]
        score_ps = [room.ps(f"score{n}", [P, CHUNK]) for n in range(2)]
        o_ps = [room.ps(f"o{n}", [P, CHUNK]) for n in range(HT)]

        x_ln_in, x_ln_used, x_res_in, x_stored = sem("x_ln_in"), sem("x_ln_used"), sem("x_res_in"), sem("x_stored")
        var_ready, rstd_ready, rows_ready = sem("var_ready"), sem("rstd_ready"), sem("rows_ready")
        constants, gate_copied, marked = room.sem("constants"), sem("gate_copied"), sem("marked")
        shared_full = sem("shared_full")
        xt_ready, x_t_ready = sem("xt_ready"), sem("x_t_ready")
        qk_ready, qk_split = sem("qk_ready"), sem("qk_split")
        gate_ready = sem("gate_ready")
        v_biased, v_hi_ready, v_ready = sem("v_biased"), sem("v_hi_ready"), sem("v_ready")
        score_full, relu_ready, attn_hi_ready, attn_ready = (
            sem("score_full"), sem("relu_ready"), sem("attn_hi_ready"), sem("attn_ready"))
        o_step = sem("o_step")
        og_scaled, og_hi_ready, og_ready = sem("og_scaled"), sem("og_hi_ready"), sem("og_ready")
        y_biased, y_gated, x_ready = sem("y_biased"), sem("y_gated"), sem("x_ready")
        vec_step = room.sem("vec_step")

        src_x = x_in.rearrange("(b t p) n -> b p t n", b=BATCH, p=P)
        src_res = x_in.rearrange("(b c t p) n -> b p c t n", b=BATCH, c=CHUNKS, p=P)
        dst_x = x_out.rearrange("(b c t p) n -> b p c t n", b=BATCH, c=CHUNKS, p=P)

        def trips(engine, body):
            with engine.Fori(0, BATCH - 1) as trip:
                body(trip, False)
            body(BATCH - 1, True)

        def shared_free(pe, trip, use):
            u = use - 2
            if u < 0:
                pe.wait_ge(y_biased, at(trip, TILES, 0))
            elif u < QK0:
                pe.wait_ge(xt_ready, at(trip, CHUNKS * KT, u - T0 + 1))
            elif u < G0:
                pe.wait_ge(qk_ready, at(trip, CHUNKS, u - QK0 + 1))
            elif u < V0:
                pe.wait_ge(gate_ready, at(trip, CHUNKS * HT, u - G0 + 1))
            elif u < Y0:
                pe.wait_ge(v_biased, at(trip, TILES, u - V0 + 1))
            else:
                pe.wait_ge(y_biased, at(trip, TILES, u - Y0 + 1))

        start_counters(nc, room)
        with nc.Block() as block:
            @block.sync
            def _(sp):
                sp.dma_start(x_ln[:], src_x[0]).then_inc(x_ln_in, 16)

                def trip_of(trip, last):
                    sp.wait_ge(x_stored, at(trip, 16 * CHUNKS, 0))
                    sp.dma_start(x_res[:], src_res[trip]).then_inc(x_res_in, 16)
                    if not last:
                        sp.wait_ge(x_ln_used, at(trip, 1, 1))
                        sp.dma_start(x_ln[:], src_x[trip + 1]).then_inc(x_ln_in, 16)
                    for c in range(CHUNKS):
                        sp.wait_ge(x_ready, at(trip, TILES, CT * (c + 1)))
                        sp.dma_start(dst_x[trip, :, c], x_res[:, c]).then_inc(x_stored, 16)
                trips(sp, trip_of)
                sp.wait_ge(x_stored, at(BATCH, 16 * CHUNKS, 0))

            @block.gpsimd
            def _(pool):
                pool.memset(power[:], -0.5).then_inc(constants, 1)
                pool.wait_ge(constants, 1)

                def rsqrt(index, n):
                    pool.wait_ge(var_ready, at(index, 2, n))
                    pool.tensor_tensor(rstd[:], var[:], power[:], ALU.pow).then_inc(rstd_ready, 1)

                rsqrt(0, 1)
                rsqrt(0, 2)

                def trip_of(trip, last):
                    pool.wait_ge(x_ready, at(trip, TILES, 0))
                    pool.tensor_tensor(mark[:], power[:, 0:1], power[:, 0:1], ALU.mult).then_inc(marked, 1)
                    pool.tensor_copy(gate_now[:], mod[:, trip, GATE_A]).then_inc(gate_copied, 1)
                    pool.wait_ge(gate_copied, at(trip, 1, 1))
                    pool.wait_ge(marked, at(trip, 1, 1))
                    pool.wait_ge(x_res_in, at(trip, 16, 16))
                    for c in range(CHUNKS):
                        if not last:
                            rsqrt(trip + 1, c + 1)
                        for t in range(CT):
                            n = c * CT + t
                            pool.wait_ge(y_biased, at(trip, TILES, n + 1))
                            pool.tensor_tensor(y_tmp[:, n % 2], y_tmp[:, n % 2], gate_now[:],
                                               ALU.mult).then_inc(y_gated, 1)
                            pool.wait_ge(y_gated, at(trip, TILES, n + 1))
                            pool.tensor_tensor(x_res[:, c, t], x_res[:, c, t], y_tmp[:, n % 2],
                                               ALU.add).then_inc(x_ready, 1)
                trips(pool, trip_of)

            @block.tensor
            def _(pe):
                def trip_of(trip, last):
                    pe.wait_ge(rows_ready, at(trip, 1, 1))
                    for c in range(CHUNKS):
                        for k in range(KT):
                            use = T0 + c * KT + k
                            shared_free(pe, trip, use)
                            for t in range(CT):
                                mm = pe.transpose(shared_ps[use % 2][:, t * P:(t + 1) * P],
                                                  rows[:, c * CT + t, k * P:(k + 1) * P], ident[:])
                            mm.then_inc(shared_full, 1)
                    for c in range(CHUNKS):
                        use = QK0 + c
                        shared_free(pe, trip, use)
                        pe.wait_ge(x_t_ready, at(trip, CHUNKS * KT, KT * (c + 1)))
                        for k in range(KT):
                            mm = product3(pe, shared_ps[use % 2][:], cut(w_qk, slice(None), k),
                                          cut(x_t, slice(None), k, slice(c * CHUNK, (c + 1) * CHUNK)),
                                          k == 0, k == KT - 1)
                        mm.then_inc(shared_full, 1)
                    for m in range(HT):
                        for c in range(CHUNKS):
                            use = G0 + m * CHUNKS + c
                            shared_free(pe, trip, use)
                            for k in range(KT):
                                mm = product3(pe, shared_ps[use % 2][:],
                                              cut(w_hidden, slice(None), k, slice(HID + m * P, HID + (m + 1) * P)),
                                              cut(x_t, slice(None), k, slice(c * CHUNK, (c + 1) * CHUNK)),
                                              k == 0, k == KT - 1)
                            mm.then_inc(shared_full, 1)

                    def scores(s):
                        c, j = divmod(s, TILES)
                        pe.wait_ge(qk_split, at(trip, CHUNKS, max(c, j // CT) + 1))
                        pe.wait_ge(relu_ready, at(trip, STEPS, max(0, s - 1)))
                        product3(pe, score_ps[s % 2][:], cut(k_t, slice(None), slice(j * P, (j + 1) * P)),
                                 cut(q_t, slice(None), slice(c * CHUNK, (c + 1) * CHUNK)),
                                 True, True).then_inc(score_full, 1)

                    scores(0)
                    scores(1)
                    for t in range(TILES):
                        use = V0 + t
                        shared_free(pe, trip, use)
                        for k in range(KT):
                            mm = product3(pe, shared_ps[use % 2][:], cut(x_t, slice(None), k, slice(t * P, (t + 1) * P)),
                                          cut(w_hidden, slice(None), k, slice(0, HID)), k == 0, k == KT - 1)
                        mm.then_inc(shared_full, 1)

                    def project(c):
                        pe.wait_ge(og_ready, at(trip, CHUNKS * HT, HT * (c + 1)))
                        for t in range(CT):
                            use = Y0 + c * CT + t
                            shared_free(pe, trip, use)
                            for m in range(HT):
                                mm = product3(pe, shared_ps[use % 2][:, 0:DIM],
                                              cut(og, slice(None), m, slice(t * P, (t + 1) * P)),
                                              cut(w_out, slice(None), m), m == 0, m == HT - 1)
                            mm.then_inc(shared_full, 1)

                    for s in range(STEPS):
                        c, j = divmod(s, TILES)
                        if s + 2 < STEPS:
                            scores(s + 2)
                        pe.wait_ge(attn_ready, at(trip, STEPS, s + 1))
                        pe.wait_ge(v_ready, at(trip, TILES, j + 1))
                        for m in range(HT):
                            if j == 0 and c > 0:
                                pe.wait_ge(og_scaled, at(trip, CHUNKS * HT, HT * (c - 1) + m + 1))
                            mm = product3(pe, o_ps[m][:], cut(v, slice(None), j, slice(m * P, (m + 1) * P)),
                                          cut(attn, slice(None), s % RING), j == 0, j == TILES - 1)
                        mm.then_inc(o_step, 1)
                        if s == TILES + 1:
                            project(0)
                    project(1)
                trips(pe, trip_of)

            @block.scalar
            def _(act):
                def trip_of(trip, last):
                    for u in range(CHUNKS * KT):
                        c, k = divmod(u, KT)
                        act.wait_ge(shared_full, at(trip, USES, T0 + u + 1))
                        act.wait_ge(x_t_ready, at(trip, CHUNKS * KT, max(0, u - 1)))
                        for out in (xt[:, u % 2], x_t[0][:, k, c * CHUNK:(c + 1) * CHUNK]):
                            ins = act.activation(out, shared_ps[(T0 + u) % 2][:], ACT.Identity,
                                                 bias=ln_col[:, 1, k:k + 1], scale=ln_col[:, 0, k:k + 1])
                        ins.then_inc(xt_ready, 1)
                    for c in range(CHUNKS):
                        act.wait_ge(shared_full, at(trip, USES, QK0 + c + 1))
                        act.activation(qk_act[:, c], shared_ps[(QK0 + c) % 2][:], ACT.Silu,
                                       bias=qk_cols[:, 0:1]).then_inc(qk_ready, 1)
                    for m in range(HT):
                        for c in range(CHUNKS):
                            use = G0 + m * CHUNKS + c
                            act.wait_ge(shared_full, at(trip, USES, use + 1))
                            act.activation(gate_t[:, m, c * CHUNK:(c + 1) * CHUNK], shared_ps[use % 2][:], ACT.Silu,
                                           bias=gate_bias[:, m:m + 1]).then_inc(gate_ready, 1)

                    def squares(s):
                        act.wait_ge(score_full, at(trip, STEPS, s + 1))
                        act.wait_ge(attn_ready, at(trip, STEPS, max(0, s - RING + 1)))
                        act.activation(relu[:, s % RING], score_ps[s % 2][:], ACT.Relu,
                                       scale=1.0 / SEQ).then_inc(relu_ready, 1)
                        act.wait_ge(relu_ready, at(trip, STEPS, s + 1))
                        act.wait_ge(o_step, at(trip, STEPS, max(0, s - RING + 1)))
                        act.activation(attn[0][:, s % RING], relu[:, s % RING], ACT.Square).then_inc(attn_hi_ready, 1)

                    squares(0)
                    squares(1)
                    for t in range(TILES):
                        act.wait_ge(v_biased, at(trip, TILES, t + 1))
                        for out in (v[0][:, t], v_tmp[:, t % 2]):
                            ins = act.activation(out, v_tmp[:, t % 2], ACT.Silu)
                        ins.then_inc(v_hi_ready, 1)

                    def round_og(c):
                        for m in range(HT):
                            n = c * HT + m
                            act.wait_ge(og_scaled, at(trip, CHUNKS * HT, n + 1))
                            act.activation(og[0][:, m], og_tmp[:, n % 2], ACT.Copy).then_inc(og_hi_ready, 1)

                    for s in range(2, STEPS):
                        squares(s)
                        if s == TILES + 1:
                            round_og(0)
                    round_og(1)
                trips(act, trip_of)

            @block.vector
            def _(vec):
                step = Steps(vec, vec_step)

                def normalise(index):
                    def statistics():
                        vec.wait_ge(x_ln_in, at(index, 16, 16))
                        for t in range(TILES):
                            vec.bn_stats(stats[:, t], x_ln[:, t]).then_inc(vec_step, step.one())

                    def variance():
                        step.wait()
                        for t in range(TILES):
                            vec.bn_aggr(moments[:, t], stats[:, t]).then_inc(vec_step, step.one())
                        step.wait()
                        vec.tensor_scalar(var[:], moments[:, :, 1], EPS, None, ALU.add).then_inc(var_ready, 1)

                    def deviation(n):
                        vec.wait_ge(rstd_ready, at(index, 2, n))
                        newton_rsqrt(vec, step, rstd[:], var[:], scratch[:])

                    def modulate(t):
                        step.wait()
                        ins = vec.tensor_scalar(rows[:, t], x_ln[:, t], moments[:, t, 0:1], rstd[:, t:t + 1],
                                                ALU.subtract, ALU.mult)
                        if t == TILES - 1:
                            ins.then_inc(x_ln_used, 1)
                            vec.wait_ge(x_ln_used, at(index, 1, 1))
                        else:
                            ins.then_inc(vec_step, step.one())
                            step.wait()
                        vec.tensor_tensor(rows[:, t], rows[:, t], mod[:, index, SCALE_A],
                                          ALU.mult).then_inc(vec_step, step.one())
                        step.wait()
                        vec.tensor_tensor(rows[:, t], rows[:, t], mod[:, index, SHIFT_A],
                                          ALU.add).then_inc(vec_step, step.one())
                        step.wait()
                        vec.bn_stats(stats[:, t], rows[:, t]).then_inc(vec_step, step.one())

                    def again():
                        step.wait()
                        for t in range(TILES):
                            ins = vec.tensor_scalar(rows[:, t], rows[:, t], moments[:, t, 0:1], rstd[:, t:t + 1],
                                                    ALU.subtract, ALU.mult)
                        ins.then_inc(rows_ready, 1)

                    return ([statistics, variance, lambda: deviation(1)]
                            + [lambda t=t: modulate(t) for t in range(TILES)]
                            + [variance, lambda: deviation(2), again])

                for piece in normalise(0):
                    piece()
                step.restart()

                def trip_of(trip, last):
                    for u in range(CHUNKS * KT):
                        c, k = divmod(u, KT)
                        part = (slice(None), k, slice(c * CHUNK, (c + 1) * CHUNK))
                        vec.wait_ge(xt_ready, at(trip, CHUNKS * KT, u + 1))
                        vec.tensor_tensor(x_t[1][part], xt[:, u % 2], x_t[0][part].bitcast(F32),
                                          ALU.subtract).then_inc(x_t_ready, 1)
                    for c in range(CHUNKS):
                        part = (slice(None), slice(c * CHUNK, (c + 1) * CHUNK))
                        vec.wait_ge(qk_ready, at(trip, CHUNKS, c + 1))
                        vec.wait_ge(qk_split, at(trip, CHUNKS, c))
                        for n, tmp in enumerate((q_tmp, k_tmp)):
                            vec.tensor_scalar(tmp[:], qk_act[:, c], qk_cols[:, 1 + n:2 + n], qk_cols[:, 3 + n:4 + n],
                                              ALU.mult, ALU.add).then_inc(vec_step, step.one())
                        for n, (tmp, pair) in enumerate(((q_tmp, q_t), (k_tmp, k_t))):
                            step.wait(back=1)
                            vec.tensor_copy(pair[0][part], tmp[:]).then_inc(vec_step, step.one())
                        for n, (tmp, pair) in enumerate(((q_tmp, q_t), (k_tmp, k_t))):
                            step.wait(back=1 - n)
                            vec.tensor_tensor(pair[1][part], tmp[:], pair[0][part].bitcast(F32),
                                              ALU.subtract).then_inc(qk_split if n else vec_step, 1 if n else step.one())

                    def squares(s):
                        vec.wait_ge(relu_ready, at(trip, STEPS, s + 1))
                        vec.wait_ge(attn_ready, at(trip, STEPS, s))
                        vec.tensor_tensor(square[:], relu[:, s % RING], relu[:, s % RING],
                                          ALU.mult).then_inc(vec_step, step.one())
                        step.wait()
                        vec.wait_ge(attn_hi_ready, at(trip, STEPS, s + 1))
                        vec.tensor_tensor(attn[1][:, s % RING], square[:], attn[0][:, s % RING].bitcast(F32),
                                          ALU.subtract).then_inc(attn_ready, 1)

                    squares(0)
                    squares(1)

                    def v_low(t):
                        vec.wait_ge(v_hi_ready, at(trip, TILES, t + 1))
                        vec.tensor_tensor(v[1][:, t], v_tmp[:, t % 2], v[0][:, t].bitcast(F32),
                                          ALU.subtract).then_inc(v_ready, 1)

                    for t in range(TILES):
                        vec.wait_ge(shared_full, at(trip, USES, V0 + t + 1))
                        vec.wait_ge(v_ready, at(trip, TILES, max(0, t - 1)))
                        vec.tensor_tensor(v_tmp[:, t % 2], shared_ps[(V0 + t) % 2][:], v_bias[:],
                                          ALU.add).then_inc(v_biased, 1)
                        if t > 0:
                            v_low(t - 1)
                    v_low(TILES - 1)

                    def scale_og(c):
                        def low(m):
                            n = c * HT + m
                            vec.wait_ge(og_hi_ready, at(trip, CHUNKS * HT, n + 1))
                            vec.tensor_tensor(og[1][:, m], og_tmp[:, n % 2], og[0][:, m].bitcast(F32),
                                              ALU.subtract).then_inc(og_ready, 1)
                        vec.wait_ge(o_step, at(trip, STEPS, TILES * (c + 1)))
                        vec.wait_ge(shared_full, at(trip, USES, Y0 + CT * c))
                        for m in range(HT):
                            n = c * HT + m
                            vec.wait_ge(og_ready, at(trip, CHUNKS * HT, max(0, n - 1)))
                            vec.tensor_tensor(og_tmp[:, n % 2], o_ps[m][:], gate_t[:, m, c * CHUNK:(c + 1) * CHUNK],
                                              ALU.mult).then_inc(og_scaled, 1)
                            vec.wait_ge(og_scaled, at(trip, CHUNKS * HT, n + 1))
                            if m > 0:
                                low(m - 1)
                        low(HT - 1)

                    def bias_y(c):
                        for t in range(CT):
                            n = c * CT + t
                            vec.wait_ge(shared_full, at(trip, USES, Y0 + n + 1))
                            vec.wait_ge(x_ready, at(trip, TILES, max(0, n - 1)))
                            vec.tensor_tensor(y_tmp[:, n % 2], shared_ps[(Y0 + n) % 2][:, 0:DIM], out_bias[:],
                                              ALU.add).then_inc(y_biased, 1)

                    pieces = [] if last else normalise(trip + 1)
                    for s in range(2, STEPS):
                        squares(s)
                        if s == TILES + 1:
                            scale_og(0)
                        if s == TILES + 3:
                            bias_y(0)
                        if pieces:
                            pieces.pop(0)()
                    assert not pieces
                    scale_og(1)
                    bias_y(1)
                    step.restart()
                trips(vec, trip_of)


def stage_experts(nc, x_in, x_out, mod_cols_d, w):
    EXPERTS, TOP, HID = 64, 8, 64
    PAIRS = EXPERTS * HID // P
    SHARED = 2 * 512 // P
    HIDDEN = PAIRS + SHARED
    GROUP, PARTS = 32, 3
    GROUPS, ROWS = EXPERTS // GROUP, GROUP * PARTS
    NCHUNK = TOKENS // CHUNK
    PER_BATCH = SEQ // CHUNK
    LAG = 2
    with ExitStack() as ctx:
        room = Room(nc, ctx, "moe")
        sb, sem = room.sb, room.counter
        ident, ident_b = sb("ident", [P, P]), sb("ident_b", [P, P], BF16)
        w1 = room.pair("w1", [P, KT, HIDDEN * P])
        w2 = room.pair("w2", [P, HIDDEN, DIM])
        w_r = room.pair("w_r", [P, KT, EXPERTS])
        b1 = sb("b1", [P, HIDDEN])
        b2 = sb("b2", [ROWS, PARTS, GROUPS, DIM], BF16)
        shared_b2 = sb("shared_b2", [P, 2, KT])
        b2_col = sb("b2_col", [P, KT])
        router_b = sb("router_b", [P, EXPERTS])
        mod = sb("mod", [P, MOD // P, BATCH])
        spread = sb("spread", [ROWS, GROUP, HID], BF16)
        power = sb("power", [P, CT])
        QUARTER = 1024
        pieces = []
        for k in range(KT):
            for source, start, width in ((w["w1"], 0, PAIRS * P), (w["sw1"], PAIRS * P, SHARED * P)):
                for n in range(0, width, QUARTER):
                    pieces.append(((w1[0][:, k, start + n:start + n + QUARTER], w1[1][:, k, start + n:start + n + QUARTER]),
                                   source[k * P:(k + 1) * P, n:n + QUARTER]))
        for source, start, count in ((w["w2"], 0, PAIRS), (w["sw2"], PAIRS, SHARED)):
            for n in range(0, count, 4):
                pieces.append(((w2[0][:, start + n:start + n + 4], w2[1][:, start + n:start + n + 4]),
                               source[n * P:(n + 4) * P].rearrange("(m p) n -> p m n", p=P)))
        pieces.append(((w_r[0][:], w_r[1][:]), w["router_w"].rearrange("(k p) n -> p k n", p=P)))
        load_block(nc, room, [(b1[:], w["b1_cols"]), (shared_b2[:], w["sb2_cols"]),
                              (router_b[:], w["router_b"].partition_broadcast(P)), (mod[:], mod_cols_d[:, 0])],
                   pieces, ident[:])

        with ExitStack() as small_ctx:
            small = Room(nc, small_ctx, "moe_small")
            b2_raw = small.sb("b2_raw", [ROWS, GROUPS, DIM])
            b2_in, small_step, spread_step = small.sem("b2_in"), small.sem("step"), small.sem("spread_step")
            with nc.Block() as block:
                @block.sync
                def _(sp):
                    for part in range(PARTS):
                        sp.dma_start(b2_raw[part * GROUP:(part + 1) * GROUP],
                                     w["b2"].rearrange("(g e) n -> e g n", g=GROUPS)).then_inc(b2_in, 16)

                @block.gpsimd
                def _(pool):
                    step = Steps(pool, spread_step)
                    pool.memset(spread[:], 0.0).then_inc(spread_step, step.one())
                    pool.memset(power[:], -0.5).then_inc(spread_step, step.one())
                    for part in range(PARTS):
                        step.wait()
                        pool.affine_select(out=spread[:], in_=spread[:], compare_op=ALU.not_equal, fill=1.0,
                                           base=-part * GROUP, pattern=[[-1, GROUP], [0, HID]],
                                           channel_multiplier=1).then_inc(spread_step, step.one())

                @block.vector
                def _(vec):
                    step = Steps(vec, small_step)
                    vec.tensor_copy(ident_b[:], ident[:]).then_inc(small_step, step.one())
                    vec.tensor_tensor(b2_col[:], shared_b2[:, 0], shared_b2[:, 1], ALU.add).then_inc(small_step, step.one())
                    vec.wait_ge(b2_in, 16 * PARTS)
                    for part in range(PARTS):
                        step.wait()
                        vec.tensor_copy(b2[:, part], b2_raw[:]).then_inc(small_step, step.one())
                        if part < PARTS - 1:
                            step.wait()
                            vec.tensor_tensor(b2_raw[:], b2_raw[:], b2[:, part], ALU.subtract).then_inc(small_step, step.one())

        x = sb("x", [P, CT, DIM])
        rows = x
        logits, marked, weight, rest = (x[:, n].rearrange("p (t e) -> p t e", t=CT) for n in range(4))
        stats, moments = sb("stats", [P, CT, 6]), sb("moments", [P, CT, 2])
        var, rstd, scratch = sb("var", [P, CT]), sb("rstd", [P, CT]), sb("scratch", [P, CT])
        row_max, row_sum, top_sum = sb("row_max", [P, CT]), sb("row_sum", [P, CT]), sb("top_sum", [P, CT])
        top = sb("top", [P, CT, TOP])
        parts = sb("parts", [P, CT, GROUPS, PARTS, GROUP], BF16)
        xt = x[:].rearrange("p (k t) n -> p k (t n)", k=KT)
        x_t = [room.pair(f"x_t{n}", [P, KT, CHUNK]) for n in range(2)]
        weight_t = [sb(f"weight_t{n}", [ROWS, GROUPS, CHUNK], BF16) for n in range(2)]
        hidden = sb("hidden", [P, 2, CHUNK])
        y_t = hidden
        scaled = room.pair("scaled", [P, LAG, CHUNK])
        y_ps = [room.ps(f"y{n}", [P, CHUNK]) for n in range(KT)]
        hidden_ps = [room.ps(f"hidden{n}", [P, CHUNK]) for n in range(2)]
        spread_ps = [room.ps(f"spread{n}", [P, CHUNK]) for n in range(2)]
        misc_ps = [room.ps(f"misc{n}", [P, 512]) for n in range(2)]
        weight_ps = misc_ps[1][0:ROWS, :].bitcast(BF16).rearrange("p (g n) -> p g n", g=GROUPS)

        x_in_sem, res_in, x_stored = sem("x_in"), sem("res_in"), sem("x_stored")
        var_ready, rstd_ready, rows_ready = sem("var_ready"), sem("rstd_ready"), sem("rows_ready")
        turned, xt_ready, x_t_ready = sem("turned"), sem("xt_ready"), sem("x_t_ready")
        router_full, shifted, exp_ready = sem("router_full"), sem("shifted"), sem("exp_ready")
        weight_split, weight_full, weight_t_ready = sem("weight_split"), sem("weight_full"), sem("weight_t_ready")
        hidden_full, hidden_ready, scaled_ready, y_step = (
            sem("hidden_full"), sem("hidden_ready"), sem("scaled_ready"), sem("y_step"))
        y_t_ready, y_back, x_ready = sem("y_t_ready"), sem("y_back"), sem("x_ready")
        vec_step = room.sem("vec_step")

        src = x_in.rearrange("(c t p) n -> c p t n", c=NCHUNK, p=P)
        dst = x_out.rearrange("(c t p) n -> c p t n", c=NCHUNK, p=P)

        def chunks(engine, prepare_first, main, end):
            prepare_first()
            main(0, 0, False, True)
            with engine.Fori(0, (NCHUNK - 2) // 2) as trip:
                main(trip * 2 + 1, 1, True, True)
                main(trip * 2 + 2, 0, True, True)
            main(NCHUNK - 1, 1, True, False)
            end()

        start_counters(nc, room)
        with nc.Block() as block:
            @block.sync
            def _(sp):
                def load_next(c):
                    sp.dma_start(x[:], src[c]).then_inc(x_in_sem, 16)

                def store(c):
                    sp.wait_ge(x_ready, at(c, KT, KT))
                    sp.dma_start(dst[c], x[:]).then_inc(x_stored, 16)
                    sp.wait_ge(x_stored, at(c, 16, 16))

                def main(c, slot, back, prepare):
                    if back:
                        store(c - 1)
                    if prepare:
                        load_next(c + 1)
                        sp.wait_ge(weight_split, at(c + 1, 1, 1))
                    sp.dma_start(x[:], src[c]).then_inc(res_in, 16)

                def first():
                    load_next(0)
                    sp.wait_ge(weight_split, at(0, 1, 1))
                chunks(sp, first, main, lambda: store(NCHUNK - 1))

            @block.gpsimd
            def _(pool):
                def rsqrt(c):
                    pool.wait_ge(var_ready, at(c, 1, 1))
                    pool.tensor_tensor(rstd[:], var[:], power[:], ALU.pow).then_inc(rstd_ready, 1)
                chunks(pool, lambda: rsqrt(0), lambda c, slot, back, prepare: rsqrt(c + 1) if prepare else None,
                       lambda: None)

            @block.tensor
            def _(pe):
                def turn(c, slot):
                    pe.wait_ge(rows_ready, at(c, 1, 1))
                    if not (isinstance(c, int) and c == 0):
                        pe.wait_ge(x_ready, at(c - 1, KT, 0))
                    for k in range(KT):
                        for t in range(CT):
                            mm = pe.transpose(misc_ps[k][:, t * P:(t + 1) * P], rows[:, t, k * P:(k + 1) * P], ident[:])
                        mm.then_inc(turned, 1)

                def route(c, slot):
                    pe.wait_ge(x_t_ready, at(c, KT, KT))
                    for t in range(CT):
                        for k in range(KT):
                            mm = product3(pe, misc_ps[0][:, t * EXPERTS:(t + 1) * EXPERTS],
                                          cut(x_t[slot], slice(None), k, slice(t * P, (t + 1) * P)),
                                          cut(w_r, slice(None), k), k == 0, k == KT - 1)
                    mm.then_inc(router_full, 1)

                def turn_weights(c, slot):
                    pe.wait_ge(weight_split, at(c, 1, 1))
                    for t in range(CT):
                        for g in range(GROUPS):
                            mm = pe.transpose(weight_ps[:, g, t * P:(t + 1) * P],
                                              parts[:, t, g].rearrange("p a e -> p (a e)"), ident_b[:])
                    mm.then_inc(weight_full, 1)

                def turn_back(c):
                    pe.wait_ge(y_t_ready, at(c, KT, KT))
                    pe.wait_ge(x_ready, at(c, KT, 0))
                    for t in range(CT):
                        for d in range(KT):
                            mm = pe.transpose(misc_ps[t // 2][:, (t % 2) * DIM + d * P:(t % 2) * DIM + (d + 1) * P],
                                              y_t[:, d, t * P:(t + 1) * P], ident[:])
                        if t % 2:
                            mm.then_inc(y_back, 1)

                def main(c, slot, back, prepare):
                    def first_product(q):
                        pe.wait_ge(scaled_ready, at(c, HIDDEN, max(0, q - 1)))
                        if q < PAIRS:
                            g, e = divmod(2 * q, GROUP)
                            pe.matmul(spread_ps[q % 2][:], spread[:, e:e + 2].rearrange("p e h -> p (e h)"), weight_t[slot][:, g],
                                      start=True, stop=True)
                        for k in range(KT):
                            mm = product3(pe, hidden_ps[q % 2][:], cut(w1, slice(None), k, slice(q * P, (q + 1) * P)),
                                          cut(x_t[slot], slice(None), k), k == 0, k == KT - 1)
                        mm.then_inc(hidden_full, 1)

                    def second_product(q):
                        pe.wait_ge(scaled_ready, at(c, HIDDEN, q + 1))
                        for d in range(KT):
                            mm = product3(pe, y_ps[d][:], cut(w2, slice(None), q, slice(d * P, (d + 1) * P)),
                                          cut(scaled, slice(None), q % LAG), False, q == HIDDEN - 1)
                        mm.then_inc(y_step, 1)

                    pe.wait_ge(weight_t_ready, at(c, 1, 1))
                    first_product(0)
                    first_product(1)
                    if back:
                        turn_back(c - 1)
                    for d in range(KT):
                        for part in range(PARTS):
                            for g in range(GROUPS):
                                pe.matmul(y_ps[d][:], b2[:, part, g, d * P:(d + 1) * P], weight_t[slot][:, g],
                                          start=(part == 0 and g == 0), stop=False)
                    for q in range(LAG, HIDDEN):
                        first_product(q)
                        second_product(q - LAG)
                        if prepare:
                            {10: turn, 14: route, 28: turn_weights}.get(q, lambda *_: None)(c + 1, 1 - slot)
                    second_product(HIDDEN - 2)
                    second_product(HIDDEN - 1)

                def first():
                    turn(0, 0)
                    route(0, 0)
                    turn_weights(0, 0)
                chunks(pe, first, main, lambda: turn_back(NCHUNK - 1))

            @block.scalar
            def _(act):
                def turn(c, slot):
                    b = c // PER_BATCH
                    for k in range(KT):
                        act.wait_ge(turned, at(c, KT, KT))
                        for out in (xt[:, k], x_t[slot][0][:, k]):
                            ins = act.activation(out, misc_ps[k][:], ACT.Identity,
                                                 bias=mod[:, SHIFT_B * KT + k, bass.ds(b, 1)],
                                                 scale=mod[:, SCALE_B * KT + k, bass.ds(b, 1)])
                        ins.then_inc(xt_ready, 1)

                def exponentials(c):
                    act.wait_ge(shifted, at(c, 1, 1))
                    act.activation(logits, logits, ACT.Exp).then_inc(exp_ready, 1)

                def turn_weights(c, slot):
                    act.wait_ge(weight_full, at(c, 1, 1))
                    act.activation(weight_t[slot][:], weight_ps, ACT.Copy).then_inc(weight_t_ready, 1)

                def main(c, slot, back, prepare):
                    act.wait_ge(y_back, at(c, KT, 0))
                    for q in range(HIDDEN):
                        act.wait_ge(hidden_full, at(c, HIDDEN, q + 1))
                        act.wait_ge(scaled_ready, at(c, HIDDEN, max(0, q - 1)))
                        act.activation(hidden[:, q % 2], hidden_ps[q % 2][:], ACT.Silu,
                                       bias=b1[:, q:q + 1]).then_inc(hidden_ready, 1)
                        if prepare and q == 10:
                            turn(c + 1, 1 - slot)
                        if prepare and q == 16:
                            exponentials(c + 1)
                        if prepare and q == 28:
                            turn_weights(c + 1, 1 - slot)

                def first():
                    turn(0, 0)
                    exponentials(0)
                    turn_weights(0, 0)
                chunks(act, first, main, lambda: None)

            @block.vector
            def _(vec):
                step = Steps(vec, vec_step)

                def own(ins):
                    return ins.then_inc(vec_step, step.one())

                def prepare_pieces(c, slot):
                    def statistics():
                        vec.wait_ge(x_in_sem, at(c, 16, 16))
                        for t in range(CT):
                            vec.bn_stats(stats[:, t], x[:, t]).then_inc(vec_step, step.one())
                        step.wait()
                        for t in range(CT):
                            vec.bn_aggr(moments[:, t], stats[:, t]).then_inc(vec_step, step.one())
                        step.wait()
                        vec.tensor_scalar(var[:], moments[:, :, 1], EPS, None, ALU.add).then_inc(var_ready, 1)

                    def normalise():
                        vec.wait_ge(rstd_ready, at(c, 1, 1))
                        newton_rsqrt(vec, step, rstd[:], var[:], scratch[:])
                        step.wait()
                        for t in range(CT):
                            ins = vec.tensor_scalar(rows[:, t], x[:, t], moments[:, t, 0:1], rstd[:, t:t + 1],
                                                    ALU.subtract, ALU.mult)
                        ins.then_inc(rows_ready, 1)

                    def low_halves():
                        for k in range(KT):
                            vec.wait_ge(xt_ready, at(c, KT, k + 1))
                            vec.tensor_tensor(x_t[slot][1][:, k], xt[:, k], x_t[slot][0][:, k].bitcast(F32),
                                              ALU.subtract).then_inc(x_t_ready, 1)

                    def shift():
                        vec.wait_ge(router_full, at(c, 1, 1))
                        vec.tensor_tensor(logits, misc_ps[0][:, 0:CT * EXPERTS].rearrange("p (t e) -> p t e", t=CT),
                                          router_b[:].unsqueeze(1).to_broadcast([P, CT, EXPERTS]),
                                          ALU.add).then_inc(vec_step, step.one())
                        step.wait()
                        vec.tensor_reduce(row_max[:], logits, X_AXIS, ALU.max).then_inc(vec_step, step.one())
                        step.wait()
                        vec.tensor_tensor(logits, logits, column(row_max[:], CT, EXPERTS),
                                          ALU.subtract).then_inc(shifted, 1)

                    def probabilities():
                        vec.wait_ge(exp_ready, at(c, 1, 1))
                        vec.tensor_reduce(row_sum[:], logits, X_AXIS, ALU.add).then_inc(vec_step, step.one())
                        step.wait()
                        vec.reciprocal(row_sum[:], row_sum[:]).then_inc(vec_step, step.one())
                        step.wait()
                        vec.tensor_tensor(logits, logits, column(row_sum[:], CT, EXPERTS),
                                          ALU.mult).then_inc(vec_step, step.one())

                    def choose():
                        step.wait()
                        for t in range(CT):
                            vec.max(top[:, t], logits[:, t]).then_inc(vec_step, step.one())
                        step.wait()
                        for t in range(CT):
                            vec.match_replace(marked[:, t], top[:, t], logits[:, t], -1.0).then_inc(vec_step, step.one())
                        vec.tensor_reduce(top_sum[:], top[:], X_AXIS, ALU.add).then_inc(vec_step, step.one())
                        step.wait()
                        vec.scalar_tensor_tensor(weight, marked, 0.0, logits, ALU.is_lt, ALU.mult).then_inc(vec_step, step.one())
                        vec.reciprocal(top_sum[:], top_sum[:]).then_inc(vec_step, step.one())
                        step.wait()
                        vec.tensor_tensor(weight, weight, column(top_sum[:], CT, EXPERTS),
                                          ALU.mult).then_inc(vec_step, step.one())

                    def split():
                        for part in range(PARTS):
                            from_ = weight if part == 0 else rest
                            step.wait()
                            ins = vec.tensor_copy(parts[:, :, :, part], from_.rearrange("p t (g e) -> p t g e", g=GROUPS))
                            if part == PARTS - 1:
                                ins.then_inc(weight_split, 1)
                            else:
                                ins.then_inc(vec_step, step.one())
                                step.wait()
                                vec.tensor_tensor(rest.rearrange("p t (g e) -> p t g e", g=GROUPS),
                                                  from_.rearrange("p t (g e) -> p t g e", g=GROUPS),
                                                  parts[:, :, :, part], ALU.subtract).then_inc(vec_step, step.one())

                    return {5: statistics, 7: normalise, 10: low_halves, 15: shift, 18: probabilities, 20: choose,
                            23: split}

                def add_back(c):
                    vec.wait_ge(res_in, at(c, 16, 16))
                    for half in range(KT):
                        vec.wait_ge(y_back, at(c, KT, half + 1))
                        part = x[:, 2 * half:2 * half + 2].rearrange("p t n -> p (t n)")
                        vec.tensor_tensor(part, part, misc_ps[half][:], ALU.add).then_inc(x_ready, 1)

                def main(c, slot, back, prepare):
                    b = c // PER_BATCH
                    if back:
                        add_back(c - 1)
                    pieces = prepare_pieces(c + 1, 1 - slot) if prepare else {}
                    for q in range(HIDDEN):
                        vec.wait_ge(hidden_ready, at(c, HIDDEN, q + 1))
                        if q < PAIRS:
                            vec.tensor_tensor(hidden[:, q % 2], hidden[:, q % 2], spread_ps[q % 2][:],
                                              ALU.mult).then_inc(vec_step, step.one())
                            step.wait()
                        vec.wait_ge(y_step, at(c, HIDDEN, max(0, q - LAG + 1)))
                        vec.tensor_copy(scaled[0][:, q % LAG], hidden[:, q % 2]).then_inc(vec_step, step.one())
                        step.wait()
                        vec.tensor_tensor(scaled[1][:, q % LAG], hidden[:, q % 2], scaled[0][:, q % LAG].bitcast(F32),
                                          ALU.subtract).then_inc(scaled_ready, 1)
                        if q in pieces:
                            pieces[q]()
                    vec.wait_ge(y_step, at(c, HIDDEN, HIDDEN))
                    vec.wait_ge(scaled_ready, at(c, HIDDEN, HIDDEN))
                    for d in range(KT):
                        vec.tensor_scalar(y_t[:, d], y_ps[d][:], b2_col[:, d:d + 1], mod[:, GATE_B * KT + d, bass.ds(b, 1)],
                                          ALU.add, ALU.mult).then_inc(y_t_ready, 1)
                    step.restart()

                def first():
                    for piece in prepare_pieces(0, 0).values():
                        piece()
                    step.restart()
                chunks(vec, first, main, lambda: add_back(NCHUNK - 1))


HEADS, HEAD_DIM = 16, 16
ROWS_V, QUERY_V = 8, 32
V_ALL = ROWS_V * HEAD_DIM
V_SCORE, V_ONE, V_QUERY = V_ALL, V_ALL + ROWS_V, V_ALL + ROWS_V + 2
V_WIDTH = V_QUERY + HEADS
V_USED = V_ONE + 1
SPLITS = 3


def stage_project(nc, x_in, h_d, parts_d, values_d, mod_d, w):
    T_USES, QK_USES, V_USES = CHUNKS * KT, 2 * KT * CHUNKS, TILES
    USES, BANKS = T_USES + QK_USES + V_USES, 4
    assert USES % BANKS == 0
    with ExitStack() as ctx:
        room = Room(nc, ctx, "pj")
        sb, sem = room.sb, room.counter
        ident = sb("ident", [P, P])
        w_q, w_k = room.pair("w_q", [P, KT, DIM]), room.pair("w_k", [P, KT, DIM])
        w_v = room.pair("w_v", [P, KT, V_WIDTH])
        cols = sb("cols", [P, 4, KT])
        q_bias = sb("q_bias", [P, KT])
        v_bias = sb("v_bias", [P, V_WIDTH])
        mod = sb("mod", [P, BATCH, 2, DIM])
        mod_now = sb("mod_now", [P, 2, DIM])
        power = sb("power", [P, TILES])
        load_block(nc, room, [
            (cols[:], w["cols"]),
            (mod[:], mod_d[1, :, 0:2 * DIM].rearrange("b (w n) -> b w n", n=DIM).partition_broadcast(P)),
        ], [((w_q[0][:, k], w_q[1][:, k]), w["WqT"][k * P:(k + 1) * P]) for k in range(KT)]
            + [((w_k[0][:, k], w_k[1][:, k]), w["WkT"][k * P:(k + 1) * P]) for k in range(KT)], ident[:])

        with ExitStack() as fold_ctx:
            fold = Room(nc, fold_ctx, "pj_fold")
            raw = fold.sb("raw", [P, KT, V_WIDTH])
            wqv = fold.sb("wqv", [P, KT, HEADS * QUERY_V])
            bqv = fold.sb("bqv", [P, HEADS * QUERY_V])
            ws = fold.sb("ws", [P, QUERY_V + HEAD_DIM + 1])
            prod_v = fold.sb("prod_v", [P, KT + 1, V_ALL])
            fold_in, fold_step, fold_const = fold.sem("in"), fold.sem("step"), fold.sem("const")
            with nc.Block() as block:
                @block.sync
                def _(sp):
                    loads = [(raw[:, :, 0:V_ALL], w["WvT"].rearrange("(k p) n -> p k n", p=P)),
                             (wqv[:], w["WqvT"].rearrange("(k p) n -> p k n", p=P)),
                             (bqv[:], w["bqv"].partition_broadcast(P)),
                             (v_bias[:, 0:V_ALL], w["bv"].partition_broadcast(P)),
                             (ws[:, 0:QUERY_V + HEAD_DIM], w["Ws"].rearrange("a n -> (a n)").partition_broadcast(P)),
                             (ws[:, QUERY_V + HEAD_DIM:], w["bs"].partition_broadcast(P))]
                    for destination, source in loads:
                        sp.dma_start(destination, source).then_inc(fold_in, 16)

                @block.gpsimd
                def _(pool):
                    pool.memset(power[:], -0.5).then_inc(fold_const, 1)

                @block.vector
                def _(vec):
                    step = Steps(vec, fold_step)
                    vec.memset(raw[:, :, V_ONE:V_QUERY], 0.0).then_inc(fold_step, step.one())
                    vec.memset(v_bias[:, V_ONE:V_ONE + 1], 1.0).then_inc(fold_step, step.one())
                    vec.memset(v_bias[:, V_ONE + 1:V_QUERY], 0.0).then_inc(fold_step, step.one())
                    vec.tensor_scalar(q_bias[:], cols[:, 2], float(HEAD_DIM) ** -0.5, None,
                                      ALU.mult).then_inc(fold_step, step.one())
                    vec.wait_ge(fold_in, 16 * 6)
                    for n, source in enumerate([raw[:, k, 0:V_ALL] for k in range(KT)] + [v_bias[:, 0:V_ALL]]):
                        vec.tensor_tensor(prod_v[:, n].rearrange("p (r d) -> p r d", d=HEAD_DIM),
                                          source.rearrange("p (r d) -> p r d", d=HEAD_DIM),
                                          ws[:, QUERY_V:QUERY_V + HEAD_DIM].unsqueeze(1).to_broadcast([P, ROWS_V, HEAD_DIM]),
                                          ALU.mult).then_inc(fold_step, step.one())
                    step.wait()
                    for n, out in enumerate([raw[:, k, V_SCORE:V_ONE] for k in range(KT)] + [v_bias[:, V_SCORE:V_ONE]]):
                        vec.tensor_reduce(out, prod_v[:, n].rearrange("p (r d) -> p r d", d=HEAD_DIM), X_AXIS,
                                          ALU.add).then_inc(fold_step, step.one())
                    query = [(wqv[:, k], raw[:, k, V_QUERY:]) for k in range(KT)] + [(bqv[:], v_bias[:, V_QUERY:])]
                    for source, out in query:
                        vec.tensor_tensor(source.rearrange("p (h n) -> p h n", n=QUERY_V),
                                          source.rearrange("p (h n) -> p h n", n=QUERY_V),
                                          ws[:, 0:QUERY_V].unsqueeze(1).to_broadcast([P, HEADS, QUERY_V]),
                                          ALU.mult).then_inc(fold_step, step.one())
                    step.wait()
                    for source, out in query:
                        vec.tensor_reduce(out, source.rearrange("p (h n) -> p h n", n=QUERY_V), X_AXIS,
                                          ALU.add).then_inc(fold_step, step.one())
                    step.wait()
                    for source, out in query:
                        vec.tensor_scalar(out, out, float(QUERY_V) ** -0.5, None, ALU.mult).then_inc(fold_step, step.one())
                    step.wait()
                    vec.tensor_scalar(v_bias[:, V_QUERY:], v_bias[:, V_QUERY:], ws[:, QUERY_V + HEAD_DIM:], None,
                                      ALU.add).then_inc(fold_step, step.one())
                    vec.tensor_copy(w_v[0][:], raw[:]).then_inc(fold_step, step.one())
                    step.wait()
                    vec.tensor_tensor(w_v[1][:], raw[:], w_v[0][:].bitcast(F32), ALU.subtract).then_inc(fold_step, step.one())

        x = sb("x", [P, TILES, DIM])
        h = sb("h", [P, TILES, DIM])
        rows = sb("rows", [P, TILES, DIM])
        stats, moments = sb("stats", [P, TILES, 6]), sb("moments", [P, TILES, 2])
        var, rstd, scratch = sb("var", [P, TILES]), sb("rstd", [P, TILES]), sb("scratch", [P, TILES])
        xt = sb("xt", [P, 2, CHUNK])
        x_t = room.pair("x_t", [P, KT, SEQ])
        qk_tmp = sb("qk_tmp", [P, 2, CHUNK])
        parts = sb("parts", [P, 2, KT, SPLITS, SEQ], BF16)
        values = sb("values", [P, TILES, V_WIDTH])
        banks = [room.ps(f"bank{n}", [P, 512]) for n in range(BANKS)]

        x_in_sem, x_used = sem("x_in"), sem("x_used")
        var_ready, rstd_ready = sem("var_ready"), sem("rstd_ready")
        normal_ready, h_scaled, h_ready, h_stored = sem("normal_ready"), sem("h_scaled"), sem("h_ready"), sem("h_stored")
        mod_copied = sem("mod_copied")
        rows_ready = sem("rows_ready")
        full = sem("full")
        xt_ready, x_t_ready = sem("xt_ready"), sem("x_t_ready")
        part_ready, parts_ready, parts_stored = sem("part_ready"), sem("parts_ready"), sem("parts_stored")
        values_ready, values_stored = sem("values_ready"), sem("values_stored")
        vec_step = room.sem("vec_step")

        src = x_in.rearrange("(b t p) n -> b p t n", b=BATCH, p=P)
        dst_h = h_d.rearrange("(b t p) n -> b p t n", b=BATCH, p=P)
        dst_v = values_d.rearrange("(b t p) n -> b p t n", b=BATCH, p=P)

        def trips(engine, body):
            with engine.Fori(0, BATCH - 1) as trip:
                body(trip, False)
            body(BATCH - 1, True)

        def bank_free(pe, trip, use):
            u = use - BANKS
            if u < 0:
                pe.wait_ge(values_ready, at(trip, TILES, 0))
            elif u < T_USES:
                pe.wait_ge(xt_ready, at(trip, T_USES, u + 1))
            elif u < T_USES + QK_USES:
                pe.wait_ge(part_ready, at(trip, QK_USES, u - T_USES + 1))
            else:
                pe.wait_ge(values_ready, at(trip, TILES, u - T_USES - QK_USES + 1))

        start_counters(nc, room)
        with nc.Block() as block:
            @block.sync
            def _(sp):
                def h_out(index):
                    sp.wait_ge(h_ready, at(index, TILES, TILES))
                    sp.dma_start(dst_h[index], h[:]).then_inc(h_stored, 16)
                sp.dma_start(x[:], src[0]).then_inc(x_in_sem, 16)
                h_out(0)

                def trip_of(trip, last):
                    if not last:
                        sp.wait_ge(x_used, at(trip, 1, 1))
                        sp.dma_start(x[:], src[trip + 1]).then_inc(x_in_sem, 16)
                    for n in range(2 * KT):
                        which, m = divmod(n, KT)
                        sp.wait_ge(parts_ready, at(trip, QK_USES, CHUNKS * (n + 1)))
                        sp.dma_start(parts_d[which, trip, :, m * P:(m + 1) * P, :].rearrange("s p n -> p s n"),
                                     parts[:, which, m]).then_inc(parts_stored, 16)
                    sp.wait_ge(values_ready, at(trip, TILES, TILES))
                    sp.dma_start(dst_v[trip], values[:]).then_inc(values_stored, 16)
                    if not last:
                        h_out(trip + 1)
                trips(sp, trip_of)
                sp.wait_ge(h_stored, at(BATCH, 16, 0))
                sp.wait_ge(parts_stored, at(BATCH, 16 * 2 * KT, 0))
                sp.wait_ge(values_stored, at(BATCH, 16, 0))

            @block.gpsimd
            def _(pool):
                def rows_of(index):
                    pool.wait_ge(h_ready, at(index, TILES, 0))
                    pool.wait_ge(var_ready, at(index, 2, 1))
                    pool.tensor_tensor(rstd[:], var[:], power[:], ALU.pow).then_inc(rstd_ready, 1)
                    pool.tensor_copy(mod_now[:], mod[:, index]).then_inc(mod_copied, 1)
                    pool.wait_ge(mod_copied, at(index, 1, 1))
                    for t in range(TILES):
                        pool.wait_ge(normal_ready, at(index, TILES, t + 1))
                        pool.tensor_tensor(h[:, t], h[:, t], mod_now[:, SCALE_A], ALU.mult).then_inc(h_scaled, 1)
                        pool.wait_ge(h_scaled, at(index, TILES, t + 1))
                        pool.tensor_tensor(h[:, t], h[:, t], mod_now[:, SHIFT_A], ALU.add).then_inc(h_ready, 1)
                    pool.wait_ge(var_ready, at(index, 2, 2))
                    pool.tensor_tensor(rstd[:], var[:], power[:], ALU.pow).then_inc(rstd_ready, 1)
                rows_of(0)
                trips(pool, lambda trip, last: None if last else rows_of(trip + 1))

            @block.tensor
            def _(pe):
                def trip_of(trip, last):
                    pe.wait_ge(rows_ready, at(trip, 1, 1))
                    for u in range(T_USES):
                        c, k = divmod(u, KT)
                        bank_free(pe, trip, u)
                        for t in range(CT):
                            mm = pe.transpose(banks[u % BANKS][:, t * P:(t + 1) * P],
                                              rows[:, c * CT + t, k * P:(k + 1) * P], ident[:])
                        mm.then_inc(full, 1)
                    for n in range(QK_USES):
                        which, m, c = n // (KT * CHUNKS), n // CHUNKS % KT, n % CHUNKS
                        use = T_USES + n
                        bank_free(pe, trip, use)
                        pe.wait_ge(x_t_ready, at(trip, T_USES, KT * (c + 1)))
                        for k in range(KT):
                            mm = product3(pe, banks[use % BANKS][:],
                                          cut((w_q, w_k)[which], slice(None), k, slice(m * P, (m + 1) * P)),
                                          cut(x_t, slice(None), k, slice(c * CHUNK, (c + 1) * CHUNK)),
                                          k == 0, k == KT - 1)
                        mm.then_inc(full, 1)
                    for t in range(TILES):
                        use = T_USES + QK_USES + t
                        bank_free(pe, trip, use)
                        for k in range(KT):
                            mm = product3(pe, banks[use % BANKS][:, 0:V_WIDTH],
                                          cut(x_t, slice(None), k, slice(t * P, (t + 1) * P)),
                                          cut(w_v, slice(None), k), k == 0, k == KT - 1)
                        mm.then_inc(full, 1)
                trips(pe, trip_of)

            @block.scalar
            def _(act):
                def trip_of(trip, last):
                    for u in range(T_USES):
                        c, k = divmod(u, KT)
                        act.wait_ge(full, at(trip, USES, u + 1))
                        act.wait_ge(x_t_ready, at(trip, T_USES, max(0, u - 1)))
                        for out in (xt[:, u % 2], x_t[0][:, k, c * CHUNK:(c + 1) * CHUNK]):
                            ins = act.activation(out, banks[u % BANKS][:], ACT.Identity,
                                                 bias=cols[:, 1, k:k + 1], scale=cols[:, 0, k:k + 1])
                        ins.then_inc(xt_ready, 1)
                    act.wait_ge(parts_stored, at(trip, 16 * 2 * KT, 0))
                    for n in range(QK_USES):
                        which, m, c = n // (KT * CHUNKS), n // CHUNKS % KT, n % CHUNKS
                        use = T_USES + n
                        act.wait_ge(full, at(trip, USES, use + 1))
                        act.wait_ge(parts_ready, at(trip, QK_USES, max(0, n - 1)))
                        bias = cols[:, 3, m:m + 1] if which else q_bias[:, m:m + 1]
                        for out in (qk_tmp[:, n % 2], parts[:, which, m, 0, c * CHUNK:(c + 1) * CHUNK]):
                            ins = act.activation(out, banks[use % BANKS][:], ACT.Identity, bias=bias,
                                                 scale=1.0 if which else float(HEAD_DIM) ** -0.5)
                        ins.then_inc(part_ready, 1)
                trips(act, trip_of)

            @block.vector
            def _(vec):
                step = Steps(vec, vec_step)

                def normalise(index):
                    def variance():
                        step.wait()
                        for t in range(TILES):
                            vec.bn_aggr(moments[:, t], stats[:, t]).then_inc(vec_step, step.one())
                        step.wait()
                        vec.tensor_scalar(var[:], moments[:, :, 1], EPS, None, ALU.add).then_inc(var_ready, 1)

                    def statistics():
                        vec.wait_ge(x_in_sem, at(index, 16, 16))
                        for t in range(TILES):
                            vec.bn_stats(stats[:, t], x[:, t]).then_inc(vec_step, step.one())
                        variance()

                    def first():
                        vec.wait_ge(rstd_ready, at(index, 2, 1))
                        newton_rsqrt(vec, step, rstd[:], var[:], scratch[:])
                        step.wait()
                        vec.wait_ge(h_stored, at(index, 16, 0))
                        for t in range(TILES):
                            vec.tensor_scalar(h[:, t], x[:, t], moments[:, t, 0:1], rstd[:, t:t + 1],
                                              ALU.subtract, ALU.mult).then_inc(normal_ready, 1)

                    def statistics_h(t):
                        vec.wait_ge(h_ready, at(index, TILES, t + 1))
                        vec.bn_stats(stats[:, t], h[:, t]).then_inc(vec_step, step.one())

                    def last():
                        vec.wait_ge(rstd_ready, at(index, 2, 2))
                        newton_rsqrt(vec, step, rstd[:], var[:], scratch[:])
                        step.wait()
                        for t in range(TILES):
                            ins = vec.tensor_scalar(rows[:, t], h[:, t], moments[:, t, 0:1], rstd[:, t:t + 1],
                                                    ALU.subtract, ALU.mult)
                        ins.then_inc(rows_ready, 1)

                    def x_free():
                        vec.wait_ge(normal_ready, at(index, TILES, TILES))
                        vec.tensor_copy(scratch[:, 0:1], scratch[:, 0:1]).then_inc(x_used, 1)

                    return ([statistics, first, x_free] + [lambda t=t: statistics_h(t) for t in range(TILES)]
                            + [variance, last])

                for piece in normalise(0):
                    piece()
                step.restart()

                def trip_of(trip, last):
                    pieces = [] if last else normalise(trip + 1)
                    for u in range(T_USES):
                        c, k = divmod(u, KT)
                        part = (slice(None), k, slice(c * CHUNK, (c + 1) * CHUNK))
                        vec.wait_ge(xt_ready, at(trip, T_USES, u + 1))
                        vec.tensor_tensor(x_t[1][part], xt[:, u % 2], x_t[0][part].bitcast(F32),
                                          ALU.subtract).then_inc(x_t_ready, 1)
                    for n in range(QK_USES):
                        which, m, c = n // (KT * CHUNKS), n // CHUNKS % KT, n % CHUNKS
                        tmp = qk_tmp[:, n % 2]
                        out = [parts[:, which, m, s, c * CHUNK:(c + 1) * CHUNK] for s in range(SPLITS)]
                        vec.wait_ge(part_ready, at(trip, QK_USES, n + 1))
                        vec.tensor_tensor(tmp, tmp, out[0], ALU.subtract).then_inc(vec_step, step.one())
                        step.wait()
                        vec.tensor_copy(out[1], tmp).then_inc(vec_step, step.one())
                        step.wait()
                        vec.tensor_tensor(out[2], tmp, out[1], ALU.subtract).then_inc(parts_ready, 1)
                        if pieces and n >= 1:
                            pieces.pop(0)()
                    vec.wait_ge(values_stored, at(trip, 16, 0))
                    for t in range(TILES):
                        use = T_USES + QK_USES + t
                        vec.wait_ge(full, at(trip, USES, use + 1))
                        vec.tensor_tensor(values[:, t], banks[use % BANKS][:, 0:V_WIDTH], v_bias[:],
                                          ALU.add).then_inc(values_ready, 1)
                        if pieces:
                            pieces.pop(0)()
                    for piece in pieces:
                        piece()
                    step.restart()
                trips(vec, trip_of)


def stage_attention(nc, parts_d, values_d, attended):
    ALL = BATCH * HEADS
    TERMS = 6
    STACK = TERMS * HEAD_DIM
    SHIFT = SPLITS * TILES
    FULL = STACK + SHIFT
    SLOTS = 4
    HALVES = SEQ // 512
    GROUP = 3
    GROUPS = -(-TILES // GROUP)
    AHEAD = 2
    SPREAD_SLOT = TILES - AHEAD
    COMPOSE_SLOT = 1
    with ExitStack() as ctx:
        room = Room(nc, ctx, "at")
        sb, sem = room.sb, room.counter
        values = sb("values", [P, BATCH * TILES, V_WIDTH])
        q_stack = [sb(f"q_stack{n}", [P, SEQ], BF16) for n in range(SLOTS)]
        k_stack = [sb(f"k_stack{n}", [P, SEQ], BF16) for n in range(SLOTS)]
        prob = [sb(f"prob{n}", [P, TILES, SEQ]) for n in range(2)]
        half_max, q_max = sb("half_max", [P, TILES, HALVES]), sb("q_max", [P, TILES])
        max_cols = sb("max_cols", [P, P], BF16)
        ident = sb("ident", [P, P], BF16)
        mask = sb("mask", [P, TILES])
        mixed = [sb(f"mixed{n}", [P, TILES, V_USED]) for n in range(2)]
        recip, weight = sb("recip", [P, TILES]), sb("weight", [P, TILES, ROWS_V])
        row_max, row_sum = sb("row_max", [P, TILES]), sb("row_sum", [P, TILES])
        product = sb("product", [P, TILES, ROWS_V, HEAD_DIM])
        max_ps = [room.ps(f"max{n}", [P, 512]) for n in range(HALVES)]
        score_ps = [room.ps(f"score{n}", [P, SEQ]) for n in range(2)]
        out_ps = [room.ps(f"out{n}", [P, 512]) for n in range(2)]
        turned_ps = max_ps[0][:].bitcast(BF16)[:, 0:P]

        values_in = room.sem("values_in")
        constants, const_step = room.sem("constants"), room.sem("const_step")
        q_in, k_in = [sem(f"q_in{n}") for n in range(SLOTS)], [sem(f"k_in{n}") for n in range(SLOTS)]
        max_full = [sem(f"max_full{n}") for n in range(HALVES)]
        max_read, max_split, max_turned, shift_ready = (
            sem("max_read"), sem("max_split"), sem("max_turned"), sem("shift_ready"))
        score_full, prob_ready = sem("score_full"), sem("prob_ready")
        out_full, mixed_ready = sem("out_full"), sem("mixed_ready")
        weight_shifted, weight_exp, weight_ready = sem("weight_shifted"), sem("weight_exp"), sem("weight_ready")
        composed, pool_step, vec_step = sem("composed"), room.sem("pool_step"), room.sem("vec_step")
        STACK_DMAS = TERMS

        class Head:
            def __init__(self, trip, offset):
                self.trip, self.offset = trip, offset
                self.slot, self.half = offset % SLOTS, offset % 2
                self.number = trip * SLOTS + offset

            def back(self, n):
                return Head(self.trip, self.offset - n)

            def at(self, per_head, step):
                return self.trip * (SLOTS * per_head) + (START + self.offset * per_head + step)

            def slot_at(self, per_use):
                return self.trip * per_use + (START + (self.offset // SLOTS + 1) * per_use)

        def steps(engine, body):
            fill = 3
            for n in range(-1, fill):
                body(Head(0, n), n)
            loops = (ALL - 2 - fill) // SLOTS
            with engine.Fori(0, loops) as trip:
                for n in range(SLOTS):
                    body(Head(trip, fill + n), None)
            for n in range(fill + loops * SLOTS, ALL + 3):
                body(Head(0, n), n)

        def stages(u, number):
            def there(back):
                return number is None or 0 <= number - back < ALL
            return [u.back(n) if there(n) else None for n in (0, 1, 2, 3, -1)]

        def max_work(maxima, following, t):
            head, tile = (maxima, t + AHEAD) if t < TILES - AHEAD else (following, t + AHEAD - TILES)
            return (head, tile) if head else None

        start_counters(nc, room)
        with nc.Block() as block:
            @block.sync
            def _(sp):
                sp.dma_start(values[:], values_d.rearrange("(t p) n -> p t n", p=P)).then_inc(values_in, 16)

                def load(head):
                    number = head.number
                    b, h = number // HEADS, number % HEADS
                    for n, (q_part, k_part) in enumerate(((0, 0), (1, 0), (2, 0), (0, 1), (1, 1), (0, 2))):
                        for which, part, stack, landed in ((0, q_part, q_stack, q_in), (1, k_part, k_stack, k_in)):
                            sp.dma_start(stack[head.slot][n * HEAD_DIM:(n + 1) * HEAD_DIM, :],
                                         parts_d[which, b, part, bass.ds(h * HEAD_DIM, HEAD_DIM), :]
                                         ).then_inc(landed[head.slot], 16)

                load(Head(0, 0))

                def step_of(u, number):
                    if number is None or number + 2 < ALL:
                        if number is None or number >= 2:
                            sp.wait_ge(score_full, u.back(2).at(TILES, TILES))
                        load(u.back(-2))
                steps(sp, step_of)

            @block.gpsimd
            def _(pool):
                step = Steps(pool, const_step)
                for buffer, value in [(max_cols[:], 0.0), (ident[:], 0.0), (mask[:], 0.0)] + [
                        (k_stack[n][STACK:P, :], 1.0) for n in range(SLOTS)]:
                    pool.memset(buffer, value).then_inc(const_step, step.one())
                    step.wait()
                pool.affine_select(out=ident[:], in_=ident[:], compare_op=ALU.not_equal, fill=1.0, base=0,
                                   pattern=[[-1, P]], channel_multiplier=1).then_inc(const_step, step.one())
                step.wait()
                for part in range(SPLITS):
                    pool.affine_select(out=mask[:], in_=mask[:], compare_op=ALU.not_equal, fill=1.0,
                                       base=-(STACK + part * TILES), pattern=[[-1, TILES]],
                                       channel_multiplier=1).then_inc(const_step, step.one())
                    step.wait()
                pool.memset(product[:, 0, 0, 0:1], 0.0).then_inc(constants, 1)
                sums = Steps(pool, pool_step)

                def step_of(u, number):
                    head = stages(u, number)[3]
                    if head is None:
                        return
                    b, h = head.number // HEADS, head.number % HEADS
                    pool.wait_ge(weight_ready, head.at(1, 1))
                    pool.wait_ge(composed, head.at(1, 0))
                    pool.tensor_tensor(product[:].rearrange("p t r d -> p t (r d)").rearrange("p t (r d) -> p t r d", d=HEAD_DIM),
                                       mixed[head.half][:, :, 0:V_ALL].rearrange("p t (r d) -> p t r d", d=HEAD_DIM),
                                       weight[:].unsqueeze(3).to_broadcast([P, TILES, ROWS_V, HEAD_DIM]),
                                       ALU.mult).then_inc(pool_step, sums.one())
                    n = ROWS_V // 2
                    while n > 1:
                        sums.wait()
                        pool.tensor_tensor(product[:, :, 0:n], product[:, :, 0:n], product[:, :, n:2 * n],
                                           ALU.add).then_inc(pool_step, sums.one())
                        n //= 2
                    sums.wait()
                    pool.tensor_tensor(attended[:, bass.ds(b * TILES, TILES), bass.ds(h * HEAD_DIM, HEAD_DIM)],
                                       product[:, :, 0], product[:, :, 1], ALU.add).then_inc(composed, 1)
                    sums.restart()
                steps(pool, step_of)

            @block.tensor
            def _(pe):
                pe.wait_ge(constants, 1)
                pe.wait_ge(values_in, 16)

                def step_of(u, number):
                    maxima, scoring, mixing, _, following = stages(u, number)

                    def max_tile(head, t):
                        if t == 0:
                            pe.wait_ge(q_in[head.slot], head.slot_at(16 * STACK_DMAS))
                            pe.wait_ge(k_in[head.slot], head.slot_at(16 * STACK_DMAS))
                        for half in range(HALVES):
                            if t == 0 and half == 0:
                                pe.wait_ge(shift_ready, head.at(1, 0))
                            pe.wait_ge(max_read, head.at(TILES * HALVES, max(0, t * HALVES + half - HALVES + 1)))
                            pe.matmul(max_ps[half][:], q_stack[head.slot][0:STACK, t * P:(t + 1) * P],
                                      k_stack[head.slot][0:STACK, half * 512:(half + 1) * 512],
                                      start=True, stop=True).then_inc(max_full[half], 1)

                    def score_tile(j):
                        head = scoring
                        if j == 0:
                            pe.wait_ge(shift_ready, head.at(1, 1))
                        pe.wait_ge(prob_ready, head.at(TILES, max(0, j - 1)))
                        for half in range(HALVES):
                            mm = pe.matmul(score_ps[j % 2][:, half * 512:(half + 1) * 512],
                                           k_stack[head.slot][0:FULL, j * P:(j + 1) * P],
                                           q_stack[head.slot][0:FULL, half * 512:(half + 1) * 512],
                                           start=True, stop=True)
                        mm.then_inc(score_full, 1)

                    def mix_tile(t, between=None):
                        head = mixing
                        b = head.number // HEADS
                        group = head.offset * GROUPS + t // GROUP
                        bank = out_ps[group % 2]
                        place = (t % GROUP) * V_USED
                        if t == 0:
                            pe.wait_ge(prob_ready, head.at(TILES, TILES))
                        if t % GROUP == 0:
                            back = t // GROUP - 1
                            if back >= 0:
                                pe.wait_ge(mixed_ready, head.at(GROUPS, back))
                            elif number is None or head.offset > 0:
                                pe.wait_ge(mixed_ready, head.back(1).at(GROUPS, GROUPS - 1))
                        for j in range(TILES):
                            if j == TILES // 2 and between:
                                between()
                            mm = pe.matmul(bank[:, place:place + V_USED], prob[head.half][:, j, t * P:(t + 1) * P],
                                           values[:, b * TILES + j, 0:V_USED], start=(j == 0), stop=(j == TILES - 1))
                        if t % GROUP == GROUP - 1 or t == TILES - 1:
                            mm.then_inc(out_full, 1)

                    for t in range(TILES):
                        work = max_work(maxima, following, t)
                        middle = t > SPREAD_SLOT and mixing
                        if work and t != SPREAD_SLOT and not middle:
                            max_tile(*work)
                        if scoring:
                            score_tile(t)
                        if maxima and t == SPREAD_SLOT:
                            pe.wait_ge(max_split, maxima.at(1, 1))
                            pe.transpose(turned_ps, max_cols[:], ident[:]).then_inc(max_turned, 1)
                        if mixing:
                            mix_tile(t, (lambda: max_tile(*work)) if work and middle else None)
                        if work and t == SPREAD_SLOT:
                            max_tile(*work)
                steps(pe, step_of)

            @block.scalar
            def _(act):
                def step_of(u, number):
                    _, scoring, mixing, composing, _ = stages(u, number)

                    def copy_group(g):
                        head = mixing
                        act.wait_ge(out_full, head.at(GROUPS, g + 1))
                        if g == 0 and (number is None or number >= 4):
                            act.wait_ge(composed, head.back(2).at(1, 1))
                        n = min(GROUP, TILES - g * GROUP)
                        bank = out_ps[(head.offset * GROUPS + g) % 2]
                        act.activation(mixed[head.half][:, g * GROUP:g * GROUP + n],
                                       bank[:, 0:n * V_USED].rearrange("p (t v) -> p t v", v=V_USED),
                                       ACT.Copy).then_inc(mixed_ready, 1)

                    for t in range(TILES):
                        if scoring:
                            act.wait_ge(score_full, scoring.at(TILES, t + 1))
                            act.activation(prob[scoring.half][:, t], score_ps[t % 2][:], ACT.Exp).then_inc(prob_ready, 1)
                        if mixing and t in (GROUP, 2 * GROUP):
                            copy_group(t // GROUP - 1)
                        if composing and t == COMPOSE_SLOT + 1:
                            act.wait_ge(weight_shifted, composing.at(1, 1))
                            act.activation(weight[:], weight[:], ACT.Exp).then_inc(weight_exp, 1)
                    if mixing:
                        copy_group(GROUPS - 1)
                steps(act, step_of)

            @block.vector
            def _(vec):
                step = Steps(vec, vec_step)
                vec.wait_ge(constants, 1)
                vec.wait_ge(values_in, 16)

                def step_of(u, number):
                    maxima, _, _, composing, following = stages(u, number)

                    def read_max(head, t):
                        for half in range(HALVES):
                            vec.wait_ge(max_full[half], head.at(TILES, t + 1))
                            vec.tensor_reduce(half_max[:, t, half:half + 1], max_ps[half][:], X_AXIS,
                                              ALU.max).then_inc(max_read, 1)

                    def split_max():
                        vec.wait_ge(max_read, maxima.at(TILES * HALVES, TILES * HALVES))
                        vec.tensor_reduce(q_max[:], half_max[:], X_AXIS, ALU.max, negate=True).then_inc(vec_step, step.one())
                        for part in range(SPLITS):
                            step.wait()
                            place = max_cols[:, STACK + part * TILES:STACK + (part + 1) * TILES]
                            ins = vec.tensor_copy(place, q_max[:])
                            if part == SPLITS - 1:
                                ins.then_inc(max_split, 1)
                            else:
                                ins.then_inc(vec_step, step.one())
                                step.wait()
                                vec.tensor_tensor(q_max[:], q_max[:], place, ALU.subtract).then_inc(vec_step, step.one())

                    def spread_max():
                        vec.wait_ge(max_turned, maxima.at(1, 1))
                        vec.tensor_tensor(q_stack[maxima.slot][STACK:FULL, :].rearrange("p (t n) -> p t n", t=TILES),
                                          turned_ps[STACK:FULL, :].unsqueeze(1).to_broadcast([SHIFT, TILES, P]),
                                          mask[STACK:FULL, :].unsqueeze(2).to_broadcast([SHIFT, TILES, P]),
                                          ALU.mult).then_inc(shift_ready, 1)

                    def composition():
                        head = composing
                        b, h = head.number // HEADS, head.number % HEADS
                        m = mixed[head.half]
                        vec.wait_ge(mixed_ready, head.at(GROUPS, GROUPS))
                        vec.reciprocal(recip[:], m[:, :, V_ONE]).then_inc(vec_step, step.one())
                        step.wait()
                        if number is None or head.offset > 0:
                            vec.wait_ge(composed, head.at(1, 0))
                        vec.tensor_tensor(weight[:], m[:, :, V_SCORE:V_ONE], column(recip[:], TILES, ROWS_V),
                                          ALU.mult).then_inc(vec_step, step.one())
                        step.wait()
                        vec.tensor_tensor(weight[:], weight[:],
                                          values[:, bass.ds(b * TILES, TILES), bass.ds(h + V_QUERY, 1)].to_broadcast([P, TILES, ROWS_V]),
                                          ALU.add).then_inc(vec_step, step.one())
                        step.wait()
                        vec.tensor_reduce(row_max[:], weight[:], X_AXIS, ALU.max).then_inc(vec_step, step.one())
                        step.wait()
                        vec.tensor_tensor(weight[:], weight[:], column(row_max[:], TILES, ROWS_V),
                                          ALU.subtract).then_inc(weight_shifted, 1)

                    def composition_weights():
                        vec.wait_ge(weight_exp, composing.at(1, 1))
                        vec.tensor_reduce(row_sum[:], weight[:], X_AXIS, ALU.add).then_inc(vec_step, step.one())
                        step.wait()
                        vec.reciprocal(row_sum[:], row_sum[:]).then_inc(vec_step, step.one())
                        step.wait()
                        vec.tensor_tensor(row_sum[:], row_sum[:], recip[:], ALU.mult).then_inc(vec_step, step.one())
                        step.wait()
                        vec.tensor_tensor(weight[:], weight[:], column(row_sum[:], TILES, ROWS_V),
                                          ALU.mult).then_inc(weight_ready, 1)

                    for t in range(TILES):
                        work = max_work(maxima, following, t)
                        if maxima and t == SPREAD_SLOT:
                            spread_max()
                        if work:
                            read_max(*work)
                        if composing and t == COMPOSE_SLOT:
                            composition()
                        if composing and t == COMPOSE_SLOT + 2:
                            composition_weights()
                        if maxima and t == SPREAD_SLOT - 1:
                            split_max()
                    step.restart()
                steps(vec, step_of)


def stage_tail(nc, attended, h_d, x_in, out_d, mod_d, mod_cols_d, w):
    HIDDEN = 2 * DIM
    HT = HIDDEN // P
    PAIRS = CT // 2
    BANKS, F_SLOTS = 8, HT + HT // 2
    uses = []
    for kind, n in (("A", CHUNKS * KT), ("B", CHUNKS * PAIRS), ("C", CHUNKS * KT)):
        uses += [(kind, i) for i in range(n)]
    uses += [("D", i) for i in range(HT + HT // 2)] + [("E", i) for i in range(PAIRS)]
    uses += [("D", i) for i in range(HT + HT // 2, 2 * HT)] + [("E", i) for i in range(PAIRS, 2 * PAIRS)]
    uses += [("G", i) for i in range(CHUNKS * KT)]
    for c in range(CHUNKS):
        uses += [("R", c * PAIRS + i) for i in range(PAIRS)] + [("K", c * KT + i) for i in range(KT)]
    uses += [("V", i) for i in range(CHUNKS * PAIRS)]
    USES = len(uses)
    assert USES % BANKS == 0
    KINDS = {kind: sum(k == kind for k, _ in uses) for kind in "ABCDEGRKV"}
    with ExitStack() as ctx:
        room = Room(nc, ctx, "tl")
        sb, sem = room.sb, room.counter
        ident = sb("ident", [P, P])
        w_f, w_r1, w_r2 = (room.pair("w_f", [P, KT, DIM]), room.pair("w_r1", [P, KT, HIDDEN]),
                           room.pair("w_r2", [P, HT, DIM]))
        w_r, w_k, w_v = (room.pair(f"w_{n}", [P, KT, DIM]) for n in "rkv")
        cols = sb("cols", [P, 12])
        G2, B2, BR1, MU = 0, KT, 2 * KT, 2 * KT + HT
        rest = sb("rest", [P, 2, KT])
        f_bias, r2_bias = sb("f_bias", [P, DIM]), sb("r2_bias", [P, DIM])
        mod_cols = sb("mod_cols", [P, MOD // P, BATCH])
        by_k = lambda source: source.rearrange("(k p) n -> p k n", p=P)
        load_block(nc, room, [
            (cols[:], w["cols"]),
            (f_bias[:], w["bf"].partition_broadcast(P)),
            (r2_bias[:], w["br2"].partition_broadcast(P)),
            (mod_cols[:], mod_cols_d[:, 1]),
        ], [((pair[0][:], pair[1][:]), by_k(source)) for pair, source in (
            (w_f, w["WfT"]), (w_r1, w["Wr1T"]), (w_r2, w["Wr2T"]),
            (w_r, w["W_rT"]), (w_k, w["W_kT"]), (w_v, w["W_vT"]))], ident[:])

        att = sb("att", [P, TILES, DIM])
        h, x, r, hat = (sb(n, [P, TILES, DIM]) for n in ("h", "x", "r", "hat"))
        a_t = room.pair("a_t", [P, KT, SEQ])
        b_t = room.pair("b_t", [P, KT, SEQ])
        f = room.pair("f", [P, F_SLOTS, CHUNK])
        tmp = sb("tmp", [P, 2, CHUNK])
        y = sb("y", [P, 2, 2, DIM])
        h_t = sb("h_t", [P, KT, SEQ + 1])
        before, mixed = sb("before", [P, 2, CHUNK]), sb("mixed", [P, 2, CHUNK])
        relu, square = sb("relu", [P, 2, CHUNK]), sb("square", [P, CHUNK])
        sig = sb("sig", [P, TILES, DIM])
        gates = sb("gates", [P, 2, DIM])
        gated_bias = sb("gated_bias", [P, DIM])
        mod_now = sb("mod_now", [P, 2, KT])
        stats, moments = sb("stats", [P, TILES, 6]), sb("moments", [P, TILES, 2])
        var, rstd, scratch = sb("var", [P, TILES]), sb("rstd", [P, TILES]), sb("scratch", [P, TILES])
        power = sb("power", [P, CT])
        banks = [room.ps(f"bank{n}", [P, 512]) for n in range(BANKS)]

        att_in, h_in, x_in_sem, gates_in, out_stored = (
            sem("att_in"), sem("h_in"), sem("x_in"), sem("gates_in"), sem("out_stored"))
        zero_ready, rest_ready, full = room.sem("zero_ready"), room.sem("rest_ready"), sem("full")
        a_hi_ready, a_ready = sem("a_hi_ready"), sem("a_ready")
        h_biased, r_ready = sem("h_biased"), sem("r_ready")
        var_ready, rstd_ready, hat_ready = sem("var_ready"), sem("rstd_ready"), sem("hat_ready")
        b_hi_ready, b_ready = sem("b_hi_ready"), sem("b_ready")
        f_hi_ready, f_ready = sem("f_hi_ready"), sem("f_ready")
        y_ready, x1_ready = sem("y_ready"), sem("x1_ready")
        h_t_ready, before_ready, mixed_ready = sem("h_t_ready"), sem("before_ready"), sem("mixed_ready")
        rows_hi_ready, rows_ready = sem("rows_hi_ready"), sem("rows_ready")
        sig_ready, relu_ready, k_hi_ready, k_ready = (
            sem("sig_ready"), sem("relu_ready"), sem("k_hi_ready"), sem("k_ready"))
        product_ready, out_ready = sem("product_ready"), sem("out_ready")
        vec_step, pool_step = room.sem("vec_step"), room.sem("pool_step")

        bank_read = {"A": a_ready, "B": r_ready, "C": b_hi_ready, "D": f_hi_ready, "E": y_ready,
                     "G": h_t_ready, "R": sig_ready, "K": relu_ready, "V": product_ready}
        number = {use: n for n, use in enumerate(uses)}

        def bank(kind, n):
            return banks[number[kind, n] % BANKS]

        def wait_full(engine, trip, kind, n):
            engine.wait_ge(full, at(trip, USES, number[kind, n] + 1))

        rows_of = lambda dram: dram.rearrange("(b t p) n -> b p t n", b=BATCH, p=P)
        chunk = lambda c: slice(c * CHUNK, (c + 1) * CHUNK)
        pair_of = lambda n: slice(2 * n, 2 * n + 2)

        start_counters(nc, room)
        with nc.Block() as block:
            @block.sync
            def _(sp):
                def load_first(index):
                    sp.dma_start(att[:], attended[:, bass.ds(index * TILES, TILES), :]).then_inc(att_in, 16)

                def load_h(index):
                    sp.dma_start(h[:], rows_of(h_d)[index]).then_inc(h_in, 16)

                load_first(0)
                load_h(0)

                def trip_of(trip, last):
                    sp.wait_ge(out_ready, at(trip, CHUNKS * PAIRS, 0))
                    sp.dma_start(gates[:, 0], mod_d[1, trip, GATE_A * DIM:(GATE_A + 1) * DIM]
                                 .partition_broadcast(P)).then_inc(gates_in, 16)
                    sp.dma_start(gates[:, 1], mod_d[1, trip, GATE_B * DIM:(GATE_B + 1) * DIM]
                                 .partition_broadcast(P)).then_inc(gates_in, 16)
                    sp.wait_ge(out_stored, at(trip, 16, 0))
                    sp.dma_start(x[:], rows_of(x_in)[trip]).then_inc(x_in_sem, 16)
                    if not last:
                        wait_full(sp, trip, "A", CHUNKS * KT - 1)
                        load_first(trip + 1)
                        sp.wait_ge(r_ready, at(trip, KINDS["B"], KINDS["B"]))
                        load_h(trip + 1)
                    sp.wait_ge(out_ready, at(trip, CHUNKS * PAIRS, CHUNKS * PAIRS))
                    sp.dma_start(rows_of(out_d)[trip], x[:]).then_inc(out_stored, 16)

                with sp.Fori(0, BATCH - 1) as trip:
                    trip_of(trip, False)
                trip_of(BATCH - 1, True)
                sp.wait_ge(out_stored, at(BATCH, 16, 0))

            @block.gpsimd
            def _(pool):
                pool.memset(power[:], -0.5).then_inc(pool_step, 1)
                pool.wait_ge(pool_step, 1)
                pool.memset(h_t[:, :, 0:1], 0.0).then_inc(zero_ready, 1)
                pool.wait_ge(zero_ready, 1)
                pool.sem_clear(pool_step)
                step = Steps(pool, pool_step)

                with pool.Fori(0, BATCH) as trip:
                    def deviation(norm, c):
                        pool.wait_ge(var_ready, at(trip, 2 * CHUNKS, norm * CHUNKS + c + 1))
                        pool.tensor_tensor(rstd[:, c * CT:(c + 1) * CT], var[:, c * CT:(c + 1) * CT], power[:],
                                           ALU.pow).then_inc(rstd_ready, 1)

                    def over_tiles(row, n):
                        return row.unsqueeze(1).to_broadcast([P, n, DIM])

                    pool.wait_ge(h_t_ready, at(trip, KINDS["G"], 0))
                    pool.wait_ge(h_in, at(trip, 16, 16))
                    for c in range(CHUNKS):
                        part = h[:, c * CT:(c + 1) * CT]
                        pool.tensor_tensor(part, part, over_tiles(f_bias[:], CT), ALU.add).then_inc(h_biased, 1)
                    pool.tensor_copy(mod_now[:].rearrange("p w k -> p (w k)"),
                                     mod_cols[:, SHIFT_B * KT:(SCALE_B + 1) * KT, trip]).then_inc(pool_step, step.one())
                    deviation(0, 0)
                    deviation(0, 1)
                    pool.wait_ge(gates_in, at(trip, 32, 32))
                    pool.tensor_tensor(gated_bias[:], gates[:, 0], r2_bias[:], ALU.mult).then_inc(pool_step, step.one())
                    pool.wait_ge(x_in_sem, at(trip, 16, 16))
                    step.wait()
                    for c in range(CHUNKS):
                        part = x[:, c * CT:(c + 1) * CT]
                        pool.tensor_tensor(part, part, over_tiles(gated_bias[:], CT), ALU.add).then_inc(pool_step, step.one())
                    step.wait()
                    for n in range(CHUNKS * PAIRS):
                        part = y[:, n % 2]
                        pool.wait_ge(y_ready, at(trip, KINDS["E"], n + 1))
                        pool.tensor_tensor(part, part, over_tiles(gates[:, 0], 2), ALU.mult).then_inc(pool_step, step.one())
                        step.wait()
                        pool.tensor_tensor(x[:, pair_of(n)], x[:, pair_of(n)], part, ALU.add).then_inc(x1_ready, 1)
                        if n == PAIRS - 1:
                            deviation(1, 0)
                    deviation(1, 1)
                    pool.wait_ge(x1_ready, at(trip, CHUNKS * PAIRS, CHUNKS * PAIRS))
                    for n in range(CHUNKS * PAIRS):
                        part = sig[:, pair_of(n)]
                        pool.wait_ge(product_ready, at(trip, KINDS["V"], n + 1))
                        pool.tensor_tensor(part, part, over_tiles(gates[:, 1], 2), ALU.mult).then_inc(pool_step, step.one())
                        step.wait()
                        pool.tensor_tensor(x[:, pair_of(n)], x[:, pair_of(n)], part, ALU.add).then_inc(out_ready, 1)
                    step.restart()

            @block.tensor
            def _(pe):
                with pe.Fori(0, BATCH) as trip:
                    def free(kind, n):
                        u = number[kind, n] - BANKS
                        if u >= 0:
                            old, i = uses[u]
                            pe.wait_ge(bank_read[old], at(trip, KINDS[old], i + 1))
                        else:
                            old, _ = uses[u + USES]
                            pe.wait_ge(bank_read[old], at(trip, KINDS[old], 0))

                    def turn(kind, n, source):
                        c, k = divmod(n, KT)
                        free(kind, n)
                        for t in range(CT):
                            mm = pe.transpose(bank(kind, n)[:, t * P:(t + 1) * P],
                                              source[:, c * CT + t, k * P:(k + 1) * P], ident[:])
                        mm.then_inc(full, 1)

                    def to_features(kind, n, weights, m, moving, c):
                        free(kind, n)
                        for k in range(KT):
                            mm = product3(pe, bank(kind, n)[:], cut(weights, slice(None), k, slice(m * P, (m + 1) * P)),
                                          cut(moving, slice(None), k, chunk(c)), k == 0, k == KT - 1)
                        mm.then_inc(full, 1)

                    def to_tokens(kind, n, tiles, weights, inner):
                        free(kind, n)
                        for i in range(2):
                            for k in range(inner):
                                mm = product3(pe, bank(kind, n)[:, i * DIM:(i + 1) * DIM], tiles(k, 2 * n + i),
                                              cut(weights, slice(None), k), k == 0, k == inner - 1)
                        mm.then_inc(full, 1)

                    def tiles_of(pair):
                        return lambda k, t: cut(pair, slice(None), k, slice(t * P, (t + 1) * P))

                    pe.wait_ge(att_in, at(trip, 16, 16))
                    for n in range(KINDS["A"]):
                        turn("A", n, att)
                    for n in range(KINDS["B"]):
                        pe.wait_ge(a_ready, at(trip, KINDS["A"], KT * (n // PAIRS + 1)))
                        to_tokens("B", n, tiles_of(a_t), w_f, KT)
                    for n in range(KINDS["C"]):
                        pe.wait_ge(hat_ready, at(trip, 2 * CHUNKS, n // KT + 1))
                        turn("C", n, hat)

                    def expand(n):
                        c, m = divmod(n, HT)
                        pe.wait_ge(b_ready, at(trip, KINDS["C"], KT * (c + 1)))
                        to_features("D", n, w_r1, m, b_t, c)

                    def contract(c):
                        pe.wait_ge(f_ready, at(trip, KINDS["D"], HT * (c + 1)))
                        for i in range(PAIRS):
                            to_tokens("E", c * PAIRS + i, lambda m, t: cut(
                                f, slice(None), (c * HT + m) % F_SLOTS, slice(t % CT * P, (t % CT + 1) * P)), w_r2, HT)

                    for n in range(F_SLOTS):
                        expand(n)
                    contract(0)
                    for n in range(F_SLOTS, 2 * HT):
                        expand(n)
                    contract(1)
                    for n in range(KINDS["G"]):
                        pe.wait_ge(hat_ready, at(trip, 2 * CHUNKS, CHUNKS + n // KT + 1))
                        turn("G", n, hat)
                    for c in range(CHUNKS):
                        pe.wait_ge(rows_ready, at(trip, 4 * KT, 2 * KT * c + KT))
                        for i in range(PAIRS):
                            to_tokens("R", c * PAIRS + i, tiles_of(a_t), w_r, KT)
                        pe.wait_ge(rows_ready, at(trip, 4 * KT, 2 * KT * c + 2 * KT))
                        for m in range(KT):
                            to_features("K", c * KT + m, w_k, m, b_t, c)
                    for n in range(KINDS["V"]):
                        c = n // PAIRS
                        pe.wait_ge(k_ready, at(trip, KINDS["K"], KT * (c + 1)))
                        to_tokens("V", n, lambda m, t: cut(
                            f, slice(None), c * KT + m, slice(t % CT * P, (t % CT + 1) * P)), w_v, KT)

            @block.scalar
            def _(act):
                act.wait_ge(zero_ready, 1)
                act.wait_ge(rest_ready, 1)
                with act.Fori(0, BATCH) as trip:
                    for n in range(KINDS["A"]):
                        c, k = divmod(n, KT)
                        wait_full(act, trip, "A", n)
                        act.activation(a_t[0][:, k, chunk(c)], bank("A", n)[:], ACT.Copy).then_inc(a_hi_ready, 1)
                    for n in range(KINDS["C"]):
                        c, k = divmod(n, KT)
                        wait_full(act, trip, "C", n)
                        act.wait_ge(b_ready, at(trip, KINDS["C"], max(0, n - 1)))
                        if n < 2:
                            act.wait_ge(f_ready, at(trip, KINDS["D"], 0))
                        for out in (tmp[:, n % 2], b_t[0][:, k, chunk(c)]):
                            ins = act.activation(out, bank("C", n)[:], ACT.Identity, bias=cols[:, B2 + k:B2 + k + 1],
                                                 scale=cols[:, G2 + k:G2 + k + 1])
                        ins.then_inc(b_hi_ready, 1)

                    def expanded(n):
                        m = n % HT
                        wait_full(act, trip, "D", n)
                        if n < 2:
                            act.wait_ge(b_ready, at(trip, KINDS["C"], KINDS["C"] + n - 1))
                        else:
                            act.wait_ge(f_ready, at(trip, KINDS["D"], n - 1))
                        if n >= F_SLOTS:
                            wait_full(act, trip, "E", PAIRS - 1)
                        for out in (tmp[:, n % 2], f[0][:, n % F_SLOTS]):
                            ins = act.activation(out, bank("D", n)[:], ACT.Relu, bias=cols[:, BR1 + m:BR1 + m + 1])
                        ins.then_inc(f_hi_ready, 1)
                    for n in range(KINDS["D"]):
                        expanded(n)

                    def token_before(n):
                        c, which, k = n // (2 * KT), n // KT % 2, n % KT
                        act.wait_ge(h_t_ready, at(trip, KINDS["G"], KT * c + k + 1))
                        act.wait_ge(mixed_ready, at(trip, 4 * KT, max(0, n - 1)))
                        act.activation(before[:, n % 2], h_t[:, k, chunk(c)], ACT.Copy,
                                       scale=rest[:, which, k:k + 1]).then_inc(before_ready, 1)

                    def rows_high(n):
                        c, which, k = n // (2 * KT), n // KT % 2, n % KT
                        act.wait_ge(mixed_ready, at(trip, 4 * KT, n + 1))
                        act.activation((a_t, b_t)[which][0][:, k, chunk(c)], mixed[:, n % 2],
                                       ACT.Copy).then_inc(rows_hi_ready, 1)

                    for c in range(CHUNKS):
                        for k in range(KT):
                            wait_full(act, trip, "G", c * KT + k)
                            act.activation(h_t[:, k, 1 + c * CHUNK:1 + (c + 1) * CHUNK], bank("G", c * KT + k)[:],
                                           ACT.Identity, bias=mod_now[:, 0, k:k + 1],
                                           scale=mod_now[:, 1, k:k + 1]).then_inc(h_t_ready, 1)
                        for n in range(2 * KT * c, 2 * KT * (c + 1)):
                            token_before(n)
                            if n % (2 * KT):
                                rows_high(n - 1)
                        rows_high(2 * KT * (c + 1) - 1)
                    act.wait_ge(out_ready, at(trip, CHUNKS * PAIRS, 0))
                    for c in range(CHUNKS):
                        for n in range(c * PAIRS, (c + 1) * PAIRS):
                            wait_full(act, trip, "R", n)
                            act.activation(sig[:, pair_of(n)], bank("R", n)[:].rearrange("p (t n) -> p t n", n=DIM),
                                           ACT.Sigmoid).then_inc(sig_ready, 1)
                        for n in range(c * KT, (c + 1) * KT):
                            wait_full(act, trip, "K", n)
                            act.wait_ge(k_ready, at(trip, KINDS["K"], max(0, n - 1)))
                            act.activation(relu[:, n % 2], bank("K", n)[:], ACT.Relu).then_inc(relu_ready, 1)
                            act.wait_ge(relu_ready, at(trip, KINDS["K"], n + 1))
                            act.activation(f[0][:, n], relu[:, n % 2], ACT.Square).then_inc(k_hi_ready, 1)

            @block.vector
            def _(vec):
                for which in range(2):
                    ins = vec.tensor_scalar(rest[:, which], cols[:, MU + which * KT:MU + (which + 1) * KT], -1.0, 1.0,
                                            ALU.mult, ALU.add)
                ins.then_inc(rest_ready, 1)
                vec.wait_ge(rest_ready, 1)
                vec.wait_ge(zero_ready, 1)
                step = Steps(vec, vec_step)

                with vec.Fori(0, BATCH) as trip:
                    def low(pair, index, whole, hi_sem, per, n, done):
                        vec.wait_ge(hi_sem, at(trip, per, n + 1))
                        vec.tensor_tensor(pair[1][index], whole, pair[0][index].bitcast(F32),
                                          ALU.subtract).then_inc(done, 1)

                    def statistics(rows, c):
                        for t in range(c * CT, (c + 1) * CT):
                            vec.bn_stats(stats[:, t], rows[:, t]).then_inc(vec_step, step.one())
                        step.wait()
                        for t in range(c * CT, (c + 1) * CT):
                            vec.bn_aggr(moments[:, t], stats[:, t]).then_inc(vec_step, step.one())
                        step.wait()
                        part = slice(c * CT, (c + 1) * CT)
                        vec.tensor_scalar(var[:, part], moments[:, part, 1], EPS, None, ALU.add).then_inc(var_ready, 1)

                    def normalise(rows, norm, c):
                        part = slice(c * CT, (c + 1) * CT)
                        vec.wait_ge(rstd_ready, at(trip, 2 * CHUNKS, norm * CHUNKS + c + 1))
                        newton_rsqrt(vec, step, rstd[:, part], var[:, part], scratch[:, part])
                        step.wait()
                        for t in range(c * CT, (c + 1) * CT):
                            ins = vec.tensor_scalar(hat[:, t], rows[:, t], moments[:, t, 0:1], rstd[:, t:t + 1],
                                                    ALU.subtract, ALU.mult)
                        ins.then_inc(hat_ready, 1)

                    for n in range(KINDS["A"]):
                        c, k = divmod(n, KT)
                        low(a_t, (slice(None), k, chunk(c)), bank("A", n)[:], a_hi_ready, KINDS["A"], n, a_ready)
                    for c in range(CHUNKS):
                        vec.wait_ge(h_biased, at(trip, CHUNKS, c + 1))
                        for n in range(c * PAIRS, (c + 1) * PAIRS):
                            wait_full(vec, trip, "B", n)
                            vec.tensor_tensor(r[:, pair_of(n)], bank("B", n)[:].rearrange("p (t n) -> p t n", n=DIM),
                                              h[:, pair_of(n)], ALU.add).then_inc(r_ready, 1)
                        vec.wait_ge(r_ready, at(trip, KINDS["B"], (c + 1) * PAIRS))
                        statistics(r, c)
                    for c in range(CHUNKS):
                        normalise(r, 0, c)
                    for n in range(KINDS["C"]):
                        c, k = divmod(n, KT)
                        low(b_t, (slice(None), k, chunk(c)), tmp[:, n % 2], b_hi_ready, KINDS["C"], n, b_ready)

                    def f_low(n):
                        low(f, (slice(None), n % F_SLOTS), tmp[:, n % 2], f_hi_ready, KINDS["D"], n, f_ready)

                    def with_residual(n):
                        wait_full(vec, trip, "E", n)
                        vec.wait_ge(x1_ready, at(trip, CHUNKS * PAIRS, max(0, n - 1)))
                        vec.tensor_tensor(y[:, n % 2], bank("E", n)[:].rearrange("p (t n) -> p t n", n=DIM),
                                          r[:, pair_of(n)], ALU.add).then_inc(y_ready, 1)

                    for n in range(F_SLOTS):
                        f_low(n)
                    for n in range(PAIRS):
                        with_residual(n)
                    for n in range(F_SLOTS, 2 * HT):
                        f_low(n)
                    vec.wait_ge(x1_ready, at(trip, CHUNKS * PAIRS, PAIRS))
                    statistics(x, 0)
                    for n in range(PAIRS, 2 * PAIRS):
                        with_residual(n)
                    normalise(x, 1, 0)
                    vec.wait_ge(x1_ready, at(trip, CHUNKS * PAIRS, 2 * PAIRS))
                    statistics(x, 1)
                    normalise(x, 1, 1)

                    def rows_low(n):
                        c, which, k = n // (2 * KT), n // KT % 2, n % KT
                        low((a_t, b_t)[which], (slice(None), k, chunk(c)), mixed[:, n % 2], rows_hi_ready, 4 * KT, n,
                            rows_ready)

                    for n in range(4 * KT):
                        c, which, k = n // (2 * KT), n // KT % 2, n % KT
                        vec.wait_ge(before_ready, at(trip, 4 * KT, n + 1))
                        vec.wait_ge(rows_ready, at(trip, 4 * KT, max(0, n - 1)))
                        vec.scalar_tensor_tensor(mixed[:, n % 2], h_t[:, k, 1 + c * CHUNK:1 + (c + 1) * CHUNK],
                                                 cols[:, MU + which * KT + k:MU + which * KT + k + 1],
                                                 before[:, n % 2], ALU.mult, ALU.add).then_inc(mixed_ready, 1)
                        if n % (2 * KT):
                            rows_low(n - 1)
                        if n % (2 * KT) == 2 * KT - 1:
                            rows_low(n)
                    for n in range(KINDS["K"]):
                        vec.wait_ge(relu_ready, at(trip, KINDS["K"], n + 1))
                        vec.wait_ge(k_ready, at(trip, KINDS["K"], n))
                        vec.tensor_tensor(square[:], relu[:, n % 2], relu[:, n % 2], ALU.mult).then_inc(vec_step, step.one())
                        step.wait()
                        low(f, (slice(None), n), square[:], k_hi_ready, KINDS["K"], n, k_ready)
                    for n in range(KINDS["V"]):
                        wait_full(vec, trip, "V", n)
                        vec.wait_ge(sig_ready, at(trip, KINDS["R"], n + 1))
                        vec.tensor_tensor(sig[:, pair_of(n)], bank("V", n)[:].rearrange("p (t n) -> p t n", n=DIM),
                                          sig[:, pair_of(n)], ALU.mult).then_inc(product_ready, 1)
                    step.restart()


def network(nc, x, c_t, wmod0, wmod1, ga_hidden, ga_qk, ga_out, ga_ln_cols, ga_v_bias, ga_gate_bias, ga_b_out,
            ga_qk_cols, moe_w1, moe_sw1, moe_w2, moe_sw2, router_w, router_b, moe_b1_cols, moe_sb2_cols, moe_b2,
            WqT, WkT, WvT, WqvT, qk_cols, bqv, bv, Ws, bs, WfT, Wr1T, Wr2T, W_rT, W_kT, W_vT, bf, br2, tail_cols, out):
    def scratch(name, shape, dt=F32):
        return nc.dram_tensor(name + "_dram", shape, dt, kind="Internal").ap()

    mod, mod_cols = scratch("mod", [2, BATCH, MOD]), scratch("mod_cols", [P, 2, MOD // P, BATCH])
    x_ga, x_moe, h = (scratch(n, [TOKENS, DIM]) for n in ("x_ga", "x_moe", "h"))
    parts, values = scratch("parts", [2, BATCH, SPLITS, DIM, SEQ], BF16), scratch("values", [TOKENS, V_WIDTH])
    stage_mod(nc, c_t, [wmod0, wmod1], mod, mod_cols)
    clear_semaphores(nc)
    stage_gated_attention(nc, x, x_ga, mod, dict(
        W_hidden=ga_hidden, W_qk=ga_qk, W_out=ga_out, ln_cols=ga_ln_cols, v_bias=ga_v_bias, gate_bias=ga_gate_bias,
        b_out=ga_b_out, qk_cols=ga_qk_cols))
    clear_semaphores(nc)
    stage_experts(nc, x_ga, x_moe, mod_cols, dict(
        w1=moe_w1, sw1=moe_sw1, w2=moe_w2, sw2=moe_sw2, router_w=router_w, router_b=router_b, b1_cols=moe_b1_cols,
        sb2_cols=moe_sb2_cols, b2=moe_b2))
    clear_semaphores(nc)
    stage_project(nc, x_moe, h, parts, values, mod, dict(
        WqT=WqT, WkT=WkT, WvT=WvT, WqvT=WqvT, cols=qk_cols, bqv=bqv, bv=bv, Ws=Ws, bs=bs))
    clear_semaphores(nc)
    with nc.sbuf_tensor("attended", [P, BATCH * TILES, DIM], F32) as attended:
        stage_attention(nc, parts, values, attended)
        clear_semaphores(nc)
        stage_tail(nc, attended, h, x_moe, out, mod, mod_cols, dict(
            WfT=WfT, Wr1T=Wr1T, Wr2T=Wr2T, W_rT=W_rT, W_kT=W_kT, W_vT=W_vT, bf=bf, br2=br2, cols=tail_cols))


def kernel(**inputs):
    import concourse.bacc as _bacc
    from concourse.bass_utils import run_bass_kernel_spmd as _run

    def col(a):
        return a.reshape(-1, P).T

    a = {name: np.asarray(value) for name, value in inputs.items()}
    ga = {name[8:]: a[name] for name in a if name.startswith("L0_attn_")}
    moe = {name[7:]: a[name] for name in a if name.startswith("L0_ffn_")}
    at1 = {name[8:]: a[name] for name in a if name.startswith("L1_attn_")}
    mix = {name[7:]: a[name] for name in a if name.startswith("L1_ffn_")}
    hid = ga["W_out"].shape[0]
    experts = moe["w1"].shape[0]
    arrays = {
        "x": ga["x"].reshape(TOKENS, DIM),
        "c_t": np.concatenate([a["L0_c"], a["L1_c"]], 0).T,
        "wmod0": a["L0_wmod"], "wmod1": a["L1_wmod"],
        "ga_hidden": ga["W_hidden"], "ga_qk": ga["W_qk"], "ga_out": ga["W_out"],
        "ga_ln_cols": np.stack([col(ga["ln_scale"]), col(ga["ln_bias"])], 1),
        "ga_v_bias": ga["b_hidden"][:hid], "ga_gate_bias": col(ga["b_hidden"][hid:]), "ga_b_out": ga["b_out"],
        "ga_qk_cols": np.concatenate([ga["b_qk"][None], ga["os_weight"], ga["os_bias"]], 0).T,
        "moe_w1": moe["w1"].transpose(1, 0, 2).reshape(DIM, -1),
        "moe_sw1": moe["sw1"].transpose(1, 0, 2).reshape(DIM, -1),
        "moe_w2": moe["w2"].reshape(-1, DIM), "moe_sw2": moe["sw2"].reshape(-1, DIM),
        "router_w": moe["router_w"], "router_b": moe["router_b"],
        "moe_b1_cols": np.concatenate([moe["b1"].reshape(-1, P), moe["sb1"].reshape(-1, P)]).T,
        "moe_sb2_cols": np.stack([col(row) for row in moe["sb2"]], 1),
        "moe_b2": moe["b2"].reshape(experts, DIM),
        "WqT": at1["Wq"].T, "WkT": at1["Wk"].T, "WvT": at1["Wv"].T, "WqvT": at1["Wqv"].T,
        "qk_cols": np.stack([col(at1[name]) for name in ("g1", "b1", "bq", "bk")], 1),
        "bqv": at1["bqv"], "bv": at1["bv"], "Ws": at1["Ws"], "bs": at1["bs"],
        "WfT": at1["Wf"].T, "Wr1T": at1["Wr1"].T, "Wr2T": at1["Wr2"].T,
        "W_rT": mix["W_r"].T, "W_kT": mix["W_k"].T, "W_vT": mix["W_v"].T,
        "bf": at1["bf"], "br2": at1["br2"],
        "tail_cols": np.concatenate([col(at1["g2"]), col(at1["b2"]), col(at1["br1"]), col(mix["mu_r"]),
                                     col(mix["mu_k"])], 1),
    }
    nc = _bacc.Bacc("TRN2", target_bir_lowering=False, num_devices=1)
    arrays = {f"in_{name}_dram": np.ascontiguousarray(value) for name, value in arrays.items()}
    args = [nc.dram_tensor(name, value.shape, mybir.dt.from_np(value.dtype), kind="ExternalInput").ap()
            for name, value in arrays.items()]
    out = nc.dram_tensor("out_0_dram", [TOKENS, DIM], F32, kind="ExternalOutput").ap()
    network(nc, *args, out)
    r = _run(nc, [arrays], core_ids=[0])
    return r.results[0]["out_0_dram"].reshape(BATCH, SEQ, DIM)
```

```python
from contextlib import ExitStack

import numpy as np
import concourse.bass as bass
from concourse import mybir

F32 = mybir.dt.float32
F32R = mybir.dt.float32r
BF16 = mybir.dt.bfloat16
ACT = mybir.ActivationFunctionType
ALU = mybir.AluOpType
X_AXIS = mybir.AxisListType.X

P = 128
DIM = 256
KT = DIM // P
BATCH, SEQ = 4, 1024
TILES = SEQ // P
CHUNK = 512
CT = CHUNK // P
CHUNKS = SEQ // CHUNK
TOKENS = BATCH * SEQ
EPS = 1e-5
SHIFT_A, SCALE_A, GATE_A, SHIFT_B, SCALE_B, GATE_B = range(6)
MOD = 6 * DIM
START = 1


def at(trip, per_trip, step):
    return START + trip * per_trip + step


class Steps:

    def __init__(self, engine, semaphore):
        self.engine, self.semaphore, self.n = engine, semaphore, 0

    def one(self):
        self.n += 1
        return 1

    def wait(self, back=0):
        self.engine.wait_ge(self.semaphore, self.n - back)

    def restart(self):
        self.wait()
        self.engine.sem_clear(self.semaphore)
        self.n = 0


class Room:
    raised = []

    def __init__(self, nc, ctx, name):
        self.nc, self.ctx, self.name, self.counters = nc, ctx, name, []

    def sb(self, name, shape, dt=F32):
        return self.ctx.enter_context(self.nc.sbuf_tensor(f"{self.name}_{name}", list(shape), dt))

    def ps(self, name, shape, dt=F32):
        return self.ctx.enter_context(self.nc.psum_tensor(f"{self.name}_{name}", list(shape), dt))

    def sem(self, name):
        semaphore = self.ctx.enter_context(self.nc.semaphore(f"{self.name}_{name}"))
        Room.raised.append(semaphore)
        return semaphore

    def counter(self, name):
        self.counters.append(self.sem(name))
        return self.counters[-1]

    def pair(self, name, shape):
        return self.sb(name + "_hi", shape, F32R), self.sb(name + "_lo", shape, F32R)


def start_counters(nc, room):
    with nc.Block() as block:
        @block.gpsimd
        def _(pool):
            for counter in room.counters:
                pool.sem_inc(counter, START)


def clear_semaphores(nc):
    numbers = sorted({semaphore.num for semaphore in Room.raised})
    Room.raised.clear()
    with nc.Block() as block:
        @block.gpsimd
        def _(pool):
            start = 0
            for n in range(1, len(numbers) + 1):
                if n == len(numbers) or numbers[n] != numbers[n - 1] + 1:
                    pool.sem_clear(range(numbers[start], numbers[n - 1] + 1))
                    start = n


def product3(pe, out, weights, moving, first, last):
    (w_hi, w_lo), (m_hi, m_lo) = weights, moving
    pe.matmul(out, w_hi, m_hi, start=first, stop=False)
    pe.matmul(out, w_hi, m_lo, start=False, stop=False)
    return pe.matmul(out, w_lo, m_hi, start=False, stop=last)


def cut(pair, *index):
    return tuple(half[index] for half in pair)


def column(bc, rows, n):
    return bc.unsqueeze(2).to_broadcast([bc.shape[0], rows, n])


class Loading:

    def __init__(self, room, name, loads, weights, staging, identity=None):
        self.loads, self.weights, self.slots, self.identity = loads, weights, staging, identity
        self.loaded, self.hi_done, self.lo_done = (
            room.sem(name + "_loaded"), room.sem(name + "_hi_done"), room.sem(name + "_lo_done"))
        self.landed = [room.sem(f"{name}_landed{n}") for n in range(len(staging))]
        self.zeroed, self.identity_done = room.sem(name + "_zeroed"), room.sem(name + "_identity_done")

    def slot(self, n):
        shape = self.weights[n][0][0].shape
        flat = self.slots[n % len(self.slots)][:, 0:self.weights[n][0][0].free_size()]
        if len(shape) == 3:
            return flat.rearrange("p (a b) -> p a b", b=shape[2])
        return flat

    def sync(self, sp):
        for n, (_, source) in enumerate(self.weights):
            if n >= len(self.slots):
                sp.wait_ge(self.lo_done, n - len(self.slots) + 1)
            sp.dma_start(self.slot(n), source).then_inc(self.landed[n % len(self.slots)], 16)

    def small(self, engine):
        for destination, source in self.loads:
            engine.dma_start(destination, source).then_inc(self.loaded, 16)

    def scalar(self, act, start=0, end=None):
        for n in range(start, end or len(self.weights)):
            hi = self.weights[n][0][0]
            act.wait_ge(self.landed[n % len(self.slots)], 16 * (n // len(self.slots) + 1))
            act.activation(hi, self.slot(n), ACT.Copy).then_inc(self.hi_done, 1)

    def vector(self, vec, start=0, end=None):
        for n in range(start, end or len(self.weights)):
            hi, lo = self.weights[n][0]
            vec.wait_ge(self.hi_done, n + 1)
            vec.tensor_tensor(lo, self.slot(n), hi.bitcast(F32), ALU.subtract).then_inc(self.lo_done, 1)

    def gpsimd(self, pool):
        pool.memset(self.identity, 0.0).then_inc(self.zeroed, 1)
        pool.wait_ge(self.zeroed, 1)
        pool.affine_select(out=self.identity, in_=self.identity, compare_op=ALU.not_equal, fill=1.0,
                           base=0, pattern=[[-1, P]], channel_multiplier=1).then_inc(self.identity_done, 1)

    def wait_small(self, engine):
        engine.wait_ge(self.loaded, 16 * len(self.loads))

    def wait_weights(self, engine, count=None):
        engine.wait_ge(self.lo_done, count or len(self.weights))

    def wait_identity(self, engine):
        engine.wait_ge(self.identity_done, 1)


def newton_rsqrt(vec, step, y, v, scratch):
    vec.tensor_tensor(scratch, y, y, ALU.mult).then_inc(step.semaphore, step.one())
    step.wait()
    vec.tensor_tensor(scratch, scratch, v, ALU.mult).then_inc(step.semaphore, step.one())
    step.wait()
    vec.tensor_scalar(scratch, scratch, -0.5, 1.5, ALU.mult, ALU.add).then_inc(step.semaphore, step.one())
    step.wait()
    vec.tensor_tensor(y, y, scratch, ALU.mult).then_inc(step.semaphore, step.one())


def stage_mod(nc, c_t, wmods, mod_d, mod_cols_d, beside=None):
    LAYERS = 2
    with ExitStack() as ctx:
        room = Room(nc, ctx, "mod")
        c_raw, c_act = room.sb("c_raw", [P, KT, LAYERS * BATCH]), room.sb("c_act", [P, KT, LAYERS * BATCH])
        w = room.sb("w", [P, LAYERS, KT, MOD])
        mod = room.sb("mod", [BATCH, LAYERS, MOD])
        sign = room.sb("sign", [BATCH, 4, DIM])
        out_ps = [room.ps(f"out{n}", [P, 512]) for n in range(MOD // 512 * LAYERS)]
        c_in, silu_done, mod_step, mod_out = (room.sem(n) for n in ("c_in", "silu_done", "mod_step", "mod_out"))
        w_in = [room.sem(f"w_in{layer}") for layer in range(LAYERS)]
        product_done, mod_ready = room.sem("product_done"), room.sem("mod_ready")
        ident = room.sb("ident", [BATCH, BATCH])
        cols = room.sb("cols", [P, LAYERS, MOD // P, BATCH])
        cols_ps = room.ps("cols_ps", [P, LAYERS, MOD // P, BATCH])
        ident_ready, cols_full, cols_ready = room.sem("ident_ready"), room.sem("cols_full"), room.sem("cols_ready")
        PARTS = MOD // 512
        with nc.Block() as block:
            @block.sync
            def _(sp):
                sp.dma_start(c_raw[:], c_t.rearrange("(k p) n -> p k n", p=P)).then_inc(c_in, 16)
                for layer in range(LAYERS):
                    sp.dma_start(w[:, layer], wmods[layer].rearrange("(k p) n -> p k n", p=P)).then_inc(w_in[layer], 16)
                if beside:
                    beside.sync(sp)
                sp.wait_ge(mod_ready, 1)
                sp.dma_start(mod_d.rearrange("l b n -> b l n"), mod[:]).then_inc(mod_out, 16)
                sp.wait_ge(cols_ready, 1)
                sp.dma_start(mod_cols_d, cols[:]).then_inc(mod_out, 16)
                sp.wait_ge(mod_out, 32)

            @block.gpsimd
            def _(pool):
                if beside:
                    beside.gpsimd(pool)
                pool.memset(ident[:], 0.0).then_inc(ident_ready, 1)
                pool.wait_ge(ident_ready, 1)
                pool.affine_select(out=ident[:], in_=ident[:], compare_op=ALU.not_equal, fill=1.0, base=0,
                                   pattern=[[-1, BATCH]], channel_multiplier=1).then_inc(ident_ready, 1)

            @block.scalar
            def _(act):
                act.wait_ge(c_in, 16)
                act.activation(c_act[:], c_raw[:], ACT.Silu).then_inc(silu_done, 1)
                if beside:
                    beside.small(act)
                    beside.scalar(act)
                    beside.wait_small(act)

            @block.tensor
            def _(pe):
                pe.wait_ge(silu_done, 1)
                for layer in range(LAYERS):
                    pe.wait_ge(w_in[layer], 16)
                    for n in range(PARTS):
                        for k in range(KT):
                            mm = pe.matmul(out_ps[layer * PARTS + n][0:BATCH, :],
                                           c_act[:, k, layer * BATCH:(layer + 1) * BATCH],
                                           w[:, layer, k, n * 512:(n + 1) * 512], start=(k == 0), stop=(k == KT - 1))
                        mm.then_inc(product_done, 1)
                pe.wait_ge(ident_ready, 2)
                pe.wait_ge(mod_ready, 1)
                for layer in range(LAYERS):
                    for n in range(MOD // P):
                        mm = pe.transpose(cols_ps[:, layer, n], mod[:, layer, n * P:(n + 1) * P], ident[:])
                mm.then_inc(cols_full, 1)

            @block.vector
            def _(vec):
                step = Steps(vec, mod_step)
                if beside:
                    beside.vector(vec)
                for n in range(LAYERS * PARTS):
                    vec.wait_ge(product_done, n + 1)
                    vec.tensor_copy(mod[:, n // PARTS, (n % PARTS) * 512:(n % PARTS + 1) * 512],
                                    out_ps[n][0:BATCH, :]).then_inc(mod_step, step.one())
                step.wait()
                for layer in range(LAYERS):
                    for which in (SCALE_A, SCALE_B):
                        part = mod[:, layer, which * DIM:(which + 1) * DIM]
                        vec.tensor_scalar(part, part, 1.0, None, ALU.add).then_inc(mod_step, step.one())
                    for n, which in enumerate((GATE_A, GATE_B)):
                        part = mod[:, layer, which * DIM:(which + 1) * DIM]
                        s = sign[:, 2 * layer + n]
                        vec.tensor_scalar(s, part, 0.0, 2.0, ALU.is_ge, ALU.mult).then_inc(mod_step, step.one())
                        step.wait()
                        vec.scalar_tensor_tensor(part, part, -1.0, part, ALU.mult, ALU.max).then_inc(mod_step, step.one())
                        step.wait()
                        vec.tensor_scalar(part, part, 0.25, None, ALU.max).then_inc(mod_step, step.one())
                        step.wait()
                        vec.scalar_tensor_tensor(part, s, -1.0, part, ALU.add, ALU.mult).then_inc(mod_step, step.one())
                step.wait()
                vec.tensor_copy(sign[:, 0, 0:1], sign[:, 0, 0:1]).then_inc(mod_ready, 1)
                vec.wait_ge(cols_full, 1)
                vec.tensor_copy(cols[:], cols_ps[:]).then_inc(cols_ready, 1)


class GatedAttentionWeights:

    def __init__(self, nc, ctx, w):
        self.nc, self.room = nc, Room(nc, ctx, "gw")
        sb = self.room.sb
        self.ident = sb("ident", [P, P])
        self.hidden = self.room.pair("hidden", [P, KT, w["W_hidden"].shape[1]])
        self.qk = self.room.pair("qk", [P, KT, P])
        self.out = self.room.pair("out", [P, w["W_out"].shape[0] // P, DIM])
        self.ln_col = sb("ln_col", [P, 2, KT])
        self.gate_bias = sb("gate_bias", list(w["gate_bias"].shape))
        self.qk_cols = sb("qk_cols", [P, 5])
        self.v_bias = sb("v_bias", [P, w["v_bias"].shape[0]])
        self.out_bias = sb("out_bias", [P, DIM])
        self.loads = [(self.ln_col[:], w["ln_cols"]),
                      (self.gate_bias[:], w["gate_bias"]),
                      (self.qk_cols[:], w["qk_cols"]),
                      (self.v_bias[:], w["v_bias"].partition_broadcast(P)),
                      (self.out_bias[:], w["b_out"].partition_broadcast(P))]
        self.weights = [(cut(self.hidden, slice(None), k), w["W_hidden"][k * P:(k + 1) * P]) for k in range(KT)] + [
            (cut(self.qk, slice(None)), w["W_qk"].rearrange("(k p) n -> p k n", p=P)),
            (cut(self.out, slice(None)), w["W_out"].rearrange("(m p) n -> p m n", p=P))]

    def loading(self, ctx):
        staging = Room(self.nc, ctx, "gw_load").sb("staging", [P, len(self.weights), 1024])
        return Loading(self.room, "load", self.loads, self.weights, [staging[:, n] for n in range(len(self.weights))],
                       self.ident[:])


def stage_gated_attention(nc, x_in, x_out, mod_d, w):
    HID, QK = 512, P
    HT = HID // P
    STEPS = CHUNKS * TILES
    RING = 3
    T0, QK0, G0, V0, Y0 = 0, CHUNKS * KT, CHUNKS * KT + CHUNKS, CHUNKS * KT + CHUNKS + CHUNKS * HT, \
        CHUNKS * KT + CHUNKS + CHUNKS * HT + TILES
    USES = Y0 + CT
    assert USES % 2 == 0 and CT % 2 == 0 and QK0 % 2 == 0 and CHUNKS == 2
    with ExitStack() as ctx:
        room = Room(nc, ctx, "ga")
        sb, sem = room.sb, room.counter
        ident, ln_col, gate_bias, qk_cols, v_bias, out_bias = (
            w.ident, w.ln_col, w.gate_bias, w.qk_cols, w.v_bias, w.out_bias)
        w_hidden, w_qk, w_out = w.hidden, w.qk, w.out
        mod = sb("mod", [P, BATCH, 3, DIM])
        mod_in = room.sem("mod_in")
        x_ln = sb("x_ln", [P, TILES, DIM])
        rows = sb("rows", [P, TILES, DIM])
        x_res = sb("x_res", [P, CHUNKS, CT, DIM])
        stats, moments = sb("stats", [P, TILES, 6]), sb("moments", [P, TILES, 2])
        var, rstd, scratch = sb("var", [P, TILES]), sb("rstd", [P, TILES]), sb("scratch", [P, TILES])
        gate_now, mark = sb("gate_now", [P, DIM]), sb("mark", [P, 1])
        power = sb("power", [P, TILES])
        xt = sb("xt", [P, 2, CHUNK])
        x_t = room.pair("x_t", [P, KT, SEQ])
        qk_act = sb("qk_act", [P, CHUNKS, CHUNK])
        q_tmp, k_tmp = sb("q_tmp", [P, CHUNK]), sb("k_tmp", [P, CHUNK])
        q_t, k_t = room.pair("q_t", [P, SEQ]), room.pair("k_t", [P, SEQ])
        v_tmp = sb("v_tmp", [P, 2, HID])
        v = room.pair("v", [P, TILES, HID])
        gate_t = sb("gate_t", [P, HT, SEQ])
        relu = sb("relu", [P, RING, CHUNK])
        square = sb("square", [P, CHUNK])
        attn = room.pair("attn", [P, RING, CHUNK])
        og_tmp = sb("og_tmp", [P, 2, CHUNK])
        og = room.pair("og", [P, HT, CHUNK])
        y_tmp = sb("y_tmp", [P, 2, DIM])
        shared_ps = [room.ps(f"shared{n}", [P, 512]) for n in range(2)]
        score_ps = [room.ps(f"score{n}", [P, CHUNK]) for n in range(2)]
        o_ps = [room.ps(f"o{n}", [P, CHUNK]) for n in range(HT)]

        x_ln_in, x_ln_used, x_res_in, x_stored = sem("x_ln_in"), sem("x_ln_used"), sem("x_res_in"), sem("x_stored")
        var_ready, rstd_ready, rows_ready = sem("var_ready"), sem("rstd_ready"), sem("rows_ready")
        constants, gate_copied, marked = room.sem("constants"), sem("gate_copied"), sem("marked")
        shared_full = sem("shared_full")
        xt_ready, x_t_ready = sem("xt_ready"), sem("x_t_ready")
        qk_ready, qk_split = sem("qk_ready"), sem("qk_split")
        gate_ready = sem("gate_ready")
        v_biased, v_hi_ready, v_ready = sem("v_biased"), sem("v_hi_ready"), sem("v_ready")
        score_full, relu_ready, attn_hi_ready, attn_ready = (
            sem("score_full"), sem("relu_ready"), sem("attn_hi_ready"), sem("attn_ready"))
        o_step = sem("o_step")
        og_scaled, og_hi_ready, og_ready = sem("og_scaled"), sem("og_hi_ready"), sem("og_ready")
        y_full1 = sem("y_full1")
        y_biased, y_gated, x_ready = [sem("y_biased0"), sem("y_biased1")], sem("y_gated"), sem("x_ready")
        vec_step = room.sem("vec_step")

        src_x = x_in.rearrange("(b t p) n -> b p t n", b=BATCH, p=P)
        src_res = x_in.rearrange("(b c t p) n -> b p c t n", b=BATCH, c=CHUNKS, p=P)
        dst_x = x_out.rearrange("(b c t p) n -> b p c t n", b=BATCH, c=CHUNKS, p=P)

        def trips(engine, body):
            body(0, True, False)
            with engine.Fori(0, BATCH - 2) as trip:
                body(trip + 1, False, False)
            body(BATCH - 1, False, True)

        def shared_free(pe, trip, use):
            u = use - 2
            if u < 0:
                pe.wait_ge(y_biased[0], at(trip, CT, 0))
            elif u < QK0:
                pe.wait_ge(xt_ready, at(trip, CHUNKS * KT, u - T0 + 1))
                if use >= QK0:
                    pe.wait_ge(y_biased[1], at(trip, CT, 0))
            elif u < G0:
                pe.wait_ge(qk_ready, at(trip, CHUNKS, u - QK0 + 1))
            elif u < V0:
                pe.wait_ge(gate_ready, at(trip, CHUNKS * HT, u - G0 + 1))
            elif u < Y0:
                pe.wait_ge(v_biased, at(trip, TILES, u - V0 + 1))
            else:
                pe.wait_ge(y_biased[0], at(trip, CT, u - Y0 + 1))

        start_counters(nc, room)
        with nc.Block() as block:
            @block.sync
            def _(sp):
                sp.dma_start(x_ln[:], src_x[0]).then_inc(x_ln_in, 16)
                sp.dma_start(mod[:], mod_d[0, :, 0:3 * DIM].rearrange("b (w n) -> b w n", n=DIM)
                             .partition_broadcast(P)).then_inc(mod_in, 16)

                def store(batch, c):
                    sp.wait_ge(x_ready, at(batch, TILES, CT * (c + 1)))
                    sp.dma_start(dst_x[batch, :, c], x_res[:, c]).then_inc(x_stored, 16)

                def trip_of(trip, first, last):
                    if not last:
                        sp.wait_ge(x_ln_used, at(trip, 1, 1))
                        sp.dma_start(x_ln[:], src_x[trip + 1]).then_inc(x_ln_in, 16)
                    if not first:
                        store(trip - 1, 1)
                    sp.wait_ge(x_stored, at(trip, 16 * CHUNKS, 0))
                    sp.dma_start(x_res[:], src_res[trip]).then_inc(x_res_in, 16)
                    store(trip, 0)
                trips(sp, trip_of)
                store(BATCH - 1, 1)
                sp.wait_ge(x_stored, at(BATCH, 16 * CHUNKS, 0))

            @block.gpsimd
            def _(pool):
                pool.memset(power[:], -0.5).then_inc(constants, 1)
                pool.wait_ge(constants, 1)

                def rsqrt(index, n):
                    pool.wait_ge(var_ready, at(index, 2, n))
                    pool.tensor_tensor(rstd[:], var[:], power[:], ALU.pow).then_inc(rstd_ready, 1)

                rsqrt(0, 1)
                rsqrt(0, 2)
                pool.wait_ge(mod_in, 16)

                def gate_and_add(batch, c):
                    for t in range(CT):
                        n = c * CT + t
                        pool.wait_ge(y_biased[c], at(batch, CT, t + 1))
                        pool.tensor_tensor(y_tmp[:, n % 2], y_tmp[:, n % 2], gate_now[:],
                                           ALU.mult).then_inc(y_gated, 1)
                        pool.wait_ge(y_gated, at(batch, TILES, n + 1))
                        pool.tensor_tensor(x_res[:, c, t], x_res[:, c, t], y_tmp[:, n % 2],
                                           ALU.add).then_inc(x_ready, 1)

                def trip_of(trip, first, last):
                    if not first:
                        gate_and_add(trip - 1, 1)
                    pool.wait_ge(x_ready, at(trip, TILES, 0))
                    pool.tensor_tensor(mark[:], power[:, 0:1], power[:, 0:1], ALU.mult).then_inc(marked, 1)
                    pool.tensor_copy(gate_now[:], mod[:, trip, GATE_A]).then_inc(gate_copied, 1)
                    pool.wait_ge(gate_copied, at(trip, 1, 1))
                    pool.wait_ge(marked, at(trip, 1, 1))
                    if not last:
                        rsqrt(trip + 1, 1)
                    pool.wait_ge(x_res_in, at(trip, 16, 16))
                    gate_and_add(trip, 0)
                    if not last:
                        rsqrt(trip + 1, 2)
                trips(pool, trip_of)
                gate_and_add(BATCH - 1, 1)

            @block.tensor
            def _(pe):
                def project(batch, c, trip):
                    pe.wait_ge(og_ready, at(batch, CHUNKS * HT, HT * (c + 1)))
                    for t in range(CT):
                        if c == 0:
                            shared_free(pe, trip, Y0 + t)
                        elif t >= 2:
                            pe.wait_ge(y_biased[1], at(batch, CT, t - 1))
                        elif trip is None:
                            pe.wait_ge(y_biased[0], at(batch, CT, CT))
                        else:
                            pe.wait_ge(xt_ready, at(trip, CHUNKS * KT, CHUNKS * KT + t - 1))
                        for m in range(HT):
                            mm = product3(pe, shared_ps[t % 2][:, 0:DIM],
                                          cut(og, slice(None), m, slice(t * P, (t + 1) * P)),
                                          cut(w_out, slice(None), m), m == 0, m == HT - 1)
                        mm.then_inc(y_full1 if c else shared_full, 1)

                def trip_of(trip, first, last):
                    pe.wait_ge(rows_ready, at(trip, 1, 1))
                    for c in range(CHUNKS):
                        for k in range(KT):
                            use = T0 + c * KT + k
                            shared_free(pe, trip, use)
                            for t in range(CT):
                                mm = pe.transpose(shared_ps[use % 2][:, t * P:(t + 1) * P],
                                                  rows[:, c * CT + t, k * P:(k + 1) * P], ident[:])
                            mm.then_inc(shared_full, 1)
                    if not first:
                        project(trip - 1, 1, trip)
                    for c in range(CHUNKS):
                        use = QK0 + c
                        shared_free(pe, trip, use)
                        pe.wait_ge(x_t_ready, at(trip, CHUNKS * KT, KT * (c + 1)))
                        for k in range(KT):
                            mm = product3(pe, shared_ps[use % 2][:], cut(w_qk, slice(None), k),
                                          cut(x_t, slice(None), k, slice(c * CHUNK, (c + 1) * CHUNK)),
                                          k == 0, k == KT - 1)
                        mm.then_inc(shared_full, 1)
                    for m in range(HT):
                        for c in range(CHUNKS):
                            use = G0 + m * CHUNKS + c
                            shared_free(pe, trip, use)
                            for k in range(KT):
                                mm = product3(pe, shared_ps[use % 2][:],
                                              cut(w_hidden, slice(None), k, slice(HID + m * P, HID + (m + 1) * P)),
                                              cut(x_t, slice(None), k, slice(c * CHUNK, (c + 1) * CHUNK)),
                                              k == 0, k == KT - 1)
                            mm.then_inc(shared_full, 1)

                    def scores(s):
                        c, j = divmod(s, TILES)
                        pe.wait_ge(qk_split, at(trip, CHUNKS, max(c, j // CT) + 1))
                        pe.wait_ge(relu_ready, at(trip, STEPS, max(0, s - 1)))
                        product3(pe, score_ps[s % 2][:], cut(k_t, slice(None), slice(j * P, (j + 1) * P)),
                                 cut(q_t, slice(None), slice(c * CHUNK, (c + 1) * CHUNK)),
                                 True, True).then_inc(score_full, 1)

                    scores(0)
                    scores(1)
                    for t in range(TILES):
                        use = V0 + t
                        shared_free(pe, trip, use)
                        for k in range(KT):
                            mm = product3(pe, shared_ps[use % 2][:], cut(x_t, slice(None), k, slice(t * P, (t + 1) * P)),
                                          cut(w_hidden, slice(None), k, slice(0, HID)), k == 0, k == KT - 1)
                        mm.then_inc(shared_full, 1)

                    for s in range(STEPS):
                        c, j = divmod(s, TILES)
                        if s + 2 < STEPS:
                            scores(s + 2)
                        pe.wait_ge(attn_ready, at(trip, STEPS, s + 1))
                        pe.wait_ge(v_ready, at(trip, TILES, j + 1))
                        for m in range(HT):
                            if j == 0 and c > 0:
                                pe.wait_ge(og_scaled, at(trip, CHUNKS * HT, HT * (c - 1) + m + 1))
                            mm = product3(pe, o_ps[m][:], cut(v, slice(None), j, slice(m * P, (m + 1) * P)),
                                          cut(attn, slice(None), s % RING), j == 0, j == TILES - 1)
                        mm.then_inc(o_step, 1)
                        if s == TILES + 1:
                            project(trip, 0, trip)
                trips(pe, trip_of)
                project(BATCH - 1, 1, None)

            @block.scalar
            def _(act):
                def trip_of(trip, first, last):
                    for u in range(CHUNKS * KT):
                        c, k = divmod(u, KT)
                        act.wait_ge(shared_full, at(trip, USES, T0 + u + 1))
                        act.wait_ge(x_t_ready, at(trip, CHUNKS * KT, max(0, u - 1)))
                        for out in (xt[:, u % 2], x_t[0][:, k, c * CHUNK:(c + 1) * CHUNK]):
                            ins = act.activation(out, shared_ps[(T0 + u) % 2][:], ACT.Identity,
                                                 bias=ln_col[:, 1, k:k + 1], scale=ln_col[:, 0, k:k + 1])
                        ins.then_inc(xt_ready, 1)
                    for c in range(CHUNKS):
                        act.wait_ge(shared_full, at(trip, USES, QK0 + c + 1))
                        act.activation(qk_act[:, c], shared_ps[(QK0 + c) % 2][:], ACT.Silu,
                                       bias=qk_cols[:, 0:1]).then_inc(qk_ready, 1)
                    for m in range(HT):
                        for c in range(CHUNKS):
                            use = G0 + m * CHUNKS + c
                            act.wait_ge(shared_full, at(trip, USES, use + 1))
                            act.activation(gate_t[:, m, c * CHUNK:(c + 1) * CHUNK], shared_ps[use % 2][:], ACT.Silu,
                                           bias=gate_bias[:, m:m + 1]).then_inc(gate_ready, 1)

                    def squares(s):
                        act.wait_ge(score_full, at(trip, STEPS, s + 1))
                        act.wait_ge(attn_ready, at(trip, STEPS, max(0, s - RING + 1)))
                        act.activation(relu[:, s % RING], score_ps[s % 2][:], ACT.Relu,
                                       scale=1.0 / SEQ).then_inc(relu_ready, 1)
                        act.wait_ge(relu_ready, at(trip, STEPS, s + 1))
                        act.wait_ge(o_step, at(trip, STEPS, max(0, s - RING + 1)))
                        act.activation(attn[0][:, s % RING], relu[:, s % RING], ACT.Square).then_inc(attn_hi_ready, 1)

                    squares(0)
                    squares(1)
                    for t in range(TILES):
                        act.wait_ge(v_biased, at(trip, TILES, t + 1))
                        for out in (v[0][:, t], v_tmp[:, t % 2]):
                            ins = act.activation(out, v_tmp[:, t % 2], ACT.Silu)
                        ins.then_inc(v_hi_ready, 1)

                    def round_og(c):
                        for m in range(HT):
                            n = c * HT + m
                            act.wait_ge(og_scaled, at(trip, CHUNKS * HT, n + 1))
                            act.activation(og[0][:, m], og_tmp[:, n % 2], ACT.Copy).then_inc(og_hi_ready, 1)

                    for s in range(2, STEPS):
                        squares(s)
                        if s == TILES + 1:
                            round_og(0)
                    round_og(1)
                trips(act, trip_of)

            @block.vector
            def _(vec):
                step = Steps(vec, vec_step)

                def normalise(index):
                    def statistics():
                        vec.wait_ge(x_ln_in, at(index, 16, 16))
                        for t in range(TILES):
                            vec.bn_stats(stats[:, t], x_ln[:, t]).then_inc(vec_step, step.one())

                    def variance():
                        step.wait()
                        for t in range(TILES):
                            vec.bn_aggr(moments[:, t], stats[:, t]).then_inc(vec_step, step.one())
                        step.wait()
                        vec.tensor_scalar(var[:], moments[:, :, 1], EPS, None, ALU.add).then_inc(var_ready, 1)

                    def deviation(n):
                        vec.wait_ge(rstd_ready, at(index, 2, n))
                        newton_rsqrt(vec, step, rstd[:], var[:], scratch[:])

                    def modulate(t):
                        step.wait()
                        ins = vec.tensor_scalar(rows[:, t], x_ln[:, t], moments[:, t, 0:1], rstd[:, t:t + 1],
                                                ALU.subtract, ALU.mult)
                        if t == TILES - 1:
                            ins.then_inc(x_ln_used, 1)
                            vec.wait_ge(x_ln_used, at(index, 1, 1))
                        else:
                            ins.then_inc(vec_step, step.one())
                            step.wait()
                        vec.tensor_tensor(rows[:, t], rows[:, t], mod[:, index, SCALE_A],
                                          ALU.mult).then_inc(vec_step, step.one())
                        step.wait()
                        vec.tensor_tensor(rows[:, t], rows[:, t], mod[:, index, SHIFT_A],
                                          ALU.add).then_inc(vec_step, step.one())
                        step.wait()
                        vec.bn_stats(stats[:, t], rows[:, t]).then_inc(vec_step, step.one())

                    def again():
                        step.wait()
                        for t in range(TILES):
                            ins = vec.tensor_scalar(rows[:, t], rows[:, t], moments[:, t, 0:1], rstd[:, t:t + 1],
                                                    ALU.subtract, ALU.mult)
                        ins.then_inc(rows_ready, 1)

                    return ([statistics, variance, lambda: deviation(1)]
                            + [lambda t=t: modulate(t) for t in range(TILES)]
                            + [variance, lambda: deviation(2), again])

                def modulate_all():
                    step.wait()
                    for t in range(TILES):
                        ins = vec.tensor_scalar(rows[:, t], x_ln[:, t], moments[:, t, 0:1], rstd[:, t:t + 1],
                                                ALU.subtract, ALU.mult)
                    ins.then_inc(x_ln_used, 1)
                    vec.wait_ge(x_ln_used, at(0, 1, 1))
                    vec.wait_ge(mod_in, 16)
                    for which, op in ((SCALE_A, ALU.mult), (SHIFT_A, ALU.add)):
                        vec.tensor_tensor(rows[:], rows[:], mod[:, 0, which].unsqueeze(1).to_broadcast([P, TILES, DIM]),
                                          op).then_inc(vec_step, step.one())
                        step.wait()
                    for t in range(TILES):
                        vec.bn_stats(stats[:, t], rows[:, t]).then_inc(vec_step, step.one())

                first_pieces = normalise(0)
                for piece in first_pieces[:3] + [modulate_all] + first_pieces[3 + TILES:]:
                    piece()
                step.restart()

                def bias_y(batch, c):
                    for t in range(CT):
                        n = c * CT + t
                        if c:
                            vec.wait_ge(y_full1, at(batch, CT, t + 1))
                        else:
                            vec.wait_ge(shared_full, at(batch, USES, Y0 + t + 1))
                        vec.wait_ge(x_ready, at(batch, TILES, max(0, n - 1)))
                        vec.tensor_tensor(y_tmp[:, n % 2], shared_ps[t % 2][:, 0:DIM], out_bias[:],
                                          ALU.add).then_inc(y_biased[c], 1)

                def trip_of(trip, first, last):
                    for u in range(CHUNKS * KT):
                        c, k = divmod(u, KT)
                        part = (slice(None), k, slice(c * CHUNK, (c + 1) * CHUNK))
                        vec.wait_ge(xt_ready, at(trip, CHUNKS * KT, u + 1))
                        vec.tensor_tensor(x_t[1][part], xt[:, u % 2], x_t[0][part].bitcast(F32),
                                          ALU.subtract).then_inc(x_t_ready, 1)
                    if not first:
                        bias_y(trip - 1, 1)
                    for c in range(CHUNKS):
                        part = (slice(None), slice(c * CHUNK, (c + 1) * CHUNK))
                        vec.wait_ge(qk_ready, at(trip, CHUNKS, c + 1))
                        vec.wait_ge(qk_split, at(trip, CHUNKS, c))
                        for n, tmp in enumerate((q_tmp, k_tmp)):
                            vec.tensor_scalar(tmp[:], qk_act[:, c], qk_cols[:, 1 + n:2 + n], qk_cols[:, 3 + n:4 + n],
                                              ALU.mult, ALU.add).then_inc(vec_step, step.one())
                        for n, (tmp, pair) in enumerate(((q_tmp, q_t), (k_tmp, k_t))):
                            step.wait(back=1)
                            vec.tensor_copy(pair[0][part], tmp[:]).then_inc(vec_step, step.one())
                        for n, (tmp, pair) in enumerate(((q_tmp, q_t), (k_tmp, k_t))):
                            step.wait(back=1 - n)
                            vec.tensor_tensor(pair[1][part], tmp[:], pair[0][part].bitcast(F32),
                                              ALU.subtract).then_inc(qk_split if n else vec_step, 1 if n else step.one())

                    def squares(s):
                        vec.wait_ge(relu_ready, at(trip, STEPS, s + 1))
                        vec.wait_ge(attn_ready, at(trip, STEPS, s))
                        vec.tensor_tensor(square[:], relu[:, s % RING], relu[:, s % RING],
                                          ALU.mult).then_inc(vec_step, step.one())
                        step.wait()
                        vec.wait_ge(attn_hi_ready, at(trip, STEPS, s + 1))
                        vec.tensor_tensor(attn[1][:, s % RING], square[:], attn[0][:, s % RING].bitcast(F32),
                                          ALU.subtract).then_inc(attn_ready, 1)

                    squares(0)
                    squares(1)

                    def v_low(t):
                        vec.wait_ge(v_hi_ready, at(trip, TILES, t + 1))
                        vec.tensor_tensor(v[1][:, t], v_tmp[:, t % 2], v[0][:, t].bitcast(F32),
                                          ALU.subtract).then_inc(v_ready, 1)

                    for t in range(TILES):
                        vec.wait_ge(shared_full, at(trip, USES, V0 + t + 1))
                        vec.wait_ge(v_ready, at(trip, TILES, max(0, t - 1)))
                        vec.tensor_tensor(v_tmp[:, t % 2], shared_ps[(V0 + t) % 2][:], v_bias[:],
                                          ALU.add).then_inc(v_biased, 1)
                        if t > 0:
                            v_low(t - 1)
                    v_low(TILES - 1)

                    def scale_og(c):
                        def low(m):
                            n = c * HT + m
                            vec.wait_ge(og_hi_ready, at(trip, CHUNKS * HT, n + 1))
                            vec.tensor_tensor(og[1][:, m], og_tmp[:, n % 2], og[0][:, m].bitcast(F32),
                                              ALU.subtract).then_inc(og_ready, 1)
                        vec.wait_ge(o_step, at(trip, STEPS, TILES * (c + 1)))
                        if c:
                            vec.wait_ge(shared_full, at(trip, USES, Y0 + CT))
                        else:
                            vec.wait_ge(y_full1, at(trip, CT, 0))
                        for m in range(HT):
                            n = c * HT + m
                            vec.wait_ge(og_ready, at(trip, CHUNKS * HT, max(0, n - 1)))
                            vec.tensor_tensor(og_tmp[:, n % 2], o_ps[m][:], gate_t[:, m, c * CHUNK:(c + 1) * CHUNK],
                                              ALU.mult).then_inc(og_scaled, 1)
                            vec.wait_ge(og_scaled, at(trip, CHUNKS * HT, n + 1))
                            if m > 0:
                                low(m - 1)
                        low(HT - 1)

                    pieces = [] if last else normalise(trip + 1)
                    for s in range(2, STEPS):
                        squares(s)
                        if s == TILES + 1:
                            scale_og(0)
                        if s == TILES + 3:
                            bias_y(trip, 0)
                        if pieces:
                            pieces.pop(0)()
                    assert not pieces
                    scale_og(1)
                    step.restart()
                trips(vec, trip_of)
                bias_y(BATCH - 1, 1)


def stage_experts(nc, x_in, x_out, mod_cols_d, w):
    EXPERTS, TOP, HID = 64, 8, 64
    PAIRS = EXPERTS * HID // P
    SHARED = 2 * 512 // P
    HIDDEN = PAIRS + SHARED
    GROUP, PARTS = 32, 3
    GROUPS, ROWS = EXPERTS // GROUP, GROUP * PARTS
    NCHUNK = TOKENS // CHUNK
    PER_BATCH = SEQ // CHUNK
    LAG = 2
    with ExitStack() as ctx:
        room = Room(nc, ctx, "moe")
        sb, sem = room.sb, room.counter
        ident, ident_b = sb("ident", [P, P]), sb("ident_b", [P, P], BF16)
        w1 = room.pair("w1", [P, KT, HIDDEN * P])
        w2 = room.pair("w2", [P, HIDDEN, DIM])
        w_r = sb("w_r", [P, KT, EXPERTS])
        b1 = sb("b1", [P, HIDDEN])
        b2 = sb("b2", [ROWS, PARTS, GROUPS, DIM], BF16)
        shared_b2 = sb("shared_b2", [P, 2, KT])
        b2_col = sb("b2_col", [P, KT])
        router_b = sb("router_b", [P, EXPERTS])
        mod = sb("mod", [P, MOD // P, BATCH])
        spread = sb("spread", [ROWS, GROUP, HID], BF16)
        power = sb("power", [P, CT])
        QUARTER, STAGED = 1024, 5
        pieces = []
        for k in range(KT):
            for source, start, width in ((w["w1"], 0, PAIRS * P), (w["sw1"], PAIRS * P, SHARED * P)):
                for n in range(0, width, QUARTER):
                    pieces.append(((w1[0][:, k, start + n:start + n + QUARTER], w1[1][:, k, start + n:start + n + QUARTER]),
                                   source[k * P:(k + 1) * P, n:n + QUARTER]))
        for source, start, count in ((w["w2"], 0, PAIRS), (w["sw2"], PAIRS, SHARED)):
            for n in range(0, count, 4):
                pieces.append(((w2[0][:, start + n:start + n + 4], w2[1][:, start + n:start + n + 4]),
                               source[n * P:(n + 4) * P].rearrange("(m p) n -> p m n", p=P)))
        x = sb("x", [P, CT, DIM])
        rows = x
        logits, marked, weight, rest = (x[:, n].rearrange("p (t e) -> p t e", t=CT) for n in range(4))
        stats, moments = sb("stats", [P, CT, 6]), sb("moments", [P, CT, 2])
        var, rstd, scratch = sb("var", [P, CT]), sb("rstd", [P, CT]), sb("scratch", [P, CT])
        row_max, row_sum, top_sum = sb("row_max", [P, CT]), sb("row_sum", [P, CT]), sb("top_sum", [P, CT])
        top = sb("top", [P, CT, TOP])
        parts = sb("parts", [P, CT, GROUPS, PARTS, GROUP], BF16)
        xt = x[:].rearrange("p (k t) n -> p k (t n)", k=KT)
        x_t = [room.pair("x_t0", [P, KT, CHUNK])]
        weight_t = [sb(f"weight_t{n}", [ROWS, GROUPS, CHUNK], BF16) for n in range(2)]
        y_ps = [room.ps(f"y{n}", [P, CHUNK]) for n in range(KT)]
        hidden_ps = [room.ps(f"hidden{n}", [P, CHUNK]) for n in range(2)]
        spread_ps = [room.ps(f"spread{n}", [P, CHUNK]) for n in range(2)]
        misc_ps = [room.ps(f"misc{n}", [P, 512]) for n in range(2)]
        weight_ps = misc_ps[1][0:ROWS, :].bitcast(BF16).rearrange("p (g n) -> p g n", g=GROUPS)

        staging_ctx = ctx.enter_context(ExitStack())
        staging = Room(nc, staging_ctx, "moe_load").sb("staging", [P, STAGED, QUARTER])
        slots = [staging[:, n] for n in range(STAGED)]
        loading = Loading(room, "load", [(w_r[:], w["router_w"].rearrange("(k p) n -> p k n", p=P)), (b1[:], w["b1_cols"]), (shared_b2[:], w["sb2_cols"]),
                                         (router_b[:], w["router_b"].partition_broadcast(P)), (mod[:], mod_cols_d[:, 0])],
                          pieces, slots, ident[:])
        b2_raw = weight_t[1][:].rearrange("p g n -> p (g n)").bitcast(F32).rearrange("p (g n) -> p g n", g=GROUPS)
        b2_in, b2_step, spread_step, power_ready, small_ready = (
            room.sem("b2_in"), room.sem("b2_step"), room.sem("spread_step"), room.sem("power_ready"), room.sem("small_ready"))

        x_in_sem, res_in, x_stored = sem("x_in"), sem("res_in"), sem("x_stored")
        var_ready, rstd_ready, rows_ready = sem("var_ready"), sem("rstd_ready"), sem("rows_ready")
        turned, xt_ready, x_t_ready = sem("turned"), sem("xt_ready"), sem("x_t_ready")
        router_full, shifted, exp_ready = sem("router_full"), sem("shifted"), sem("exp_ready")
        weight_split, weight_full, weight_t_ready = sem("weight_split"), sem("weight_full"), sem("weight_t_ready")
        hidden_full, hidden_ready, scaled_ready, y_step = (
            sem("hidden_full"), sem("hidden_ready"), sem("scaled_ready"), sem("y_step"))
        y_t_ready, y_back, x_ready = sem("y_t_ready"), sem("y_back"), sem("x_ready")
        vec_step = room.sem("vec_step")

        src = x_in.rearrange("(c t p) n -> c p t n", c=NCHUNK, p=P)
        dst = x_out.rearrange("(c t p) n -> c p t n", c=NCHUNK, p=P)

        def chunks(engine, prepare_first, main, end):
            if first_block:
                prepare_first()
                return
            main(0, 0, False, True)
            with engine.Fori(0, (NCHUNK - 2) // 2) as trip:
                main(trip * 2 + 1, 1, True, True)
                main(trip * 2 + 2, 0, True, True)
            main(NCHUNK - 1, 1, True, False)
            end()

        start_counters(nc, room)
        for first_block in (True, False):
            if not first_block:
                staging_ctx.close()
                x_t.append(room.pair("x_t1", [P, KT, CHUNK]))
                hidden = sb("hidden", [P, 2, CHUNK])
                y_t = hidden
                scaled = room.pair("scaled", [P, LAG, CHUNK])
            with nc.Block() as block:
                @block.sync
                def _(sp):
                    def load_next(c):
                        sp.dma_start(x[:], src[c]).then_inc(x_in_sem, 16)

                    def store(c):
                        sp.wait_ge(x_ready, at(c, KT, KT))
                        sp.dma_start(dst[c], x[:]).then_inc(x_stored, 16)
                        sp.wait_ge(x_stored, at(c, 16, 16))

                    def main(c, slot, back, prepare):
                        if back:
                            store(c - 1)
                        if prepare:
                            load_next(c + 1)
                            sp.wait_ge(weight_split, at(c + 1, 1, 1))
                        sp.dma_start(x[:], src[c]).then_inc(res_in, 16)

                    def first():
                        load_next(0)
                        loading.small(sp)
                        for part in range(PARTS):
                            sp.dma_start(b2_raw[part * GROUP:(part + 1) * GROUP],
                                         w["b2"].rearrange("(g e) n -> e g n", g=GROUPS)).then_inc(b2_in, 16)
                        loading.sync(sp)
                        sp.wait_ge(weight_split, at(0, 1, 1))
                    chunks(sp, first, main, lambda: store(NCHUNK - 1))

                @block.gpsimd
                def _(pool):
                    def rsqrt(c):
                        pool.wait_ge(var_ready, at(c, 1, 1))
                        pool.tensor_tensor(rstd[:], var[:], power[:], ALU.pow).then_inc(rstd_ready, 1)

                    def first():
                        pool.memset(power[:], -0.5).then_inc(power_ready, 1)
                        loading.gpsimd(pool)
                        pool.wait_ge(power_ready, 1)
                        rsqrt(0)
                        step = Steps(pool, spread_step)
                        pool.memset(spread[:], 0.0).then_inc(spread_step, step.one())
                        for part in range(PARTS):
                            step.wait()
                            pool.affine_select(out=spread[:], in_=spread[:], compare_op=ALU.not_equal, fill=1.0,
                                               base=-part * GROUP, pattern=[[-1, GROUP], [0, HID]],
                                               channel_multiplier=1).then_inc(spread_step, step.one())
                    chunks(pool, first, lambda c, slot, back, prepare: rsqrt(c + 1) if prepare else None,
                           lambda: None)

                @block.tensor
                def _(pe):
                    def turn(c, slot):
                        pe.wait_ge(rows_ready, at(c, 1, 1))
                        if not (isinstance(c, int) and c == 0):
                            pe.wait_ge(x_ready, at(c - 1, KT, 0))
                        for k in range(KT):
                            for t in range(CT):
                                mm = pe.transpose(misc_ps[k][:, t * P:(t + 1) * P], rows[:, t, k * P:(k + 1) * P], ident[:])
                            mm.then_inc(turned, 1)

                    def route(c, slot):
                        pe.wait_ge(xt_ready, at(c, KT, KT))
                        for t in range(CT):
                            for k in range(KT):
                                mm = pe.matmul(misc_ps[0][:, t * EXPERTS:(t + 1) * EXPERTS], xt[:, k, t * P:(t + 1) * P],
                                               w_r[:, k], start=(k == 0), stop=(k == KT - 1))
                        mm.then_inc(router_full, 1)

                    def turn_weights(c, slot):
                        pe.wait_ge(weight_split, at(c, 1, 1))
                        for t in range(CT):
                            for g in range(GROUPS):
                                mm = pe.transpose(weight_ps[:, g, t * P:(t + 1) * P],
                                                  parts[:, t, g].rearrange("p a e -> p (a e)"), ident_b[:])
                        mm.then_inc(weight_full, 1)

                    def turn_back(c):
                        pe.wait_ge(y_t_ready, at(c, KT, KT))
                        pe.wait_ge(x_ready, at(c, KT, 0))
                        for t in range(CT):
                            for d in range(KT):
                                mm = pe.transpose(misc_ps[t // 2][:, (t % 2) * DIM + d * P:(t % 2) * DIM + (d + 1) * P],
                                                  y_t[:, d, t * P:(t + 1) * P], ident[:])
                            if t % 2:
                                mm.then_inc(y_back, 1)

                    def main(c, slot, back, prepare):
                        def first_product(q):
                            pe.wait_ge(scaled_ready, at(c, HIDDEN, max(0, q - 1)))
                            if q < PAIRS:
                                g, e = divmod(2 * q, GROUP)
                                pe.matmul(spread_ps[q % 2][:], spread[:, e:e + 2].rearrange("p e h -> p (e h)"), weight_t[slot][:, g],
                                          start=True, stop=True)
                            for k in range(KT):
                                mm = product3(pe, hidden_ps[q % 2][:], cut(w1, slice(None), k, slice(q * P, (q + 1) * P)),
                                              cut(x_t[slot], slice(None), k), k == 0, k == KT - 1)
                            mm.then_inc(hidden_full, 1)

                        def second_product(q):
                            pe.wait_ge(scaled_ready, at(c, HIDDEN, q + 1))
                            for d in range(KT):
                                mm = product3(pe, y_ps[d][:], cut(w2, slice(None), q, slice(d * P, (d + 1) * P)),
                                              cut(scaled, slice(None), q % LAG), False, q == HIDDEN - 1)
                            mm.then_inc(y_step, 1)

                        pe.wait_ge(weight_t_ready, at(c, 1, 1))
                        pe.wait_ge(x_t_ready, at(c, KT, KT))
                        first_product(0)
                        first_product(1)
                        if back:
                            turn_back(c - 1)
                        for d in range(KT):
                            for part in range(PARTS):
                                for g in range(GROUPS):
                                    pe.matmul(y_ps[d][:], b2[:, part, g, d * P:(d + 1) * P], weight_t[slot][:, g],
                                              start=(part == 0 and g == 0), stop=False)
                        for q in range(LAG, HIDDEN):
                            first_product(q)
                            second_product(q - LAG)
                            if prepare:
                                {10: turn, 14: route, 28: turn_weights}.get(q, lambda *_: None)(c + 1, 1 - slot)
                        second_product(HIDDEN - 2)
                        second_product(HIDDEN - 1)

                    def first():
                        loading.wait_identity(pe)
                        turn(0, 0)
                        loading.wait_small(pe)
                        route(0, 0)
                        pe.wait_ge(small_ready, 2)
                        turn_weights(0, 0)
                    chunks(pe, first, main, lambda: turn_back(NCHUNK - 1))

                @block.scalar
                def _(act):
                    def turn(c, slot):
                        b = c // PER_BATCH
                        for k in range(KT):
                            act.wait_ge(turned, at(c, KT, KT))
                            for out in (xt[:, k], x_t[slot][0][:, k]):
                                ins = act.activation(out, misc_ps[k][:], ACT.Identity,
                                                     bias=mod[:, SHIFT_B * KT + k, bass.ds(b, 1)],
                                                     scale=mod[:, SCALE_B * KT + k, bass.ds(b, 1)])
                            ins.then_inc(xt_ready, 1)

                    def exponentials(c):
                        act.wait_ge(shifted, at(c, 1, 1))
                        act.activation(logits, logits, ACT.Exp).then_inc(exp_ready, 1)

                    def turn_weights(c, slot):
                        act.wait_ge(weight_full, at(c, 1, 1))
                        act.activation(weight_t[slot][:], weight_ps, ACT.Copy).then_inc(weight_t_ready, 1)

                    def main(c, slot, back, prepare):
                        act.wait_ge(y_back, at(c, KT, 0))
                        for q in range(HIDDEN):
                            act.wait_ge(hidden_full, at(c, HIDDEN, q + 1))
                            act.wait_ge(scaled_ready, at(c, HIDDEN, max(0, q - 1)))
                            act.activation(hidden[:, q % 2], hidden_ps[q % 2][:], ACT.Silu,
                                           bias=b1[:, q:q + 1]).then_inc(hidden_ready, 1)
                            if prepare and q == 10:
                                turn(c + 1, 1 - slot)
                            if prepare and q == 16:
                                exponentials(c + 1)
                            if prepare and q == 28:
                                turn_weights(c + 1, 1 - slot)

                    def first():
                        loading.wait_small(act)
                        loading.scalar(act, 0, 3)
                        turn(0, 0)
                        loading.scalar(act, 3, 8)
                        exponentials(0)
                        loading.scalar(act, 8, 12)
                        turn_weights(0, 0)
                        loading.scalar(act, 12)
                    chunks(act, first, main, lambda: None)

                @block.vector
                def _(vec):
                    step = Steps(vec, vec_step)

                    def own(ins):
                        return ins.then_inc(vec_step, step.one())

                    def prepare_pieces(c, slot):
                        def statistics():
                            vec.wait_ge(x_in_sem, at(c, 16, 16))
                            for t in range(CT):
                                vec.bn_stats(stats[:, t], x[:, t]).then_inc(vec_step, step.one())
                            step.wait()
                            for t in range(CT):
                                vec.bn_aggr(moments[:, t], stats[:, t]).then_inc(vec_step, step.one())
                            step.wait()
                            vec.tensor_scalar(var[:], moments[:, :, 1], EPS, None, ALU.add).then_inc(var_ready, 1)

                        def normalise():
                            vec.wait_ge(rstd_ready, at(c, 1, 1))
                            newton_rsqrt(vec, step, rstd[:], var[:], scratch[:])
                            step.wait()
                            for t in range(CT):
                                ins = vec.tensor_scalar(rows[:, t], x[:, t], moments[:, t, 0:1], rstd[:, t:t + 1],
                                                        ALU.subtract, ALU.mult)
                            ins.then_inc(rows_ready, 1)

                        def low_halves():
                            for k in range(KT):
                                vec.wait_ge(xt_ready, at(c, KT, k + 1))
                                vec.tensor_tensor(x_t[slot][1][:, k], xt[:, k], x_t[slot][0][:, k].bitcast(F32),
                                                  ALU.subtract).then_inc(x_t_ready, 1)

                        def shift():
                            vec.wait_ge(x_t_ready, at(c, KT, KT))
                            vec.wait_ge(router_full, at(c, 1, 1))
                            vec.tensor_tensor(logits, misc_ps[0][:, 0:CT * EXPERTS].rearrange("p (t e) -> p t e", t=CT),
                                              router_b[:].unsqueeze(1).to_broadcast([P, CT, EXPERTS]),
                                              ALU.add).then_inc(vec_step, step.one())
                            step.wait()
                            vec.tensor_reduce(row_max[:], logits, X_AXIS, ALU.max).then_inc(vec_step, step.one())
                            step.wait()
                            vec.tensor_tensor(logits, logits, column(row_max[:], CT, EXPERTS),
                                              ALU.subtract).then_inc(shifted, 1)

                        def probabilities():
                            vec.wait_ge(exp_ready, at(c, 1, 1))
                            vec.tensor_reduce(row_sum[:], logits, X_AXIS, ALU.add).then_inc(vec_step, step.one())
                            step.wait()
                            vec.reciprocal(row_sum[:], row_sum[:]).then_inc(vec_step, step.one())
                            step.wait()
                            vec.tensor_tensor(logits, logits, column(row_sum[:], CT, EXPERTS),
                                              ALU.mult).then_inc(vec_step, step.one())

                        def choose():
                            step.wait()
                            for t in range(CT):
                                vec.max(top[:, t], logits[:, t]).then_inc(vec_step, step.one())
                            step.wait()
                            for t in range(CT):
                                vec.match_replace(marked[:, t], top[:, t], logits[:, t], -1.0).then_inc(vec_step, step.one())
                            vec.tensor_reduce(top_sum[:], top[:], X_AXIS, ALU.add).then_inc(vec_step, step.one())
                            step.wait()
                            vec.scalar_tensor_tensor(weight, marked, 0.0, logits, ALU.is_lt, ALU.mult).then_inc(vec_step, step.one())
                            vec.reciprocal(top_sum[:], top_sum[:]).then_inc(vec_step, step.one())
                            step.wait()
                            vec.tensor_tensor(weight, weight, column(top_sum[:], CT, EXPERTS),
                                              ALU.mult).then_inc(vec_step, step.one())

                        def split():
                            for part in range(PARTS):
                                from_ = weight if part == 0 else rest
                                step.wait()
                                ins = vec.tensor_copy(parts[:, :, :, part], from_.rearrange("p t (g e) -> p t g e", g=GROUPS))
                                if part == PARTS - 1:
                                    ins.then_inc(weight_split, 1)
                                else:
                                    ins.then_inc(vec_step, step.one())
                                    step.wait()
                                    vec.tensor_tensor(rest.rearrange("p t (g e) -> p t g e", g=GROUPS),
                                                      from_.rearrange("p t (g e) -> p t g e", g=GROUPS),
                                                      parts[:, :, :, part], ALU.subtract).then_inc(vec_step, step.one())

                        return {5: statistics, 7: normalise, 10: low_halves, 15: shift, 18: probabilities, 20: choose,
                                23: split}

                    def add_back(c):
                        vec.wait_ge(res_in, at(c, 16, 16))
                        for half in range(KT):
                            vec.wait_ge(y_back, at(c, KT, half + 1))
                            part = x[:, 2 * half:2 * half + 2].rearrange("p t n -> p (t n)")
                            vec.tensor_tensor(part, part, misc_ps[half][:], ALU.add).then_inc(x_ready, 1)

                    def main(c, slot, back, prepare):
                        b = c // PER_BATCH
                        if back:
                            add_back(c - 1)
                        pieces = prepare_pieces(c + 1, 1 - slot) if prepare else {}
                        for q in range(HIDDEN):
                            vec.wait_ge(hidden_ready, at(c, HIDDEN, q + 1))
                            if q < PAIRS:
                                vec.tensor_tensor(hidden[:, q % 2], hidden[:, q % 2], spread_ps[q % 2][:],
                                                  ALU.mult).then_inc(vec_step, step.one())
                                step.wait()
                            vec.wait_ge(y_step, at(c, HIDDEN, max(0, q - LAG + 1)))
                            vec.tensor_copy(scaled[0][:, q % LAG], hidden[:, q % 2]).then_inc(vec_step, step.one())
                            step.wait()
                            vec.tensor_tensor(scaled[1][:, q % LAG], hidden[:, q % 2], scaled[0][:, q % LAG].bitcast(F32),
                                              ALU.subtract).then_inc(scaled_ready, 1)
                            if q in pieces:
                                pieces[q]()
                        vec.wait_ge(y_step, at(c, HIDDEN, HIDDEN))
                        vec.wait_ge(scaled_ready, at(c, HIDDEN, HIDDEN))
                        for d in range(KT):
                            vec.tensor_scalar(y_t[:, d], y_ps[d][:], b2_col[:, d:d + 1], mod[:, GATE_B * KT + d, bass.ds(b, 1)],
                                              ALU.add, ALU.mult).then_inc(y_t_ready, 1)
                        step.restart()

                    def first():
                        statistics, normalise, low_halves, shift, probabilities, choose, split = prepare_pieces(0, 0).values()
                        statistics()
                        loading.vector(vec, 0, 1)
                        loading.wait_small(vec)
                        loading.wait_identity(vec)
                        vec.tensor_copy(ident_b[:], ident[:]).then_inc(small_ready, 1)
                        vec.tensor_tensor(b2_col[:], shared_b2[:, 0], shared_b2[:, 1], ALU.add).then_inc(small_ready, 1)
                        normalise()
                        loading.vector(vec, 1, 3)
                        low_halves()
                        loading.vector(vec, 3, 6)
                        shift()
                        loading.vector(vec, 6, 8)
                        probabilities()
                        choose()
                        split()
                        loading.vector(vec, 8)
                        own_step = Steps(vec, b2_step)
                        vec.wait_ge(b2_in, 16 * PARTS)
                        for part in range(PARTS):
                            vec.tensor_copy(b2[:, part], b2_raw[:]).then_inc(b2_step, own_step.one())
                            if part < PARTS - 1:
                                own_step.wait()
                                vec.tensor_tensor(b2_raw[:], b2_raw[:], b2[:, part], ALU.subtract).then_inc(b2_step, own_step.one())
                                own_step.wait()
                        step.restart()
                    chunks(vec, first, main, lambda: add_back(NCHUNK - 1))


HEADS, HEAD_DIM = 16, 16
ROWS_V, QUERY_V = 8, 32
V_ALL = ROWS_V * HEAD_DIM
V_SCORE, V_ONE, V_QUERY = V_ALL, V_ALL + ROWS_V, V_ALL + ROWS_V + 2
V_WIDTH = V_QUERY + HEADS
V_USED = V_ONE + 1
SPLITS = 3


def stage_project(nc, x_in, h_d, parts_d, values_d, mod_d, w):
    T_USES, QK_USES, V_USES = CHUNKS * KT, 2 * KT * CHUNKS, TILES
    USES, BANKS = T_USES + QK_USES + V_USES, 4
    assert USES % BANKS == 0
    with ExitStack() as ctx:
        room = Room(nc, ctx, "pj")
        sb, sem = room.sb, room.counter
        ident = sb("ident", [P, P])
        w_q, w_k = room.pair("w_q", [P, KT, DIM]), room.pair("w_k", [P, KT, DIM])
        w_v = room.pair("w_v", [P, KT, V_WIDTH])
        cols = sb("cols", [P, 4, KT])
        q_bias = sb("q_bias", [P, KT])
        v_bias = sb("v_bias", [P, V_WIDTH])
        mod = sb("mod", [P, BATCH, 2, DIM])
        mod_now = sb("mod_now", [P, 2, DIM])
        power = sb("power", [P, TILES])
        loading_of = lambda pair, source: (cut(pair, slice(None)), source.rearrange("(k p) n -> p k n", p=P))
        staging = sb("staging", [P, 2, KT * DIM])
        loading = Loading(room, "load", [
            (cols[:], w["cols"]),
            (mod[:], mod_d[1, :, 0:2 * DIM].rearrange("b (w n) -> b w n", n=DIM).partition_broadcast(P)),
        ], [loading_of(w_q, w["WqT"]), loading_of(w_k, w["WkT"])], [staging[:, n] for n in range(2)], ident[:])

        raw = sb("raw", [P, KT, V_WIDTH])
        wqv = sb("wqv", [P, KT, HEADS * QUERY_V])
        bqv = sb("bqv", [P, HEADS * QUERY_V])
        ws = sb("ws", [P, QUERY_V + HEAD_DIM + 1])
        prod_v = sb("prod_v", [P, KT + 1, V_ALL])
        fold_in, fold_step, power_ready, folded = (
            room.sem("fold_in"), room.sem("fold_step"), room.sem("power_ready"), room.sem("folded"))

        def load_fold(sp):
            loads = [(raw[:, :, 0:V_ALL], w["WvT"].rearrange("(k p) n -> p k n", p=P)),
                     (wqv[:], w["WqvT"].rearrange("(k p) n -> p k n", p=P)),
                     (bqv[:], w["bqv"].partition_broadcast(P)),
                     (v_bias[:, 0:V_ALL], w["bv"].partition_broadcast(P)),
                     (ws[:, 0:QUERY_V + HEAD_DIM], w["Ws"].rearrange("a n -> (a n)").partition_broadcast(P)),
                     (ws[:, QUERY_V + HEAD_DIM:], w["bs"].partition_broadcast(P))]
            for destination, source in loads:
                sp.dma_start(destination, source).then_inc(fold_in, 16)

        def query_scale(vec):
            vec.memset(raw[:, :, V_ONE:V_QUERY], 0.0).then_inc(fold_step, 1)
            vec.memset(v_bias[:, V_ONE:V_ONE + 1], 1.0).then_inc(fold_step, 1)
            vec.memset(v_bias[:, V_ONE + 1:V_QUERY], 0.0).then_inc(fold_step, 1)
            loading.wait_small(vec)
            vec.tensor_scalar(q_bias[:], cols[:, 2], float(HEAD_DIM) ** -0.5, None, ALU.mult).then_inc(fold_step, 1)

        def fold(vec):
            step = Steps(vec, fold_step)
            step.n = 4
            vec.wait_ge(fold_in, 16 * 6)
            for n, source in enumerate([raw[:, k, 0:V_ALL] for k in range(KT)] + [v_bias[:, 0:V_ALL]]):
                vec.tensor_tensor(prod_v[:, n].rearrange("p (r d) -> p r d", d=HEAD_DIM),
                                  source.rearrange("p (r d) -> p r d", d=HEAD_DIM),
                                  ws[:, QUERY_V:QUERY_V + HEAD_DIM].unsqueeze(1).to_broadcast([P, ROWS_V, HEAD_DIM]),
                                  ALU.mult).then_inc(fold_step, step.one())
            step.wait()
            for n, out in enumerate([raw[:, k, V_SCORE:V_ONE] for k in range(KT)] + [v_bias[:, V_SCORE:V_ONE]]):
                vec.tensor_reduce(out, prod_v[:, n].rearrange("p (r d) -> p r d", d=HEAD_DIM), X_AXIS,
                                  ALU.add).then_inc(fold_step, step.one())
            query = [(wqv[:, k], raw[:, k, V_QUERY:]) for k in range(KT)] + [(bqv[:], v_bias[:, V_QUERY:])]
            for source, out in query:
                vec.tensor_tensor(source.rearrange("p (h n) -> p h n", n=QUERY_V),
                                  source.rearrange("p (h n) -> p h n", n=QUERY_V),
                                  ws[:, 0:QUERY_V].unsqueeze(1).to_broadcast([P, HEADS, QUERY_V]),
                                  ALU.mult).then_inc(fold_step, step.one())
            step.wait()
            for source, out in query:
                vec.tensor_reduce(out, source.rearrange("p (h n) -> p h n", n=QUERY_V), X_AXIS,
                                  ALU.add).then_inc(fold_step, step.one())
            step.wait()
            for source, out in query:
                vec.tensor_scalar(out, out, float(QUERY_V) ** -0.5, None, ALU.mult).then_inc(fold_step, step.one())
            step.wait()
            vec.tensor_scalar(v_bias[:, V_QUERY:], v_bias[:, V_QUERY:], ws[:, QUERY_V + HEAD_DIM:], None,
                              ALU.add).then_inc(fold_step, step.one())
            vec.tensor_copy(w_v[0][:], raw[:]).then_inc(fold_step, step.one())
            step.wait()
            vec.tensor_tensor(w_v[1][:], raw[:], w_v[0][:].bitcast(F32), ALU.subtract).then_inc(folded, 1)

        x = sb("x", [P, TILES, DIM])
        h = sb("h", [P, TILES, DIM])
        rows = sb("rows", [P, TILES, DIM])
        stats, moments = sb("stats", [P, TILES, 6]), sb("moments", [P, TILES, 2])
        var, rstd, scratch = sb("var", [P, TILES]), sb("rstd", [P, TILES]), sb("scratch", [P, TILES])
        xt = sb("xt", [P, 2, CHUNK])
        x_t = room.pair("x_t", [P, KT, SEQ])
        qk_tmp = sb("qk_tmp", [P, 2, CHUNK])
        parts = sb("parts", [P, 2, KT, SPLITS, SEQ], BF16)
        values = sb("values", [P, TILES, V_WIDTH])
        banks = [room.ps(f"bank{n}", [P, 512]) for n in range(BANKS)]

        x_in_sem, x_used = sem("x_in"), sem("x_used")
        var_ready, rstd_ready = sem("var_ready"), sem("rstd_ready")
        normal_ready, h_scaled, h_ready, h_stored = sem("normal_ready"), sem("h_scaled"), sem("h_ready"), sem("h_stored")
        mod_copied = sem("mod_copied")
        rows_ready = sem("rows_ready")
        full = sem("full")
        xt_ready, x_t_ready = sem("xt_ready"), sem("x_t_ready")
        part_ready, parts_ready, parts_stored = sem("part_ready"), sem("parts_ready"), sem("parts_stored")
        values_ready, values_stored = sem("values_ready"), sem("values_stored")
        vec_step = room.sem("vec_step")

        src = x_in.rearrange("(b t p) n -> b p t n", b=BATCH, p=P)
        dst_h = h_d.rearrange("(b t p) n -> b p t n", b=BATCH, p=P)
        dst_v = values_d.rearrange("(b t p) n -> b p t n", b=BATCH, p=P)

        def trips(engine, body):
            with engine.Fori(0, BATCH - 1) as trip:
                body(trip, False)
            body(BATCH - 1, True)

        def bank_free(pe, trip, use):
            u = use - BANKS
            if u < 0:
                pe.wait_ge(values_ready, at(trip, TILES, 0))
            elif u < T_USES:
                pe.wait_ge(xt_ready, at(trip, T_USES, u + 1))
            elif u < T_USES + QK_USES:
                pe.wait_ge(part_ready, at(trip, QK_USES, u - T_USES + 1))
            else:
                pe.wait_ge(values_ready, at(trip, TILES, u - T_USES - QK_USES + 1))

        start_counters(nc, room)
        with nc.Block() as block:
            @block.sync
            def _(sp):
                def h_out(index):
                    sp.wait_ge(h_ready, at(index, TILES, TILES))
                    sp.dma_start(dst_h[index], h[:]).then_inc(h_stored, 16)
                sp.dma_start(x[:], src[0]).then_inc(x_in_sem, 16)
                loading.small(sp)
                loading.sync(sp)
                load_fold(sp)
                h_out(0)

                def trip_of(trip, last):
                    if not last:
                        sp.wait_ge(x_used, at(trip, 1, 1))
                        sp.dma_start(x[:], src[trip + 1]).then_inc(x_in_sem, 16)
                    for n in range(2 * KT):
                        which, m = divmod(n, KT)
                        sp.wait_ge(parts_ready, at(trip, QK_USES, CHUNKS * (n + 1)))
                        sp.dma_start(parts_d[which, trip, :, m * P:(m + 1) * P, :].rearrange("s p n -> p s n"),
                                     parts[:, which, m]).then_inc(parts_stored, 16)
                    sp.wait_ge(values_ready, at(trip, TILES, TILES))
                    sp.dma_start(dst_v[trip], values[:]).then_inc(values_stored, 16)
                    if not last:
                        h_out(trip + 1)
                trips(sp, trip_of)
                sp.wait_ge(h_stored, at(BATCH, 16, 0))
                sp.wait_ge(parts_stored, at(BATCH, 16 * 2 * KT, 0))
                sp.wait_ge(values_stored, at(BATCH, 16, 0))

            @block.gpsimd
            def _(pool):
                pool.memset(power[:], -0.5).then_inc(power_ready, 1)
                pool.wait_ge(power_ready, 1)
                loading.gpsimd(pool)
                loading.wait_small(pool)

                def rows_of(index):
                    pool.wait_ge(h_ready, at(index, TILES, 0))
                    pool.wait_ge(var_ready, at(index, 2, 1))
                    pool.tensor_tensor(rstd[:], var[:], power[:], ALU.pow).then_inc(rstd_ready, 1)
                    pool.tensor_copy(mod_now[:], mod[:, index]).then_inc(mod_copied, 1)
                    pool.wait_ge(mod_copied, at(index, 1, 1))
                    for t in range(TILES):
                        pool.wait_ge(normal_ready, at(index, TILES, t + 1))
                        pool.tensor_tensor(h[:, t], h[:, t], mod_now[:, SCALE_A], ALU.mult).then_inc(h_scaled, 1)
                        pool.wait_ge(h_scaled, at(index, TILES, t + 1))
                        pool.tensor_tensor(h[:, t], h[:, t], mod_now[:, SHIFT_A], ALU.add).then_inc(h_ready, 1)
                    pool.wait_ge(var_ready, at(index, 2, 2))
                    pool.tensor_tensor(rstd[:], var[:], power[:], ALU.pow).then_inc(rstd_ready, 1)
                rows_of(0)
                trips(pool, lambda trip, last: None if last else rows_of(trip + 1))

            @block.tensor
            def _(pe):
                loading.wait_identity(pe)
                loading.wait_weights(pe)

                def trip_of(trip, last):
                    pe.wait_ge(rows_ready, at(trip, 1, 1))
                    for u in range(T_USES):
                        c, k = divmod(u, KT)
                        bank_free(pe, trip, u)
                        for t in range(CT):
                            mm = pe.transpose(banks[u % BANKS][:, t * P:(t + 1) * P],
                                              rows[:, c * CT + t, k * P:(k + 1) * P], ident[:])
                        mm.then_inc(full, 1)
                    for n in range(QK_USES):
                        which, m, c = n // (KT * CHUNKS), n // CHUNKS % KT, n % CHUNKS
                        use = T_USES + n
                        bank_free(pe, trip, use)
                        pe.wait_ge(x_t_ready, at(trip, T_USES, KT * (c + 1)))
                        for k in range(KT):
                            mm = product3(pe, banks[use % BANKS][:],
                                          cut((w_q, w_k)[which], slice(None), k, slice(m * P, (m + 1) * P)),
                                          cut(x_t, slice(None), k, slice(c * CHUNK, (c + 1) * CHUNK)),
                                          k == 0, k == KT - 1)
                        mm.then_inc(full, 1)
                    pe.wait_ge(folded, 1)
                    for t in range(TILES):
                        use = T_USES + QK_USES + t
                        bank_free(pe, trip, use)
                        for k in range(KT):
                            mm = product3(pe, banks[use % BANKS][:, 0:V_WIDTH],
                                          cut(x_t, slice(None), k, slice(t * P, (t + 1) * P)),
                                          cut(w_v, slice(None), k), k == 0, k == KT - 1)
                        mm.then_inc(full, 1)
                trips(pe, trip_of)

            @block.scalar
            def _(act):
                loading.scalar(act)
                loading.wait_small(act)
                act.wait_ge(fold_step, 4)

                def trip_of(trip, last):
                    for u in range(T_USES):
                        c, k = divmod(u, KT)
                        act.wait_ge(full, at(trip, USES, u + 1))
                        act.wait_ge(x_t_ready, at(trip, T_USES, max(0, u - 1)))
                        for out in (xt[:, u % 2], x_t[0][:, k, c * CHUNK:(c + 1) * CHUNK]):
                            ins = act.activation(out, banks[u % BANKS][:], ACT.Identity,
                                                 bias=cols[:, 1, k:k + 1], scale=cols[:, 0, k:k + 1])
                        ins.then_inc(xt_ready, 1)
                    act.wait_ge(parts_stored, at(trip, 16 * 2 * KT, 0))
                    for n in range(QK_USES):
                        which, m, c = n // (KT * CHUNKS), n // CHUNKS % KT, n % CHUNKS
                        use = T_USES + n
                        act.wait_ge(full, at(trip, USES, use + 1))
                        act.wait_ge(parts_ready, at(trip, QK_USES, max(0, n - 1)))
                        bias = cols[:, 3, m:m + 1] if which else q_bias[:, m:m + 1]
                        for out in (qk_tmp[:, n % 2], parts[:, which, m, 0, c * CHUNK:(c + 1) * CHUNK]):
                            ins = act.activation(out, banks[use % BANKS][:], ACT.Identity, bias=bias,
                                                 scale=1.0 if which else float(HEAD_DIM) ** -0.5)
                        ins.then_inc(part_ready, 1)
                trips(act, trip_of)

            @block.vector
            def _(vec):
                step = Steps(vec, vec_step)

                def normalise(index):
                    def variance():
                        step.wait()
                        for t in range(TILES):
                            vec.bn_aggr(moments[:, t], stats[:, t]).then_inc(vec_step, step.one())
                        step.wait()
                        vec.tensor_scalar(var[:], moments[:, :, 1], EPS, None, ALU.add).then_inc(var_ready, 1)

                    def statistics():
                        vec.wait_ge(x_in_sem, at(index, 16, 16))
                        for t in range(TILES):
                            vec.bn_stats(stats[:, t], x[:, t]).then_inc(vec_step, step.one())
                        variance()

                    def first():
                        vec.wait_ge(rstd_ready, at(index, 2, 1))
                        newton_rsqrt(vec, step, rstd[:], var[:], scratch[:])
                        step.wait()
                        vec.wait_ge(h_stored, at(index, 16, 0))
                        for t in range(TILES):
                            vec.tensor_scalar(h[:, t], x[:, t], moments[:, t, 0:1], rstd[:, t:t + 1],
                                              ALU.subtract, ALU.mult).then_inc(normal_ready, 1)

                    def statistics_h(t):
                        vec.wait_ge(h_ready, at(index, TILES, t + 1))
                        vec.bn_stats(stats[:, t], h[:, t]).then_inc(vec_step, step.one())

                    def last():
                        vec.wait_ge(rstd_ready, at(index, 2, 2))
                        newton_rsqrt(vec, step, rstd[:], var[:], scratch[:])
                        step.wait()
                        for t in range(TILES):
                            ins = vec.tensor_scalar(rows[:, t], h[:, t], moments[:, t, 0:1], rstd[:, t:t + 1],
                                                    ALU.subtract, ALU.mult)
                        ins.then_inc(rows_ready, 1)

                    def x_free():
                        vec.wait_ge(normal_ready, at(index, TILES, TILES))
                        vec.tensor_copy(scratch[:, 0:1], scratch[:, 0:1]).then_inc(x_used, 1)

                    return ([statistics, first, x_free] + [lambda t=t: statistics_h(t) for t in range(TILES)]
                            + [variance, last])

                first = normalise(0)
                first.pop(0)()
                query_scale(vec)
                first.pop(0)()
                first.pop(0)()
                loading.vector(vec)
                for piece in first:
                    piece()
                fold(vec)
                step.restart()

                def trip_of(trip, last):
                    pieces = [] if last else normalise(trip + 1)
                    for u in range(T_USES):
                        c, k = divmod(u, KT)
                        part = (slice(None), k, slice(c * CHUNK, (c + 1) * CHUNK))
                        vec.wait_ge(xt_ready, at(trip, T_USES, u + 1))
                        vec.tensor_tensor(x_t[1][part], xt[:, u % 2], x_t[0][part].bitcast(F32),
                                          ALU.subtract).then_inc(x_t_ready, 1)
                    for n in range(QK_USES):
                        which, m, c = n // (KT * CHUNKS), n // CHUNKS % KT, n % CHUNKS
                        tmp = qk_tmp[:, n % 2]
                        out = [parts[:, which, m, s, c * CHUNK:(c + 1) * CHUNK] for s in range(SPLITS)]
                        vec.wait_ge(part_ready, at(trip, QK_USES, n + 1))
                        vec.tensor_tensor(tmp, tmp, out[0], ALU.subtract).then_inc(vec_step, step.one())
                        step.wait()
                        vec.tensor_copy(out[1], tmp).then_inc(vec_step, step.one())
                        step.wait()
                        vec.tensor_tensor(out[2], tmp, out[1], ALU.subtract).then_inc(parts_ready, 1)
                        if pieces and n >= 1:
                            pieces.pop(0)()
                    vec.wait_ge(values_stored, at(trip, 16, 0))
                    for t in range(TILES):
                        use = T_USES + QK_USES + t
                        vec.wait_ge(full, at(trip, USES, use + 1))
                        vec.tensor_tensor(values[:, t], banks[use % BANKS][:, 0:V_WIDTH], v_bias[:],
                                          ALU.add).then_inc(values_ready, 1)
                        if pieces:
                            pieces.pop(0)()
                    for piece in pieces:
                        piece()
                    step.restart()
                trips(vec, trip_of)


def stage_attention(nc, parts_d, values_d, attended, tail):
    ALL = BATCH * HEADS
    TERMS = 6
    STACK = TERMS * HEAD_DIM
    SHIFT = SPLITS * TILES
    FULL = STACK + SHIFT
    SLOTS = 4
    HALVES = SEQ // 512
    GROUP = 3
    GROUPS = -(-TILES // GROUP)
    AHEAD = 2
    SPREAD_SLOT = TILES - AHEAD
    COMPOSE_SLOT = 1
    with ExitStack() as ctx:
        room = Room(nc, ctx, "at")
        sb, sem = room.sb, room.counter
        values = sb("values", [P, BATCH * TILES, V_WIDTH])
        q_stack = [sb(f"q_stack{n}", [P, SEQ], BF16) for n in range(SLOTS)]
        k_stack = [sb(f"k_stack{n}", [P, SEQ], BF16) for n in range(SLOTS)]
        prob = [sb(f"prob{n}", [P, TILES, SEQ]) for n in range(2)]
        half_max, q_max = sb("half_max", [P, TILES, HALVES]), sb("q_max", [P, TILES])
        max_cols = sb("max_cols", [P, P], BF16)
        ident = sb("ident", [P, P], BF16)
        mask = sb("mask", [P, TILES])
        mixed = [sb(f"mixed{n}", [P, TILES, V_USED]) for n in range(2)]
        recip, weight = sb("recip", [P, TILES]), sb("weight", [P, TILES, ROWS_V])
        row_max, row_sum = sb("row_max", [P, TILES]), sb("row_sum", [P, TILES])
        product = sb("product", [P, TILES, ROWS_V, HEAD_DIM])
        max_ps = [room.ps(f"max{n}", [P, 512]) for n in range(HALVES)]
        score_ps = [room.ps(f"score{n}", [P, SEQ]) for n in range(2)]
        out_ps = [room.ps(f"out{n}", [P, 512]) for n in range(2)]
        turned_ps = max_ps[0][:].bitcast(BF16)[:, 0:P]

        values_in = room.sem("values_in")
        constants, const_step = room.sem("constants"), room.sem("const_step")
        q_in, k_in = [sem(f"q_in{n}") for n in range(SLOTS)], [sem(f"k_in{n}") for n in range(SLOTS)]
        max_full = [sem(f"max_full{n}") for n in range(HALVES)]
        max_read, max_split, max_turned, shift_ready = (
            sem("max_read"), sem("max_split"), sem("max_turned"), sem("shift_ready"))
        score_full, prob_ready = sem("score_full"), sem("prob_ready")
        out_full, mixed_ready = sem("out_full"), sem("mixed_ready")
        weight_shifted, weight_exp, weight_ready = sem("weight_shifted"), sem("weight_exp"), sem("weight_ready")
        composed, pool_step, vec_step = sem("composed"), room.sem("pool_step"), room.sem("vec_step")
        STACK_DMAS = TERMS
        AHEAD_STEP = 0
        staging = prob[1][:].rearrange("p t n -> p (t n)")
        ahead = tail.loading([staging[:, n * SEQ:(n + 1) * SEQ] for n in range(len(tail.weights))])

        class Head:
            def __init__(self, trip, offset):
                self.trip, self.offset = trip, offset
                self.slot, self.half = offset % SLOTS, offset % 2
                self.number = trip * SLOTS + offset

            def back(self, n):
                return Head(self.trip, self.offset - n)

            def at(self, per_head, step):
                return self.trip * (SLOTS * per_head) + (START + self.offset * per_head + step)

            def slot_at(self, per_use):
                return self.trip * per_use + (START + (self.offset // SLOTS + 1) * per_use)

        def steps(engine, body):
            fill = 3
            for n in range(-1, fill):
                body(Head(0, n), n)
            loops = (ALL - 2 - fill) // SLOTS
            with engine.Fori(0, loops) as trip:
                for n in range(SLOTS):
                    body(Head(trip, fill + n), None)
            for n in range(fill + loops * SLOTS, ALL + 3):
                body(Head(0, n), n)

        def stages(u, number):
            def there(back):
                return number is None or 0 <= number - back < ALL
            return [u.back(n) if there(n) else None for n in (0, 1, 2, 3, -1)]

        def max_work(maxima, following, t):
            head, tile = (maxima, t + AHEAD) if t < TILES - AHEAD else (following, t + AHEAD - TILES)
            return (head, tile) if head else None

        start_counters(nc, room)
        with nc.Block() as block:
            @block.sync
            def _(sp):
                def load(head):
                    number = head.number
                    b, h = number // HEADS, number % HEADS
                    for n, (q_part, k_part) in enumerate(((0, 0), (1, 0), (2, 0), (0, 1), (1, 1), (0, 2))):
                        for which, part, stack, landed in ((0, q_part, q_stack, q_in), (1, k_part, k_stack, k_in)):
                            sp.dma_start(stack[head.slot][n * HEAD_DIM:(n + 1) * HEAD_DIM, :],
                                         parts_d[which, b, part, bass.ds(h * HEAD_DIM, HEAD_DIM), :]
                                         ).then_inc(landed[head.slot], 16)

                load(Head(0, 0))
                load(Head(0, 1))
                sp.dma_start(values[:], values_d.rearrange("(t p) n -> p t n", p=P)).then_inc(values_in, 16)

                def step_of(u, number):
                    if number != -1 and (number is None or number + 2 < ALL):
                        if number is None or number >= 2:
                            sp.wait_ge(score_full, u.back(2).at(TILES, TILES))
                        load(u.back(-2))
                    if number == AHEAD_STEP:
                        ahead.small(sp)
                        ahead.sync(sp)
                    if number == ALL:
                        ahead.wait_small(sp)
                steps(sp, step_of)

            @block.gpsimd
            def _(pool):
                step = Steps(pool, const_step)
                for buffer, value in [(max_cols[:], 0.0), (ident[:], 0.0), (mask[:], 0.0)] + [
                        (k_stack[n][STACK:P, :], 1.0) for n in range(SLOTS)]:
                    pool.memset(buffer, value).then_inc(const_step, step.one())
                    step.wait()
                pool.affine_select(out=ident[:], in_=ident[:], compare_op=ALU.not_equal, fill=1.0, base=0,
                                   pattern=[[-1, P]], channel_multiplier=1).then_inc(const_step, step.one())
                step.wait()
                for part in range(SPLITS):
                    pool.affine_select(out=mask[:], in_=mask[:], compare_op=ALU.not_equal, fill=1.0,
                                       base=-(STACK + part * TILES), pattern=[[-1, TILES]],
                                       channel_multiplier=1).then_inc(const_step, step.one())
                    step.wait()
                pool.memset(product[:, 0, 0, 0:1], 0.0).then_inc(constants, 1)
                ahead.gpsimd(pool)
                sums = Steps(pool, pool_step)

                def step_of(u, number):
                    head = stages(u, number)[3]
                    if head is None:
                        return
                    b, h = head.number // HEADS, head.number % HEADS
                    pool.wait_ge(weight_ready, head.at(1, 1))
                    pool.wait_ge(composed, head.at(1, 0))
                    pool.tensor_tensor(product[:].rearrange("p t r d -> p t (r d)").rearrange("p t (r d) -> p t r d", d=HEAD_DIM),
                                       mixed[head.half][:, :, 0:V_ALL].rearrange("p t (r d) -> p t r d", d=HEAD_DIM),
                                       weight[:].unsqueeze(3).to_broadcast([P, TILES, ROWS_V, HEAD_DIM]),
                                       ALU.mult).then_inc(pool_step, sums.one())
                    n = ROWS_V // 2
                    while n > 1:
                        sums.wait()
                        pool.tensor_tensor(product[:, :, 0:n], product[:, :, 0:n], product[:, :, n:2 * n],
                                           ALU.add).then_inc(pool_step, sums.one())
                        n //= 2
                    sums.wait()
                    pool.tensor_tensor(attended[:, bass.ds(b * TILES, TILES), bass.ds(h * HEAD_DIM, HEAD_DIM)],
                                       product[:, :, 0], product[:, :, 1], ALU.add).then_inc(composed, 1)
                    sums.restart()
                steps(pool, step_of)

            @block.tensor
            def _(pe):
                pe.wait_ge(constants, 1)

                def step_of(u, number):
                    maxima, scoring, mixing, _, following = stages(u, number)
                    if number == 2:
                        pe.wait_ge(values_in, 16)

                    def max_tile(head, t):
                        if t == 0:
                            pe.wait_ge(q_in[head.slot], head.slot_at(16 * STACK_DMAS))
                            pe.wait_ge(k_in[head.slot], head.slot_at(16 * STACK_DMAS))
                        for half in range(HALVES):
                            if t == 0 and half == 0:
                                pe.wait_ge(shift_ready, head.at(1, 0))
                            pe.wait_ge(max_read, head.at(TILES * HALVES, max(0, t * HALVES + half - HALVES + 1)))
                            pe.matmul(max_ps[half][:], q_stack[head.slot][0:STACK, t * P:(t + 1) * P],
                                      k_stack[head.slot][0:STACK, half * 512:(half + 1) * 512],
                                      start=True, stop=True).then_inc(max_full[half], 1)

                    def score_tile(j):
                        head = scoring
                        if j == 0:
                            pe.wait_ge(shift_ready, head.at(1, 1))
                        pe.wait_ge(prob_ready, head.at(TILES, max(0, j - 1)))
                        for half in range(HALVES):
                            mm = pe.matmul(score_ps[j % 2][:, half * 512:(half + 1) * 512],
                                           k_stack[head.slot][0:FULL, j * P:(j + 1) * P],
                                           q_stack[head.slot][0:FULL, half * 512:(half + 1) * 512],
                                           start=True, stop=True)
                        mm.then_inc(score_full, 1)

                    def mix_tile(t, between=None):
                        head = mixing
                        b = head.number // HEADS
                        group = head.offset * GROUPS + t // GROUP
                        bank = out_ps[group % 2]
                        place = (t % GROUP) * V_USED
                        if t == 0:
                            pe.wait_ge(prob_ready, head.at(TILES, TILES))
                        if t % GROUP == 0:
                            back = t // GROUP - 1
                            if back >= 0:
                                pe.wait_ge(mixed_ready, head.at(GROUPS, back))
                            elif number is None or head.offset > 0:
                                pe.wait_ge(mixed_ready, head.back(1).at(GROUPS, GROUPS - 1))
                        for j in range(TILES):
                            if j == TILES // 2 and between:
                                between()
                            mm = pe.matmul(bank[:, place:place + V_USED], prob[head.half][:, j, t * P:(t + 1) * P],
                                           values[:, b * TILES + j, 0:V_USED], start=(j == 0), stop=(j == TILES - 1))
                        if t % GROUP == GROUP - 1 or t == TILES - 1:
                            mm.then_inc(out_full, 1)

                    for t in range(TILES):
                        work = max_work(maxima, following, t)
                        middle = t > SPREAD_SLOT and mixing
                        if work and t != SPREAD_SLOT and not middle:
                            max_tile(*work)
                        if scoring:
                            score_tile(t)
                        if maxima and t == SPREAD_SLOT:
                            pe.wait_ge(max_split, maxima.at(1, 1))
                            pe.transpose(turned_ps, max_cols[:], ident[:]).then_inc(max_turned, 1)
                        if mixing:
                            mix_tile(t, (lambda: max_tile(*work)) if work and middle else None)
                        if work and t == SPREAD_SLOT:
                            max_tile(*work)
                steps(pe, step_of)

            @block.scalar
            def _(act):
                def step_of(u, number):
                    _, scoring, mixing, composing, _ = stages(u, number)
                    if number == AHEAD_STEP + 2:
                        ahead.wait_weights(act)

                    def copy_group(g):
                        head = mixing
                        act.wait_ge(out_full, head.at(GROUPS, g + 1))
                        if g == 0 and (number is None or number >= 4):
                            act.wait_ge(composed, head.back(2).at(1, 1))
                        n = min(GROUP, TILES - g * GROUP)
                        bank = out_ps[(head.offset * GROUPS + g) % 2]
                        act.activation(mixed[head.half][:, g * GROUP:g * GROUP + n],
                                       bank[:, 0:n * V_USED].rearrange("p (t v) -> p t v", v=V_USED),
                                       ACT.Copy).then_inc(mixed_ready, 1)

                    for t in range(TILES):
                        if scoring:
                            act.wait_ge(score_full, scoring.at(TILES, t + 1))
                            act.activation(prob[scoring.half][:, t], score_ps[t % 2][:], ACT.Exp).then_inc(prob_ready, 1)
                        if mixing and t in (GROUP, 2 * GROUP):
                            copy_group(t // GROUP - 1)
                        if composing and t == COMPOSE_SLOT + 1:
                            act.wait_ge(weight_shifted, composing.at(1, 1))
                            act.activation(weight[:], weight[:], ACT.Exp).then_inc(weight_exp, 1)
                    if mixing:
                        copy_group(GROUPS - 1)
                    if number == AHEAD_STEP + 1:
                        ahead.scalar(act)
                steps(act, step_of)

            @block.vector
            def _(vec):
                step = Steps(vec, vec_step)
                vec.wait_ge(constants, 1)

                def step_of(u, number):
                    maxima, _, _, composing, following = stages(u, number)
                    if number == 2:
                        vec.wait_ge(values_in, 16)

                    def read_max(head, t):
                        for half in range(HALVES):
                            vec.wait_ge(max_full[half], head.at(TILES, t + 1))
                            vec.tensor_reduce(half_max[:, t, half:half + 1], max_ps[half][:], X_AXIS,
                                              ALU.max).then_inc(max_read, 1)

                    def split_max():
                        vec.wait_ge(max_read, maxima.at(TILES * HALVES, TILES * HALVES))
                        vec.tensor_reduce(q_max[:], half_max[:], X_AXIS, ALU.max, negate=True).then_inc(vec_step, step.one())
                        for part in range(SPLITS):
                            step.wait()
                            place = max_cols[:, STACK + part * TILES:STACK + (part + 1) * TILES]
                            ins = vec.tensor_copy(place, q_max[:])
                            if part == SPLITS - 1:
                                ins.then_inc(max_split, 1)
                            else:
                                ins.then_inc(vec_step, step.one())
                                step.wait()
                                vec.tensor_tensor(q_max[:], q_max[:], place, ALU.subtract).then_inc(vec_step, step.one())

                    def spread_max():
                        vec.wait_ge(max_turned, maxima.at(1, 1))
                        vec.tensor_tensor(q_stack[maxima.slot][STACK:FULL, :].rearrange("p (t n) -> p t n", t=TILES),
                                          turned_ps[STACK:FULL, :].unsqueeze(1).to_broadcast([SHIFT, TILES, P]),
                                          mask[STACK:FULL, :].unsqueeze(2).to_broadcast([SHIFT, TILES, P]),
                                          ALU.mult).then_inc(shift_ready, 1)

                    def composition():
                        head = composing
                        b, h = head.number // HEADS, head.number % HEADS
                        m = mixed[head.half]
                        vec.wait_ge(mixed_ready, head.at(GROUPS, GROUPS))
                        vec.reciprocal(recip[:], m[:, :, V_ONE]).then_inc(vec_step, step.one())
                        step.wait()
                        if number is None or head.offset > 0:
                            vec.wait_ge(composed, head.at(1, 0))
                        vec.tensor_tensor(weight[:], m[:, :, V_SCORE:V_ONE], column(recip[:], TILES, ROWS_V),
                                          ALU.mult).then_inc(vec_step, step.one())
                        step.wait()
                        vec.tensor_tensor(weight[:], weight[:],
                                          values[:, bass.ds(b * TILES, TILES), bass.ds(h + V_QUERY, 1)].to_broadcast([P, TILES, ROWS_V]),
                                          ALU.add).then_inc(vec_step, step.one())
                        step.wait()
                        vec.tensor_reduce(row_max[:], weight[:], X_AXIS, ALU.max).then_inc(vec_step, step.one())
                        step.wait()
                        vec.tensor_tensor(weight[:], weight[:], column(row_max[:], TILES, ROWS_V),
                                          ALU.subtract).then_inc(weight_shifted, 1)

                    def composition_weights():
                        vec.wait_ge(weight_exp, composing.at(1, 1))
                        vec.tensor_reduce(row_sum[:], weight[:], X_AXIS, ALU.add).then_inc(vec_step, step.one())
                        step.wait()
                        vec.reciprocal(row_sum[:], row_sum[:]).then_inc(vec_step, step.one())
                        step.wait()
                        vec.tensor_tensor(row_sum[:], row_sum[:], recip[:], ALU.mult).then_inc(vec_step, step.one())
                        step.wait()
                        vec.tensor_tensor(weight[:], weight[:], column(row_sum[:], TILES, ROWS_V),
                                          ALU.mult).then_inc(weight_ready, 1)

                    for t in range(TILES):
                        work = max_work(maxima, following, t)
                        if maxima and t == SPREAD_SLOT:
                            spread_max()
                        if work:
                            read_max(*work)
                        if composing and t == COMPOSE_SLOT:
                            composition()
                        if composing and t == COMPOSE_SLOT + 2:
                            composition_weights()
                        if maxima and t == SPREAD_SLOT - 1:
                            split_max()
                    if number == AHEAD_STEP + 1:
                        ahead.vector(vec)
                    step.restart()
                steps(vec, step_of)


class TailWeights:

    def __init__(self, nc, ctx, mod_cols_d, w):
        self.room = Room(nc, ctx, "tw")
        sb, pair = self.room.sb, self.room.pair
        hidden = w["Wr1T"].shape[1]
        self.ident = sb("ident", [P, P])
        self.f, self.r1, self.r2 = (
            pair("f", [P, KT, DIM]), pair("r1", [P, KT, hidden]), pair("r2", [P, hidden // P, DIM]))
        self.r, self.k, self.v = (pair(n, [P, KT, DIM]) for n in "rkv")
        self.cols = sb("cols", [P, 12])
        self.f_bias, self.r2_bias = sb("f_bias", [P, DIM]), sb("r2_bias", [P, DIM])
        self.mod_cols = sb("mod_cols", [P, MOD // P, BATCH])
        self.loads = [(self.cols[:], w["cols"]),
                      (self.f_bias[:], w["bf"].partition_broadcast(P)),
                      (self.r2_bias[:], w["br2"].partition_broadcast(P)),
                      (self.mod_cols[:], mod_cols_d[:, 1])]
        self.weights = [(cut(to, slice(None)), source.rearrange("(k p) n -> p k n", p=P)) for to, source in (
            (self.f, w["WfT"]), (self.r1, w["Wr1T"]), (self.r2, w["Wr2T"]),
            (self.r, w["W_rT"]), (self.k, w["W_kT"]), (self.v, w["W_vT"]))]

    def loading(self, staging):
        return Loading(self.room, "load", self.loads, self.weights, staging, self.ident[:])


def stage_tail(nc, attended, h_d, x_in, out_d, mod_d, w):
    HIDDEN = 2 * DIM
    HT = HIDDEN // P
    PAIRS = CT // 2
    BANKS, F_SLOTS = 8, HT + HT // 2
    uses = []
    for kind, n in (("A", CHUNKS * KT), ("B", CHUNKS * PAIRS), ("C", CHUNKS * KT)):
        uses += [(kind, i) for i in range(n)]
    uses += [("D", i) for i in range(HT + HT // 2)] + [("E", i) for i in range(PAIRS)]
    uses += [("D", i) for i in range(HT + HT // 2, 2 * HT)] + [("E", i) for i in range(PAIRS, 2 * PAIRS)]
    uses += [("G", i) for i in range(CHUNKS * KT)]
    for c in range(CHUNKS):
        uses += [("R", c * PAIRS + i) for i in range(PAIRS)] + [("K", c * KT + i) for i in range(KT)]
    uses += [("V", i) for i in range(CHUNKS * PAIRS)]
    USES = len(uses)
    assert USES % BANKS == 0
    KINDS = {kind: sum(k == kind for k, _ in uses) for kind in "ABCDEGRKV"}
    with ExitStack() as ctx:
        room = Room(nc, ctx, "tl")
        sb, sem = room.sb, room.counter
        ident, cols, f_bias, r2_bias, mod_cols = w.ident, w.cols, w.f_bias, w.r2_bias, w.mod_cols
        w_f, w_r1, w_r2, w_r, w_k, w_v = w.f, w.r1, w.r2, w.r, w.k, w.v
        G2, B2, BR1, MU = 0, KT, 2 * KT, 2 * KT + HT
        rest = sb("rest", [P, 2, KT])

        att = sb("att", [P, TILES, DIM])
        h, x, r, hat = (sb(n, [P, TILES, DIM]) for n in ("h", "x", "r", "hat"))
        a_t = room.pair("a_t", [P, KT, SEQ])
        b_t = room.pair("b_t", [P, KT, SEQ])
        f = room.pair("f", [P, F_SLOTS, CHUNK])
        tmp = sb("tmp", [P, 2, CHUNK])
        y = sb("y", [P, 2, 2, DIM])
        h_t = sb("h_t", [P, KT, SEQ + 1])
        before, mixed = sb("before", [P, 2, CHUNK]), sb("mixed", [P, 2, CHUNK])
        relu, square = sb("relu", [P, 2, CHUNK]), sb("square", [P, CHUNK])
        sig = sb("sig", [P, TILES, DIM])
        gates = sb("gates", [P, 2, DIM])
        gated_bias = sb("gated_bias", [P, DIM])
        mod_now = sb("mod_now", [P, 2, KT])
        stats, moments = sb("stats", [P, TILES, 6]), sb("moments", [P, TILES, 2])
        var, rstd, scratch = sb("var", [P, TILES]), sb("rstd", [P, TILES]), sb("scratch", [P, TILES])
        power, mark = sb("power", [P, CT]), sb("mark", [P, CT])
        banks = [room.ps(f"bank{n}", [P, 512]) for n in range(BANKS)]

        att_in, h_in, x_in_sem, gates_in, out_stored = (
            sem("att_in"), sem("h_in"), sem("x_in"), sem("gates_in"), sem("out_stored"))
        zero_ready, rest_ready, full = room.sem("zero_ready"), room.sem("rest_ready"), sem("full")
        a_hi_ready, a_ready = sem("a_hi_ready"), sem("a_ready")
        h_biased, r_ready = sem("h_biased"), sem("r_ready")
        var_ready, rstd_ready, hat_ready = sem("var_ready"), sem("rstd_ready"), sem("hat_ready")
        b_hi_ready, b_ready = sem("b_hi_ready"), sem("b_ready")
        f_hi_ready, f_ready = sem("f_hi_ready"), sem("f_ready")
        y_ready, x1_ready = sem("y_ready"), sem("x1_ready")
        h_t_ready, before_ready, mixed_ready = sem("h_t_ready"), sem("before_ready"), sem("mixed_ready")
        rows_hi_ready, rows_ready = sem("rows_hi_ready"), sem("rows_ready")
        sig_ready, relu_ready, k_hi_ready, k_ready = (
            sem("sig_ready"), sem("relu_ready"), sem("k_hi_ready"), sem("k_ready"))
        product_ready, out_ready = sem("product_ready"), sem("out_ready")
        vec_step, pool_step = room.sem("vec_step"), room.sem("pool_step")

        bank_read = {"A": a_ready, "B": r_ready, "C": b_hi_ready, "D": f_hi_ready, "E": y_ready,
                     "G": h_t_ready, "R": sig_ready, "K": relu_ready, "V": product_ready}
        number = {use: n for n, use in enumerate(uses)}

        def bank(kind, n):
            return banks[number[kind, n] % BANKS]

        def wait_full(engine, trip, kind, n):
            engine.wait_ge(full, at(trip, USES, number[kind, n] + 1))

        rows_of = lambda dram: dram.rearrange("(b t p) n -> b p t n", b=BATCH, p=P)
        chunk = lambda c: slice(c * CHUNK, (c + 1) * CHUNK)
        pair_of = lambda n: slice(2 * n, 2 * n + 2)

        start_counters(nc, room)
        with nc.Block() as block:
            @block.sync
            def _(sp):
                def load_first(index):
                    sp.dma_start(att[:], attended[:, bass.ds(index * TILES, TILES), :]).then_inc(att_in, 16)

                def load_h(index):
                    sp.dma_start(h[:], rows_of(h_d)[index]).then_inc(h_in, 16)

                load_first(0)
                load_h(0)

                def trip_of(trip, last):
                    sp.wait_ge(out_ready, at(trip, CHUNKS * PAIRS, 0))
                    sp.dma_start(gates[:, 0], mod_d[1, trip, GATE_A * DIM:(GATE_A + 1) * DIM]
                                 .partition_broadcast(P)).then_inc(gates_in, 16)
                    sp.dma_start(gates[:, 1], mod_d[1, trip, GATE_B * DIM:(GATE_B + 1) * DIM]
                                 .partition_broadcast(P)).then_inc(gates_in, 16)
                    sp.wait_ge(out_stored, at(trip, 16, 0))
                    sp.dma_start(x[:], rows_of(x_in)[trip]).then_inc(x_in_sem, 16)
                    if not last:
                        wait_full(sp, trip, "A", CHUNKS * KT - 1)
                        load_first(trip + 1)
                        sp.wait_ge(r_ready, at(trip, KINDS["B"], KINDS["B"]))
                        load_h(trip + 1)
                    sp.wait_ge(out_ready, at(trip, CHUNKS * PAIRS, CHUNKS * PAIRS))
                    sp.dma_start(rows_of(out_d)[trip], x[:]).then_inc(out_stored, 16)

                with sp.Fori(0, BATCH - 1) as trip:
                    trip_of(trip, False)
                trip_of(BATCH - 1, True)
                sp.wait_ge(out_stored, at(BATCH, 16, 0))

            @block.gpsimd
            def _(pool):
                pool.memset(power[:], -0.5).then_inc(pool_step, 1)
                pool.wait_ge(pool_step, 1)
                pool.memset(h_t[:, :, 0:1], 0.0).then_inc(zero_ready, 1)
                pool.wait_ge(zero_ready, 1)
                pool.sem_clear(pool_step)
                step = Steps(pool, pool_step)

                def bias_h(index):
                    pool.wait_ge(h_in, at(index, 16, 16))
                    for c in range(CHUNKS):
                        part = h[:, c * CT:(c + 1) * CT]
                        pool.tensor_tensor(part, part, f_bias[:].unsqueeze(1).to_broadcast([P, CT, DIM]),
                                           ALU.add).then_inc(h_biased, 1)

                bias_h(0)

                def trip_of(trip, last):
                    def deviation(norm, c):
                        pool.wait_ge(var_ready, at(trip, 2 * CHUNKS, norm * CHUNKS + c + 1))
                        pool.tensor_tensor(rstd[:, c * CT:(c + 1) * CT], var[:, c * CT:(c + 1) * CT], power[:],
                                           ALU.pow).then_inc(rstd_ready, 1)

                    def over_tiles(row, n):
                        return row.unsqueeze(1).to_broadcast([P, n, DIM])

                    pool.wait_ge(h_t_ready, at(trip, KINDS["G"], 0))
                    pool.tensor_tensor(mark[:], power[:], power[:], ALU.mult).then_inc(pool_step, step.one())
                    pool.tensor_copy(mod_now[:].rearrange("p w k -> p (w k)"),
                                     mod_cols[:, SHIFT_B * KT:(SCALE_B + 1) * KT, trip]).then_inc(pool_step, step.one())
                    deviation(0, 0)
                    deviation(0, 1)
                    pool.wait_ge(gates_in, at(trip, 32, 32))
                    pool.tensor_tensor(gated_bias[:], gates[:, 0], r2_bias[:], ALU.mult).then_inc(pool_step, step.one())
                    pool.wait_ge(x_in_sem, at(trip, 16, 16))
                    step.wait()
                    for c in range(CHUNKS):
                        part = x[:, c * CT:(c + 1) * CT]
                        pool.tensor_tensor(part, part, over_tiles(gated_bias[:], CT), ALU.add).then_inc(pool_step, step.one())
                    step.wait()
                    for n in range(CHUNKS * PAIRS):
                        part = y[:, n % 2]
                        pool.wait_ge(y_ready, at(trip, KINDS["E"], n + 1))
                        pool.tensor_tensor(part, part, over_tiles(gates[:, 0], 2), ALU.mult).then_inc(pool_step, step.one())
                        step.wait()
                        pool.tensor_tensor(x[:, pair_of(n)], x[:, pair_of(n)], part, ALU.add).then_inc(x1_ready, 1)
                        if n == PAIRS - 1:
                            deviation(1, 0)
                    deviation(1, 1)
                    if not last:
                        bias_h(trip + 1)
                    pool.wait_ge(x1_ready, at(trip, CHUNKS * PAIRS, CHUNKS * PAIRS))
                    for n in range(CHUNKS * PAIRS):
                        part = sig[:, pair_of(n)]
                        pool.wait_ge(product_ready, at(trip, KINDS["V"], n + 1))
                        pool.tensor_tensor(part, part, over_tiles(gates[:, 1], 2), ALU.mult).then_inc(pool_step, step.one())
                        step.wait()
                        pool.tensor_tensor(x[:, pair_of(n)], x[:, pair_of(n)], part, ALU.add).then_inc(out_ready, 1)
                    step.restart()

                with pool.Fori(0, BATCH - 1) as trip:
                    trip_of(trip, False)
                trip_of(BATCH - 1, True)

            @block.tensor
            def _(pe):
                with pe.Fori(0, BATCH) as trip:
                    def free(kind, n):
                        u = number[kind, n] - BANKS
                        if u >= 0:
                            old, i = uses[u]
                            pe.wait_ge(bank_read[old], at(trip, KINDS[old], i + 1))
                        else:
                            old, _ = uses[u + USES]
                            pe.wait_ge(bank_read[old], at(trip, KINDS[old], 0))

                    def turn(kind, n, source):
                        c, k = divmod(n, KT)
                        free(kind, n)
                        for t in range(CT):
                            mm = pe.transpose(bank(kind, n)[:, t * P:(t + 1) * P],
                                              source[:, c * CT + t, k * P:(k + 1) * P], ident[:])
                        mm.then_inc(full, 1)

                    def to_features(kind, n, weights, m, moving, c):
                        free(kind, n)
                        for k in range(KT):
                            mm = product3(pe, bank(kind, n)[:], cut(weights, slice(None), k, slice(m * P, (m + 1) * P)),
                                          cut(moving, slice(None), k, chunk(c)), k == 0, k == KT - 1)
                        mm.then_inc(full, 1)

                    def to_tokens(kind, n, tiles, weights, inner):
                        free(kind, n)
                        for i in range(2):
                            for k in range(inner):
                                mm = product3(pe, bank(kind, n)[:, i * DIM:(i + 1) * DIM], tiles(k, 2 * n + i),
                                              cut(weights, slice(None), k), k == 0, k == inner - 1)
                        mm.then_inc(full, 1)

                    def tiles_of(pair):
                        return lambda k, t: cut(pair, slice(None), k, slice(t * P, (t + 1) * P))

                    pe.wait_ge(att_in, at(trip, 16, 16))
                    for n in range(KINDS["A"]):
                        turn("A", n, att)
                    for n in range(KINDS["B"]):
                        pe.wait_ge(a_ready, at(trip, KINDS["A"], KT * (n // PAIRS + 1)))
                        to_tokens("B", n, tiles_of(a_t), w_f, KT)
                    for n in range(KINDS["C"]):
                        pe.wait_ge(hat_ready, at(trip, 2 * CHUNKS, n // KT + 1))
                        turn("C", n, hat)

                    def expand(n):
                        c, m = divmod(n, HT)
                        pe.wait_ge(b_ready, at(trip, KINDS["C"], KT * (c + 1)))
                        to_features("D", n, w_r1, m, b_t, c)

                    def contract(c):
                        pe.wait_ge(f_ready, at(trip, KINDS["D"], HT * (c + 1)))
                        for i in range(PAIRS):
                            to_tokens("E", c * PAIRS + i, lambda m, t: cut(
                                f, slice(None), (c * HT + m) % F_SLOTS, slice(t % CT * P, (t % CT + 1) * P)), w_r2, HT)

                    for n in range(F_SLOTS):
                        expand(n)
                    contract(0)
                    for n in range(F_SLOTS, 2 * HT):
                        expand(n)
                    contract(1)
                    for n in range(KINDS["G"]):
                        pe.wait_ge(hat_ready, at(trip, 2 * CHUNKS, CHUNKS + n // KT + 1))
                        turn("G", n, hat)
                    for c in range(CHUNKS):
                        pe.wait_ge(rows_ready, at(trip, 4 * KT, 2 * KT * c + KT))
                        for i in range(PAIRS):
                            to_tokens("R", c * PAIRS + i, tiles_of(a_t), w_r, KT)
                        pe.wait_ge(rows_ready, at(trip, 4 * KT, 2 * KT * c + 2 * KT))
                        for m in range(KT):
                            to_features("K", c * KT + m, w_k, m, b_t, c)
                    for n in range(KINDS["V"]):
                        c = n // PAIRS
                        pe.wait_ge(k_ready, at(trip, KINDS["K"], KT * (c + 1)))
                        to_tokens("V", n, lambda m, t: cut(
                            f, slice(None), c * KT + m, slice(t % CT * P, (t % CT + 1) * P)), w_v, KT)

            @block.scalar
            def _(act):
                act.wait_ge(zero_ready, 1)
                act.wait_ge(rest_ready, 1)
                with act.Fori(0, BATCH) as trip:
                    for n in range(KINDS["A"]):
                        c, k = divmod(n, KT)
                        wait_full(act, trip, "A", n)
                        act.activation(a_t[0][:, k, chunk(c)], bank("A", n)[:], ACT.Copy).then_inc(a_hi_ready, 1)
                    for n in range(KINDS["C"]):
                        c, k = divmod(n, KT)
                        wait_full(act, trip, "C", n)
                        act.wait_ge(b_ready, at(trip, KINDS["C"], max(0, n - 1)))
                        if n < 2:
                            act.wait_ge(f_ready, at(trip, KINDS["D"], 0))
                        for out in (tmp[:, n % 2], b_t[0][:, k, chunk(c)]):
                            ins = act.activation(out, bank("C", n)[:], ACT.Identity, bias=cols[:, B2 + k:B2 + k + 1],
                                                 scale=cols[:, G2 + k:G2 + k + 1])
                        ins.then_inc(b_hi_ready, 1)

                    def expanded(n):
                        m = n % HT
                        wait_full(act, trip, "D", n)
                        if n < 2:
                            act.wait_ge(b_ready, at(trip, KINDS["C"], KINDS["C"] + n - 1))
                        else:
                            act.wait_ge(f_ready, at(trip, KINDS["D"], n - 1))
                        if n >= F_SLOTS:
                            wait_full(act, trip, "E", PAIRS - 1)
                        for out in (tmp[:, n % 2], f[0][:, n % F_SLOTS]):
                            ins = act.activation(out, bank("D", n)[:], ACT.Relu, bias=cols[:, BR1 + m:BR1 + m + 1])
                        ins.then_inc(f_hi_ready, 1)
                    for n in range(KINDS["D"]):
                        expanded(n)

                    def token_before(n):
                        c, which, k = n // (2 * KT), n // KT % 2, n % KT
                        act.wait_ge(h_t_ready, at(trip, KINDS["G"], KT * c + k + 1))
                        act.wait_ge(mixed_ready, at(trip, 4 * KT, max(0, n - 1)))
                        act.activation(before[:, n % 2], h_t[:, k, chunk(c)], ACT.Copy,
                                       scale=rest[:, which, k:k + 1]).then_inc(before_ready, 1)

                    def rows_high(n):
                        c, which, k = n // (2 * KT), n // KT % 2, n % KT
                        act.wait_ge(mixed_ready, at(trip, 4 * KT, n + 1))
                        act.activation((a_t, b_t)[which][0][:, k, chunk(c)], mixed[:, n % 2],
                                       ACT.Copy).then_inc(rows_hi_ready, 1)

                    for c in range(CHUNKS):
                        for k in range(KT):
                            wait_full(act, trip, "G", c * KT + k)
                            act.activation(h_t[:, k, 1 + c * CHUNK:1 + (c + 1) * CHUNK], bank("G", c * KT + k)[:],
                                           ACT.Identity, bias=mod_now[:, 0, k:k + 1],
                                           scale=mod_now[:, 1, k:k + 1]).then_inc(h_t_ready, 1)
                        for n in range(2 * KT * c, 2 * KT * (c + 1)):
                            token_before(n)
                            if n % (2 * KT):
                                rows_high(n - 1)
                        rows_high(2 * KT * (c + 1) - 1)
                    act.wait_ge(out_ready, at(trip, CHUNKS * PAIRS, 0))
                    for c in range(CHUNKS):
                        for n in range(c * PAIRS, (c + 1) * PAIRS):
                            wait_full(act, trip, "R", n)
                            act.activation(sig[:, pair_of(n)], bank("R", n)[:].rearrange("p (t n) -> p t n", n=DIM),
                                           ACT.Sigmoid).then_inc(sig_ready, 1)
                        for n in range(c * KT, (c + 1) * KT):
                            wait_full(act, trip, "K", n)
                            act.wait_ge(k_ready, at(trip, KINDS["K"], max(0, n - 1)))
                            act.activation(relu[:, n % 2], bank("K", n)[:], ACT.Relu).then_inc(relu_ready, 1)
                            act.wait_ge(relu_ready, at(trip, KINDS["K"], n + 1))
                            act.activation(f[0][:, n], relu[:, n % 2], ACT.Square).then_inc(k_hi_ready, 1)

            @block.vector
            def _(vec):
                for which in range(2):
                    ins = vec.tensor_scalar(rest[:, which], cols[:, MU + which * KT:MU + (which + 1) * KT], -1.0, 1.0,
                                            ALU.mult, ALU.add)
                ins.then_inc(rest_ready, 1)
                vec.wait_ge(rest_ready, 1)
                vec.wait_ge(zero_ready, 1)
                step = Steps(vec, vec_step)

                with vec.Fori(0, BATCH) as trip:
                    def low(pair, index, whole, hi_sem, per, n, done):
                        vec.wait_ge(hi_sem, at(trip, per, n + 1))
                        vec.tensor_tensor(pair[1][index], whole, pair[0][index].bitcast(F32),
                                          ALU.subtract).then_inc(done, 1)

                    def statistics(rows, c):
                        for t in range(c * CT, (c + 1) * CT):
                            vec.bn_stats(stats[:, t], rows[:, t]).then_inc(vec_step, step.one())
                        step.wait()
                        for t in range(c * CT, (c + 1) * CT):
                            vec.bn_aggr(moments[:, t], stats[:, t]).then_inc(vec_step, step.one())
                        step.wait()
                        part = slice(c * CT, (c + 1) * CT)
                        vec.tensor_scalar(var[:, part], moments[:, part, 1], EPS, None, ALU.add).then_inc(var_ready, 1)

                    def normalise(rows, norm, c):
                        part = slice(c * CT, (c + 1) * CT)
                        vec.wait_ge(rstd_ready, at(trip, 2 * CHUNKS, norm * CHUNKS + c + 1))
                        newton_rsqrt(vec, step, rstd[:, part], var[:, part], scratch[:, part])
                        step.wait()
                        for t in range(c * CT, (c + 1) * CT):
                            ins = vec.tensor_scalar(hat[:, t], rows[:, t], moments[:, t, 0:1], rstd[:, t:t + 1],
                                                    ALU.subtract, ALU.mult)
                        ins.then_inc(hat_ready, 1)

                    for n in range(KINDS["A"]):
                        c, k = divmod(n, KT)
                        low(a_t, (slice(None), k, chunk(c)), bank("A", n)[:], a_hi_ready, KINDS["A"], n, a_ready)

                    def residual(c):
                        vec.wait_ge(h_biased, at(trip, CHUNKS, c + 1))
                        for n in range(c * PAIRS, (c + 1) * PAIRS):
                            wait_full(vec, trip, "B", n)
                            vec.tensor_tensor(r[:, pair_of(n)], bank("B", n)[:].rearrange("p (t n) -> p t n", n=DIM),
                                              h[:, pair_of(n)], ALU.add).then_inc(r_ready, 1)
                        vec.wait_ge(r_ready, at(trip, KINDS["B"], (c + 1) * PAIRS))

                    residual(0)
                    statistics(r, 0)
                    residual(1)
                    normalise(r, 0, 0)
                    statistics(r, 1)
                    normalise(r, 0, 1)
                    for n in range(KINDS["C"]):
                        c, k = divmod(n, KT)
                        low(b_t, (slice(None), k, chunk(c)), tmp[:, n % 2], b_hi_ready, KINDS["C"], n, b_ready)

                    def f_low(n):
                        low(f, (slice(None), n % F_SLOTS), tmp[:, n % 2], f_hi_ready, KINDS["D"], n, f_ready)

                    def with_residual(n):
                        wait_full(vec, trip, "E", n)
                        vec.wait_ge(x1_ready, at(trip, CHUNKS * PAIRS, max(0, n - 1)))
                        vec.tensor_tensor(y[:, n % 2], bank("E", n)[:].rearrange("p (t n) -> p t n", n=DIM),
                                          r[:, pair_of(n)], ALU.add).then_inc(y_ready, 1)

                    for n in range(F_SLOTS):
                        f_low(n)
                    for n in range(PAIRS):
                        with_residual(n)
                    for n in range(F_SLOTS, 2 * HT):
                        f_low(n)
                    vec.wait_ge(x1_ready, at(trip, CHUNKS * PAIRS, PAIRS))
                    statistics(x, 0)
                    for n in range(PAIRS, 2 * PAIRS):
                        with_residual(n)
                    normalise(x, 1, 0)
                    vec.wait_ge(x1_ready, at(trip, CHUNKS * PAIRS, 2 * PAIRS))
                    statistics(x, 1)
                    normalise(x, 1, 1)

                    def rows_low(n):
                        c, which, k = n // (2 * KT), n // KT % 2, n % KT
                        low((a_t, b_t)[which], (slice(None), k, chunk(c)), mixed[:, n % 2], rows_hi_ready, 4 * KT, n,
                            rows_ready)

                    for n in range(4 * KT):
                        c, which, k = n // (2 * KT), n // KT % 2, n % KT
                        vec.wait_ge(before_ready, at(trip, 4 * KT, n + 1))
                        vec.wait_ge(rows_ready, at(trip, 4 * KT, max(0, n - 1)))
                        vec.scalar_tensor_tensor(mixed[:, n % 2], h_t[:, k, 1 + c * CHUNK:1 + (c + 1) * CHUNK],
                                                 cols[:, MU + which * KT + k:MU + which * KT + k + 1],
                                                 before[:, n % 2], ALU.mult, ALU.add).then_inc(mixed_ready, 1)
                        if n % (2 * KT):
                            rows_low(n - 1)
                        if n % (2 * KT) == 2 * KT - 1:
                            rows_low(n)
                    for n in range(KINDS["K"]):
                        vec.wait_ge(relu_ready, at(trip, KINDS["K"], n + 1))
                        vec.wait_ge(k_ready, at(trip, KINDS["K"], n))
                        vec.tensor_tensor(square[:], relu[:, n % 2], relu[:, n % 2], ALU.mult).then_inc(vec_step, step.one())
                        step.wait()
                        low(f, (slice(None), n), square[:], k_hi_ready, KINDS["K"], n, k_ready)
                    for n in range(KINDS["V"]):
                        wait_full(vec, trip, "V", n)
                        vec.wait_ge(sig_ready, at(trip, KINDS["R"], n + 1))
                        vec.tensor_tensor(sig[:, pair_of(n)], bank("V", n)[:].rearrange("p (t n) -> p t n", n=DIM),
                                          sig[:, pair_of(n)], ALU.mult).then_inc(product_ready, 1)
                    step.restart()


def network(nc, x, c_t, wmod0, wmod1, ga_hidden, ga_qk, ga_out, ga_ln_cols, ga_v_bias, ga_gate_bias, ga_b_out,
            ga_qk_cols, moe_w1, moe_sw1, moe_w2, moe_sw2, router_w, router_b, moe_b1_cols, moe_sb2_cols, moe_b2,
            WqT, WkT, WvT, WqvT, qk_cols, bqv, bv, Ws, bs, WfT, Wr1T, Wr2T, W_rT, W_kT, W_vT, bf, br2, tail_cols, out):
    def scratch(name, shape, dt=F32):
        return nc.dram_tensor(name + "_dram", shape, dt, kind="Internal").ap()

    mod, mod_cols = scratch("mod", [2, BATCH, MOD]), scratch("mod_cols", [P, 2, MOD // P, BATCH])
    x_ga, x_moe, h = (scratch(n, [TOKENS, DIM]) for n in ("x_ga", "x_moe", "h"))
    parts, values = scratch("parts", [2, BATCH, SPLITS, DIM, SEQ], BF16), scratch("values", [TOKENS, V_WIDTH])
    with ExitStack() as ga_ctx:
        ga = GatedAttentionWeights(nc, ga_ctx, dict(
            W_hidden=ga_hidden, W_qk=ga_qk, W_out=ga_out, ln_cols=ga_ln_cols, v_bias=ga_v_bias,
            gate_bias=ga_gate_bias, b_out=ga_b_out, qk_cols=ga_qk_cols))
        with ExitStack() as loading_ctx:
            stage_mod(nc, c_t, [wmod0, wmod1], mod, mod_cols, ga.loading(loading_ctx))
        clear_semaphores(nc)
        stage_gated_attention(nc, x, x_ga, mod, ga)
    clear_semaphores(nc)
    stage_experts(nc, x_ga, x_moe, mod_cols, dict(
        w1=moe_w1, sw1=moe_sw1, w2=moe_w2, sw2=moe_sw2, router_w=router_w, router_b=router_b, b1_cols=moe_b1_cols,
        sb2_cols=moe_sb2_cols, b2=moe_b2))
    clear_semaphores(nc)
    stage_project(nc, x_moe, h, parts, values, mod, dict(
        WqT=WqT, WkT=WkT, WvT=WvT, WqvT=WqvT, cols=qk_cols, bqv=bqv, bv=bv, Ws=Ws, bs=bs))
    clear_semaphores(nc)
    with nc.sbuf_tensor("attended", [P, BATCH * TILES, DIM], F32) as attended, ExitStack() as tail_ctx:
        tail = TailWeights(nc, tail_ctx, mod_cols, dict(
            WfT=WfT, Wr1T=Wr1T, Wr2T=Wr2T, W_rT=W_rT, W_kT=W_kT, W_vT=W_vT, bf=bf, br2=br2, cols=tail_cols))
        stage_attention(nc, parts, values, attended, tail)
        clear_semaphores(nc)
        stage_tail(nc, attended, h, x_moe, out, mod, tail)


def kernel(**inputs):
    import concourse.bacc as _bacc
    from concourse.bass_utils import run_bass_kernel_spmd as _run

    def col(a):
        return a.reshape(-1, P).T

    a = {name: np.asarray(value) for name, value in inputs.items()}
    ga = {name[8:]: a[name] for name in a if name.startswith("L0_attn_")}
    moe = {name[7:]: a[name] for name in a if name.startswith("L0_ffn_")}
    at1 = {name[8:]: a[name] for name in a if name.startswith("L1_attn_")}
    mix = {name[7:]: a[name] for name in a if name.startswith("L1_ffn_")}
    hid = ga["W_out"].shape[0]
    experts = moe["w1"].shape[0]
    arrays = {
        "x": ga["x"].reshape(TOKENS, DIM),
        "c_t": np.concatenate([a["L0_c"], a["L1_c"]], 0).T,
        "wmod0": a["L0_wmod"], "wmod1": a["L1_wmod"],
        "ga_hidden": ga["W_hidden"], "ga_qk": ga["W_qk"], "ga_out": ga["W_out"],
        "ga_ln_cols": np.stack([col(ga["ln_scale"]), col(ga["ln_bias"])], 1),
        "ga_v_bias": ga["b_hidden"][:hid], "ga_gate_bias": col(ga["b_hidden"][hid:]), "ga_b_out": ga["b_out"],
        "ga_qk_cols": np.concatenate([ga["b_qk"][None], ga["os_weight"], ga["os_bias"]], 0).T,
        "moe_w1": moe["w1"].transpose(1, 0, 2).reshape(DIM, -1),
        "moe_sw1": moe["sw1"].transpose(1, 0, 2).reshape(DIM, -1),
        "moe_w2": moe["w2"].reshape(-1, DIM), "moe_sw2": moe["sw2"].reshape(-1, DIM),
        "router_w": moe["router_w"], "router_b": moe["router_b"],
        "moe_b1_cols": np.concatenate([moe["b1"].reshape(-1, P), moe["sb1"].reshape(-1, P)]).T,
        "moe_sb2_cols": np.stack([col(row) for row in moe["sb2"]], 1),
        "moe_b2": moe["b2"].reshape(experts, DIM),
        "WqT": at1["Wq"].T, "WkT": at1["Wk"].T, "WvT": at1["Wv"].T, "WqvT": at1["Wqv"].T,
        "qk_cols": np.stack([col(at1[name]) for name in ("g1", "b1", "bq", "bk")], 1),
        "bqv": at1["bqv"], "bv": at1["bv"], "Ws": at1["Ws"], "bs": at1["bs"],
        "WfT": at1["Wf"].T, "Wr1T": at1["Wr1"].T, "Wr2T": at1["Wr2"].T,
        "W_rT": mix["W_r"].T, "W_kT": mix["W_k"].T, "W_vT": mix["W_v"].T,
        "bf": at1["bf"], "br2": at1["br2"],
        "tail_cols": np.concatenate([col(at1["g2"]), col(at1["b2"]), col(at1["br1"]), col(mix["mu_r"]),
                                     col(mix["mu_k"])], 1),
    }
    nc = _bacc.Bacc("TRN2", target_bir_lowering=False, num_devices=1)
    arrays = {f"in_{name}_dram": np.ascontiguousarray(value) for name, value in arrays.items()}
    args = [nc.dram_tensor(name, value.shape, mybir.dt.from_np(value.dtype), kind="ExternalInput").ap()
            for name, value in arrays.items()]
    out = nc.dram_tensor("out_0_dram", [TOKENS, DIM], F32, kind="ExternalOutput").ap()
    network(nc, *args, out)
    r = _run(nc, [arrays], core_ids=[0])
    return r.results[0]["out_0_dram"].reshape(BATCH, SEQ, DIM)
```
